# Optimizing a Trainium2 kernel written in Bass

```python
import numpy as np
import jax
import jax.numpy as jnp

def _softmax(x, axis=-1):
    return jax.nn.softmax(x, axis=axis)

def _gelu(x):
    return jax.nn.gelu(x, approximate=True)

def _silu(x):
    return jax.nn.silu(x)

def _sigmoid(x):
    return jax.nn.sigmoid(x)

def _layernorm(x, axis=-1, eps=1e-05):
    m = jnp.mean(x, axis=axis, keepdims=True)
    v = jnp.var(x, axis=axis, keepdims=True)
    return (x - m) / jnp.sqrt(v + eps)

def _scatter_add(tgt, idx, src, axis=0):
    return tgt.at[idx].add(src)

def _segment_sum(src, seg, n):
    return jax.ops.segment_sum(src, seg, n)
kernel_name = 'mk_conv_seq_d4_conv_nchw512_r4_7381de'

def setup_inputs(seed: int=0):
    np.random.seed(seed)
    _w = jnp.asarray

    def _rec_inputs():
        import jax
        import jax.numpy as jnp
        _gk = jax.random.key(seed)
        x = -0.000125 + 0.9999 * jax.random.normal(jax.random.fold_in(_gk, 1), (16, 128, 16, 16), jnp.float32)
        return x
    x = _rec_inputs()

    def _L0_conv_setup():
        import jax, jax.numpy as jnp
        import numpy as np
        key = jax.random.key(seed)
        k1, k2, k3 = jax.random.split(key, 3)
        B, C, H, W = (16, 128, 16, 16)
        x = jax.random.normal(k1, (B, C, H, W), dtype=jnp.float32)
        w1 = jax.random.normal(k2, (2 * C // 16, 2 * C), dtype=jnp.float32) * 0.02
        b1 = jnp.zeros((2 * C // 16,), dtype=jnp.float32)
        w2 = jax.random.normal(k3, (C, 2 * C // 16), dtype=jnp.float32) * 0.02
        b2 = jnp.zeros((C,), dtype=jnp.float32)
        return {'x': x, 'w1': w1, 'b1': b1, 'w2': w2, 'b2': b2}
    _L0_conv_all = _L0_conv_setup()
    _L0_conv_in = {k: v for k, v in _L0_conv_all.items() if k in ('w1', 'b1', 'w2', 'b2')}
    del _L0_conv_all

    def _L1_conv_setup():
        import jax, jax.numpy as jnp
        import numpy as np
        from jax import lax
        IN_DIM = 128
        MID = IN_DIM // 2
        HEADS = 8
        B, H, W = (16, 16, 16)
        BN_EPS = 1e-05
        NORM_EPS = 1e-12
        key = jax.random.key(seed)
        ks = jax.random.split(key, 16)
        r = lambda k, shape, s=0.02: jax.random.normal(k, shape, dtype=jnp.float32) * s
        return {'x': jax.random.normal(ks[0], (B, IN_DIM, H, W), dtype=jnp.float32), 'reduce_w': r(ks[1], (MID, IN_DIM)), 'reduce_b': jnp.zeros((MID,), jnp.float32), 'dw_w': r(ks[2], (MID, 1, 3, 3), 0.1), 'dw_b': jnp.zeros((MID,), jnp.float32), 'bn_gamma': jnp.ones((MID,), jnp.float32), 'bn_beta': jnp.zeros((MID,), jnp.float32), 'bn_mean': r(ks[3], (MID,), 0.1), 'bn_var': jnp.ones((MID,), jnp.float32), 'gate_w1': r(ks[4], (MID // 8, MID)), 'gate_b1': jnp.zeros((MID // 8,), jnp.float32), 'gate_w2': r(ks[5], (MID, MID // 8)), 'gate_b2': jnp.zeros((MID,), jnp.float32), 'temperature': jnp.ones((HEADS, 1, 1), jnp.float32), 'post_w': r(ks[6], (IN_DIM, 2 * MID)), 'post_b': jnp.zeros((IN_DIM,), jnp.float32)}
    _L1_conv_all = _L1_conv_setup()
    _L1_conv_in = {k: v for k, v in _L1_conv_all.items() if k in ('reduce_w', 'reduce_b', 'dw_w', 'dw_b', 'bn_gamma', 'bn_beta', 'bn_mean', 'bn_var', 'gate_w1', 'gate_b1', 'gate_w2', 'gate_b2', 'temperature', 'post_w', 'post_b')}
    del _L1_conv_all

    def _L2_conv_setup():
        import jax, jax.numpy as jnp
        import numpy as np
        NUM_HEADS = 8
        NUM_GROUPS = 32
        EPS = 1e-05

        def _group_norm(xf, gamma, beta):
            b, c, T = xf.shape
            xr = xf.reshape(b, NUM_GROUPS, c // NUM_GROUPS, T)
            mean = jnp.mean(xr, axis=(2, 3), keepdims=True)
            var = jnp.var(xr, axis=(2, 3), keepdims=True)
            xn = ((xr - mean) * jax.lax.rsqrt(var + EPS)).reshape(b, c, T)
            return xn * gamma[None, :, None] + beta[None, :, None]
        key = jax.random.key(seed)
        k1, k2, k3 = jax.random.split(key, 3)
        c = 128
        x = jax.random.normal(k1, (8, c, 32, 32), dtype=jnp.float32)
        gamma = jnp.ones((c,), dtype=jnp.float32)
        beta = jnp.zeros((c,), dtype=jnp.float32)
        w_qkv = jax.random.normal(k2, (3 * c, c), dtype=jnp.float32) * 0.02
        b_qkv = jnp.zeros((3 * c,), dtype=jnp.float32)
        w_proj = jax.random.normal(k3, (c, c), dtype=jnp.float32) * 0.02
        b_proj = jnp.zeros((c,), dtype=jnp.float32)
        return {'x': x, 'gamma': gamma, 'beta': beta, 'w_qkv': w_qkv, 'b_qkv': b_qkv, 'w_proj': w_proj, 'b_proj': b_proj}
    _L2_conv_all = _L2_conv_setup()
    _L2_conv_in = {k: v for k, v in _L2_conv_all.items() if k in ('gamma', 'beta', 'w_qkv', 'b_qkv', 'w_proj', 'b_proj')}
    del _L2_conv_all

    def _L3_conv_setup():
        import jax, jax.numpy as jnp
        import numpy as np
        DN = ('NCHW', 'OIHW', 'NCHW')

        def conv3x3(x, w):
            return jax.lax.conv_general_dilated(x, w, (1, 1), [(1, 1), (1, 1)], dimension_numbers=DN)
        key = jax.random.key(seed)
        ks = jax.random.split(key, 5)
        N, C, H, W = (16, 128, 16, 16)
        fan = C * 3 * 3
        s = 1.0 / np.sqrt(fan)
        x = jax.random.normal(ks[0], (N, C, H, W), dtype=jnp.float32)
        Wq = jax.random.normal(ks[1], (C, C, 3, 3), dtype=jnp.float32) * s
        Wk = jax.random.normal(ks[2], (C, C, 3, 3), dtype=jnp.float32) * s
        Wv = jax.random.normal(ks[3], (C, C, 3, 3), dtype=jnp.float32) * s
        Wc = jax.random.normal(ks[4], (C, C, 3, 3), dtype=jnp.float32) * s
        gamma = jnp.ones((C,), dtype=jnp.float32)
        beta = jnp.zeros((C,), dtype=jnp.float32)
        return {'x': x, 'Wq': Wq, 'Wk': Wk, 'Wv': Wv, 'Wc': Wc, 'gamma': gamma, 'beta': beta}
    _L3_conv_all = _L3_conv_setup()
    _L3_conv_in = {k: v for k, v in _L3_conv_all.items() if k in ('Wq', 'Wk', 'Wv', 'Wc', 'gamma', 'beta')}
    del _L3_conv_all
    return {'x': x, 'L0_conv_w1': _L0_conv_in['w1'], 'L0_conv_b1': _L0_conv_in['b1'], 'L0_conv_w2': _L0_conv_in['w2'], 'L0_conv_b2': _L0_conv_in['b2'], 'L1_conv_reduce_w': _L1_conv_in['reduce_w'], 'L1_conv_reduce_b': _L1_conv_in['reduce_b'], 'L1_conv_dw_w': _L1_conv_in['dw_w'], 'L1_conv_dw_b': _L1_conv_in['dw_b'], 'L1_conv_bn_gamma': _L1_conv_in['bn_gamma'], 'L1_conv_bn_beta': _L1_conv_in['bn_beta'], 'L1_conv_bn_mean': _L1_conv_in['bn_mean'], 'L1_conv_bn_var': _L1_conv_in['bn_var'], 'L1_conv_gate_w1': _L1_conv_in['gate_w1'], 'L1_conv_gate_b1': _L1_conv_in['gate_b1'], 'L1_conv_gate_w2': _L1_conv_in['gate_w2'], 'L1_conv_gate_b2': _L1_conv_in['gate_b2'], 'L1_conv_temperature': _L1_conv_in['temperature'], 'L1_conv_post_w': _L1_conv_in['post_w'], 'L1_conv_post_b': _L1_conv_in['post_b'], 'L2_conv_gamma': _L2_conv_in['gamma'], 'L2_conv_beta': _L2_conv_in['beta'], 'L2_conv_w_qkv': _L2_conv_in['w_qkv'], 'L2_conv_b_qkv': _L2_conv_in['b_qkv'], 'L2_conv_w_proj': _L2_conv_in['w_proj'], 'L2_conv_b_proj': _L2_conv_in['b_proj'], 'L3_conv_Wq': _L3_conv_in['Wq'], 'L3_conv_Wk': _L3_conv_in['Wk'], 'L3_conv_Wv': _L3_conv_in['Wv'], 'L3_conv_Wc': _L3_conv_in['Wc'], 'L3_conv_gamma': _L3_conv_in['gamma'], 'L3_conv_beta': _L3_conv_in['beta']}

def reference(x, L0_conv_w1, L0_conv_b1, L0_conv_w2, L0_conv_b2, L1_conv_reduce_w, L1_conv_reduce_b, L1_conv_dw_w, L1_conv_dw_b, L1_conv_bn_gamma, L1_conv_bn_beta, L1_conv_bn_mean, L1_conv_bn_var, L1_conv_gate_w1, L1_conv_gate_b1, L1_conv_gate_w2, L1_conv_gate_b2, L1_conv_temperature, L1_conv_post_w, L1_conv_post_b, L2_conv_gamma, L2_conv_beta, L2_conv_w_qkv, L2_conv_b_qkv, L2_conv_w_proj, L2_conv_b_proj, L3_conv_Wq, L3_conv_Wk, L3_conv_Wv, L3_conv_Wc, L3_conv_gamma, L3_conv_beta):
    import jax
    import jax.numpy as jnp

    def _L0_conv_ref(x, w1, b1, w2, b2):
        import jax, jax.numpy as jnp
        import numpy as np
        B, C, H, W = x.shape
        q = x.reshape(B, C, H * W)
        energy = jnp.einsum('bcn,bdn->bcd', q, q)
        energy_new = jnp.max(energy, axis=-1, keepdims=True) - energy
        attention = jax.nn.softmax(energy_new, axis=-1)
        out = jnp.einsum('bcd,bdn->bcn', attention, q).reshape(B, C, H, W)
        pooled = jnp.concatenate([x, out], axis=1).mean(axis=(2, 3))
        h = jax.nn.relu(pooled @ w1.T + b1)
        se = jax.nn.sigmoid(h @ w2.T + b2)[:, :, None, None]
        return se * x + (1.0 - se) * out

    def _L1_conv_ref(x, reduce_w, reduce_b, dw_w, dw_b, bn_gamma, bn_beta, bn_mean, bn_var, gate_w1, gate_b1, gate_w2, gate_b2, temperature, post_w, post_b):
        import jax, jax.numpy as jnp
        import numpy as np
        from jax import lax
        IN_DIM = 128
        MID = IN_DIM // 2
        HEADS = 8
        B, H, W = (16, 16, 16)
        BN_EPS = 1e-05
        NORM_EPS = 1e-12
        Bsz, C, Hh, Ww = x.shape
        xr = jnp.einsum('bchw,oc->bohw', x, reduce_w) + reduce_b[:, None, None]
        xr = lax.conv_general_dilated(xr, dw_w, (1, 1), 'SAME', feature_group_count=MID, dimension_numbers=('NCHW', 'OIHW', 'NCHW'))
        xr = xr + dw_b[:, None, None]
        inv = bn_gamma / jnp.sqrt(bn_var + BN_EPS)
        xr = (xr - bn_mean[:, None, None]) * inv[:, None, None] + bn_beta[:, None, None]
        xr = jax.nn.relu(xr)
        fft_feat = jnp.fft.fft2(xr, norm='ortho')
        HWn = Hh * Ww
        qkv = fft_feat.reshape(Bsz, HEADS, MID // HEADS, HWn)
        nrm = jnp.sqrt(jnp.sum(jnp.abs(qkv) ** 2, axis=-1, keepdims=True))
        qn = qkv / jnp.maximum(nrm, NORM_EPS)
        attn = jnp.einsum('bhcn,bhdn->bhcd', qn, qn)
        attn = attn * temperature
        attn = jax.nn.softmax(attn.real, axis=-1)
        out = jnp.einsum('bhcd,bhdn->bhcn', attn, qkv.real)
        out = out.reshape(Bsz, MID, Hh, Ww).astype(jnp.complex64)
        out = jnp.fft.ifft2(out, norm='ortho').real
        g = jnp.mean(xr, axis=(-2, -1))
        g = jax.nn.relu(g @ gate_w1.T + gate_b1)
        g = jax.nn.sigmoid(g @ gate_w2.T + gate_b2)
        gated = g[:, :, None, None] * xr
        fwm = jnp.fft.ifft2(fft_feat * jnp.fft.fft2(gated)).real
        fused = jnp.concatenate([out, fwm], axis=1)
        y = jnp.einsum('bchw,oc->bohw', fused, post_w) + post_b[:, None, None] + x
        return y

    def _L2_conv_ref(x, gamma, beta, w_qkv, b_qkv, w_proj, b_proj):
        import jax, jax.numpy as jnp
        import numpy as np
        NUM_HEADS = 8
        NUM_GROUPS = 32
        EPS = 1e-05

        def _group_norm(xf, gamma, beta):
            b, c, T = xf.shape
            xr = xf.reshape(b, NUM_GROUPS, c // NUM_GROUPS, T)
            mean = jnp.mean(xr, axis=(2, 3), keepdims=True)
            var = jnp.var(xr, axis=(2, 3), keepdims=True)
            xn = ((xr - mean) * jax.lax.rsqrt(var + EPS)).reshape(b, c, T)
            return xn * gamma[None, :, None] + beta[None, :, None]
        b, c, H, W = x.shape
        T = H * W
        xf = x.reshape(b, c, T)
        qkv = jnp.einsum('oc,bct->bot', w_qkv, _group_norm(xf, gamma, beta)) + b_qkv[None, :, None]
        qkv = qkv.reshape(b * NUM_HEADS, 3 * (c // NUM_HEADS), T)
        ch = c // NUM_HEADS
        q, k, v = (qkv[:, :ch], qkv[:, ch:2 * ch], qkv[:, 2 * ch:])
        scale = 1.0 / np.sqrt(np.sqrt(ch)).astype(np.float32)
        w = jnp.einsum('bct,bcs->bts', q * scale, k * scale)
        w = jax.nn.softmax(w.astype(jnp.float32), axis=-1).astype(qkv.dtype)
        h = jnp.einsum('bts,bcs->bct', w, v).reshape(b, c, T)
        h = jnp.einsum('oc,bct->bot', w_proj, h) + b_proj[None, :, None]
        return (xf + h).reshape(b, c, H, W)

    def _L3_conv_ref(x, Wq, Wk, Wv, Wc, gamma, beta):
        import jax, jax.numpy as jnp
        import numpy as np
        DN = ('NCHW', 'OIHW', 'NCHW')

        def conv3x3(x, w):
            return jax.lax.conv_general_dilated(x, w, (1, 1), [(1, 1), (1, 1)], dimension_numbers=DN)
        C = x.shape[1]
        q = conv3x3(x, Wq)
        k = conv3x3(x, Wk)
        v = conv3x3(x, Wv)
        att = jnp.einsum('nchw,mchw->nmhw', q, k) / jnp.sqrt(jnp.float32(C))
        att = jax.nn.softmax(att, axis=1)
        virt = jnp.einsum('nmhw,mchw->nchw', att, v)
        mu = jnp.mean(virt, axis=(1, 2, 3), keepdims=True)
        var = jnp.var(virt, axis=(1, 2, 3), keepdims=True)
        virt = (virt - mu) * jax.lax.rsqrt(var + 1e-05)
        virt = virt * gamma[None, :, None, None] + beta[None, :, None, None]
        virt = jax.nn.relu(virt)
        virt = conv3x3(virt, Wc)
        return x + virt

    def _gn(v, G=32, eps=1e-05):
        B_, C_, H_, W_ = v.shape
        g = v.reshape(B_, G, C_ // G, H_, W_)
        m = jnp.mean(g, axis=(2, 3, 4), keepdims=True)
        s = jnp.var(g, axis=(2, 3, 4), keepdims=True)
        return ((g - m) / jnp.sqrt(s + eps)).reshape(v.shape)

    def _ln_c(v, eps=1e-06):
        m = jnp.mean(v, axis=1, keepdims=True)
        s = jnp.var(v, axis=1, keepdims=True)
        return (v - m) / jnp.sqrt(s + eps)

    def _ln_t(v, eps=1e-05):
        m = jnp.mean(v, axis=-1, keepdims=True)
        s = jnp.var(v, axis=-1, keepdims=True)
        return (v - m) / jnp.sqrt(s + eps)

    def _to_tokens(v):
        B_, C_, H_, W_ = v.shape
        return v.reshape(B_, C_, H_ * W_).transpose(0, 2, 1)

    def _from_tokens(t, like):
        B_, C_, H_, W_ = like.shape
        return t.transpose(0, 2, 1).reshape(B_, C_, H_, W_)
    x = _L0_conv_ref(x, L0_conv_w1, L0_conv_b1, L0_conv_w2, L0_conv_b2)
    x = _L1_conv_ref(x, L1_conv_reduce_w, L1_conv_reduce_b, L1_conv_dw_w, L1_conv_dw_b, L1_conv_bn_gamma, L1_conv_bn_beta, L1_conv_bn_mean, L1_conv_bn_var, L1_conv_gate_w1, L1_conv_gate_b1, L1_conv_gate_w2, L1_conv_gate_b2, L1_conv_temperature, L1_conv_post_w, L1_conv_post_b)
    x = _L2_conv_ref(x, L2_conv_gamma, L2_conv_beta, L2_conv_w_qkv, L2_conv_b_qkv, L2_conv_w_proj, L2_conv_b_proj)
    x = _L3_conv_ref(x, L3_conv_Wq, L3_conv_Wk, L3_conv_Wv, L3_conv_Wc, L3_conv_gamma, L3_conv_beta)
    return x

_drawn_inputs = setup_inputs


def setup_inputs(seed=0):
    import zlib

    import numpy as np

    out = dict(_drawn_inputs(seed))
    spreads = {'L0_conv_b1': (0.0, 0.8),
     'L0_conv_b2': (0.0, 0.1),
     'L1_conv_reduce_b': (0.0, 0.1),
     'L1_conv_dw_b': (0.0, 0.1),
     'L1_conv_bn_gamma': (1.0, 0.2),
     'L1_conv_bn_beta': (0.0, 0.1),
     'L1_conv_bn_var': (1.0, 0.2),
     'L1_conv_gate_b1': (0.0, 2.0),
     'L1_conv_gate_b2': (0.0, 0.8),
     'L1_conv_temperature': (1.0, 0.6),
     'L1_conv_post_b': (0.0, 0.1),
     'L2_conv_gamma': (1.0, 0.6),
     'L2_conv_beta': (0.0, 0.405),
     'L2_conv_b_qkv': (0.0, 0.1),
     'L2_conv_b_proj': (0.0, 0.1),
     'L3_conv_gamma': (1.0, 0.2),
     'L3_conv_beta': (0.0, 0.1)}
    factors = {'L0_conv_w1': 8.0,
     'L0_conv_w2': 8.0,
     'L1_conv_reduce_w': 8.0,
     'L1_conv_gate_w1': 53.893,
     'L1_conv_gate_w2': 8.0}
    for name, (base, spread) in spreads.items():
        noise = np.random.default_rng([zlib.crc32(name.encode()), seed]).standard_normal(out[name].shape)
        drawn = base * np.exp(spread * noise) if base else spread * noise
        out[name] = jnp.asarray(drawn.astype(out[name].dtype))
    for name, factor in factors.items():
        out[name] = (out[name] * factor).astype(out[name].dtype)
    return out
```

```python
from contextlib import ExitStack

import numpy as np

import concourse.bass as bass
from concourse import mybir


N, C, H, W = 16, 128, 16, 16
HW = H * W
PAIRS = N // 2
PX = 2 * HW
P = 128
CH = HW // P
HID0 = 2 * C // 16
MID = C // 2
HID1 = MID // 8
HEADS = 8
DH = C // HEADS
SLOT = 32
QUADS = HEADS * SLOT // P
VW = DH + 1
TAPS = 9
PW = W + 2
GC = C // 32
GPX = P // N
BATCH = 4
BATCHES = HW // GPX // BATCH
L2_SCALE = DH ** -0.5
L3_SCALE = float(1.0 / np.sqrt(np.float32(C)))
FAR = -1e30

F32 = mybir.dt.float32
F32R = mybir.dt.float32r
ALU = mybir.AluOpType
ACT = mybir.ActivationFunctionType
X = mybir.AxisListType.X

SMALL = [("ident", P), ("mask1", P), ("mask3", P), ("group", P), ("mean_all", P),
         ("fwd", CH * 2 * P), ("inv_aa", HW), ("inv_bb", HW), ("inv_ab", HW),
         ("even_a", HW), ("even_b", HW), ("sign_b", 1), ("lo_rows", 1),
         ("w1x", HID0), ("w1o", HID0), ("w2", C), ("b1", 1), ("b2", 1),
         ("reduce_w", MID), ("reduce_b", 1), ("dw", TAPS), ("dw_b", 1), ("bn_gamma", 1), ("bn_beta", 1),
         ("bn_mean", 1), ("bn_var", 1), ("gw1", 2 * HID1), ("gb1", 1), ("gw2", P), ("gb2", 1),
         ("temp", 1), ("post1", C), ("post2", C), ("post_b", 1),
         ("gn_gamma", 1), ("gn_beta", 1), ("wq", QUADS * P), ("wk", QUADS * P), ("bq", QUADS),
         ("bk", QUADS), ("wv", C), ("bv", 1), ("wproj", C), ("bproj", 1), ("ln_gamma", 1), ("ln_beta", 1)]
AT, _o = {}, 0
for _n, _w in SMALL:
    AT[_n] = (_o, _o + _w)
    _o += _w
SMALL_W = _o


def program(nc, x, small, convs, out):
    with ExitStack() as ctx:
        def sb(name, shape, dt=F32):
            return ctx.enter_context(nc.sbuf_tensor(name, shape, dt))

        def sem(name):
            return ctx.enter_context(nc.semaphore(name))

        cst = sb("cst", [P, SMALL_W])

        def c(name, rows=P, r0=0):
            a, b = AT[name]
            return cst[r0:r0 + rows, a:b]

        w_stage = sb("w_stage", [P, TAPS * C])
        w_hi = sb("w_hi", [P, 4, TAPS, C], F32R)
        w_lo = sb("w_lo", [P, 4, TAPS, C], F32R)
        neg_b2 = sb("neg_b2", [P, 1])
        neg_gb2 = sb("neg_gb2", [P, 1])
        bn_scale = sb("bn_scale", [P, 1])
        bn_shift = sb("bn_shift", [P, 1])
        bn_tmp = sb("bn_tmp", [P, 2])
        bq_lo = sb("bq_lo", [P, QUADS])
        proj_bias = sb("proj_bias", [P, 1])
        pow_half = sb("pow_half", [P, N])
        ones_r = sb("ones_r", [P, P], F32R)
        x_in = sb("x_in", [P, 2, HW])
        x_t = sb("x_t", [P, 2, CH, C])
        e_min = sb("e_min", [P, 2])
        att0 = sb("att0", [P, 2, C])
        att0_t = sb("att0_t", [P, 2, C])
        att0_sum = sb("att0_sum", [P, 2])
        att0_inv = sb("att0_inv", [P, 2])
        o0 = sb("o0", [P, 2, HW])
        diff0 = sb("diff0", [P, 2, HW])
        sum_o0 = sb("sum_o0", [P, 2])
        sum_x = sb("sum_x", [P, 2])
        hid0 = sb("hid0", [HID0, 2])
        z0 = sb("z0", [P, 2])
        z0p = sb("z0p", [P, 2])
        se = sb("se", [P, 2])
        x1 = sb("x1", [P, 2, HW])
        red = sb("red", [P, H + 2, PW])
        dwa = sb("dwa", [P, H, W])
        xr = sb("xr", [P, HW])
        sq_junk = sb("sq_junk", [P, HW])
        sum_xr = sb("sum_xr", [P, 1])
        n2 = sb("n2", [P, 1])
        n2m = sb("n2m", [P, 1])
        rn = sb("rn", [P, 1])
        nrm = sb("nrm", [P, 1])
        xh = sb("xh", [P, HW])
        xh_t = sb("xh_t", [P, CH, P])
        hid1 = sb("hid1", [2 * HID1, 1])
        z1 = sb("z1", [P, 1])
        z1p = sb("z1p", [P, 1])
        gate1 = sb("gate1", [P, 1])
        fscale = sb("fscale", [P, 1])
        ab = sb("ab", [P, 2, P])
        b_signed = sb("b_signed", [P, P])
        ab_sq = sb("ab_sq", [P, 2, P])
        a_times_b = sb("a_times_b", [P, P])
        logit1 = sb("logit1", [P, P])
        nmax1 = sb("nmax1", [P, 1])
        att1 = sb("att1", [P, P])
        att1_sum = sb("att1_sum", [P, 1])
        att1_inv = sb("att1_inv", [P, 1])
        att1_n = sb("att1_n", [P, P])
        even = sb("even", [P, HW])
        filt = sb("filt", [P, HW])
        post_att = sb("post_att", [P, C])
        x2 = sb("x2", [P, 2, HW])
        stats = sb("stats", [P, 2, 6])
        msq = sb("msq", [P, 2, 2])
        gmv = sb("gmv", [P, 2, 2])
        gm2 = sb("gm2", [P, 2])
        gvar = sb("gvar", [P, 2])
        grstd = sb("grstd", [P, 2])
        ga = sb("ga", [P, 2])
        gma = sb("gma", [P, 2])
        gb = sb("gb", [P, 2])
        xn = sb("xn", [P, 2, HW])
        q_hm = sb("q_hm", [P, QUADS, PX], F32R)
        q_hl = sb("q_hl", [P, QUADS, PX], F32R)
        k_hi = sb("k_hi", [P, QUADS, PX], F32R)
        k_lo = sb("k_lo", [P, QUADS, PX], F32R)
        v_t = sb("v_t", [P, 2, CH, HEADS, VW])
        nmax2 = sb("nmax2", [P, 2, CH, QUADS, P])
        nmax2_t = sb("nmax2_t", [P, QUADS, HW], F32R)
        prob = sb("prob", [P, 3, CH, HW])
        den2 = sb("den2", [P, CH, HEADS])
        h_t = sb("h_t", [P, CH, C])
        h_c = sb("h_c", [P, 2, HW])
        x3 = sb("x3", [P, N * HW])
        x3_pair = sb("x3_pair", [P, 2, HW])
        pad_hi = sb("pad_hi", [P, 2, 2, H + 2, PW], F32R)
        pad_lo = sb("pad_lo", [P, 2, 2, H + 2, PW], F32R)
        qkv3 = [sb(n, [P, N * HW]) for n in ("q3", "k3", "v3")]
        logit3 = sb("logit3", [P, BATCH, P])
        nmax3 = sb("nmax3", [P, BATCH])
        att3 = sb("att3", [P, BATCH, P])
        att3_sum = sb("att3_sum", [P, BATCH])
        att3_inv = sb("att3_inv", [P, BATCH])
        att3_n = sb("att3_n", [P, BATCH, P])
        att3_t = sb("att3_t", [P, 2, BATCH, P])
        v3_t = w_stage[:, 0:2 * BATCH * C].rearrange("p (s g c) -> p s g c", s=2, g=BATCH)
        virt = qkv3[0]
        act3 = qkv3[1]
        y = qkv3[2]
        stats3 = sb("stats3", [P, N, 6])
        msq3 = sb("msq3", [P, N, 2])
        tm3 = sb("tm3", [P, N])
        tmv3 = sb("tmv3", [P, N, 2])
        var3 = sb("var3", [P, N])
        rstd3 = sb("rstd3", [P, N])
        la = sb("la", [P, N])
        lma = sb("lma", [P, N])
        lb = sb("lb", [P, N])

        bank = [ctx.enter_context(nc.psum_tensor(f"bank{n}", [P, 512], F32)) for n in range(8)]
        CONV = 5
        Y_BANK = (4, 2)

        cst_loaded, x_loaded = sem("cst_loaded"), sem("x_loaded")
        wst_loaded = sem("wst_loaded")
        w_split_hi, w_split, w_ready = sem("w_split_hi"), sem("w_split"), sem("w_ready")
        pool_set, vec_set, vec_pre, bias_mm = sem("pool_set"), sem("vec_set"), sem("vec_pre"), sem("bias_mm")
        bn_pow = sem("bn_pow")
        xt_done, xt_copied, energy_done, e_min_done = sem("xt_done"), sem("xt_copied"), sem("energy_done"), sem("e_min_done")
        att0_exp, att0_inv_done, att0t_done, att0t_copied = sem("att0_exp"), sem("att0_inv_done"), sem("att0t_done"), sem("att0t_copied")
        o0_done, o0_scaled, diff0_done, sum_x_done = sem("o0_done"), sem("o0_scaled"), sem("diff0_done"), sem("sum_x_done")
        hid0_done, hid0_relu, z0_done, z0_exp = sem("hid0_done"), sem("hid0_relu"), sem("z0_done"), sem("z0_exp")
        z0_chain, x1_done = sem("z0_chain"), sem("x1_done")
        red_done, red_copied, dw_tap, xr_done, n2_done = sem("red_done"), sem("red_copied"), sem("dw_tap"), sem("xr_done"), sem("n2_done")
        n2m_done, rn_done, xh_done = sem("n2m_done"), sem("rn_done"), sem("xh_done")
        hid1_done, hid1_relu, z1_done, z1_exp, z1_chain = sem("hid1_done"), sem("hid1_relu"), sem("z1_done"), sem("z1_exp"), sem("z1_chain")
        xht_done, xht_copied, dft_done, ab_copied = sem("xht_done"), sem("xht_copied"), sem("dft_done"), sem("ab_copied")
        b_signed_done, squares_done = sem("b_signed_done"), sem("squares_done")
        dot1_done, even_done, filt_done = sem("dot1_done"), sem("even_done"), sem("filt_done")
        logit1_done, nmax1_done, att1_exp, att1_chain = sem("logit1_done"), sem("nmax1_done"), sem("att1_exp"), sem("att1_chain")
        even_copied, filt_scaled, patt_done, patt_copied = sem("even_copied"), sem("filt_scaled"), sem("patt_done"), sem("patt_copied")
        y1_done, x2_done = sem("y1_done"), sem("x2_done")
        gn_chain, gsum_done, gvar_done, grstd_done, xn_done = sem("gn_chain"), sem("gsum_done"), sem("gvar_done"), sem("grstd_done"), sem("xn_done")
        qk_done, v_done, qk_high, qk_low, v_copied = sem("qk_done"), sem("v_done"), sem("qk_high"), sem("qk_low"), sem("v_copied")
        s_done, s_max, maxt_done, maxt_copied = sem("s_done"), sem("s_max"), sem("maxt_done"), sem("maxt_copied")
        st_done, st_exp, pv_done, den_done, h_scaled = sem("st_done"), sem("st_exp"), sem("pv_done"), sem("den_done"), sem("h_scaled")
        ht_done, ht_copied, proj_done, x3_done = sem("ht_done"), sem("ht_copied"), sem("proj_done"), sem("x3_done")
        x3_kept = sem("x3_kept")
        pad_hi_done, pad_lo_done, conv_done, conv_copied = sem("pad_hi_done"), sem("pad_lo_done"), sem("conv_done"), sem("conv_copied")
        dot3_done, v3t_done, logit3_done, nmax3_done = sem("dot3_done"), sem("v3t_done"), sem("logit3_done"), sem("nmax3_done")
        att3_exp, att3_inv_done, att3_scaled, att3t_done = sem("att3_exp"), sem("att3_inv_done"), sem("att3_scaled"), sem("att3t_done")
        att3t_copied, v3t_copied, virt_done, virt_copied = sem("att3t_copied"), sem("v3t_copied"), sem("virt_done"), sem("virt_copied")
        ln_chain, tot3_done, var3_done, rstd3_done, ln_ready = sem("ln_chain"), sem("tot3_done"), sem("var3_done"), sem("rstd3_done"), sem("ln_ready")
        act3_done, last_hi, last_lo, last_conv = sem("act3_done"), sem("last_hi"), sem("last_lo"), sem("last_conv")
        y_done, y_stored = sem("y_done"), sem("y_stored")

        def tiled(t):
            return t[:, :].rearrange("p (t n x) -> p n t x", n=N, x=GPX)

        def halves(t):
            return t[:, :, :].rearrange("p m (e k) -> p m e k", e=2)

        def after(eng, s, value):
            if not (isinstance(value, int) and value <= 0):
                eng.wait_ge(s, value)

        x_d = x.rearrange("n c h w -> c n (h w)")
        out_d = out.rearrange("n c h w -> c n (h w)")

        block = ctx.enter_context(nc.Block())

        @block.sync
        def _(sp):
            sp.dma_start(x_in[:, :, :], x_d[:, 0:2, :]).then_inc(x_loaded, 16)
            sp.dma_start(cst[:, :], small).then_inc(cst_loaded, 16)
            for k in range(4):
                if k:
                    sp.wait_ge(w_split, k)
                sp.dma_start(w_stage[:, :], convs[:, k * TAPS * C:(k + 1) * TAPS * C]).then_inc(wst_loaded, 16)
            with sp.Fori(1, PAIRS) as i:
                sp.wait_ge(xt_done, i)
                sp.wait_ge(o0_done, i)
                sp.wait_ge(sum_x_done, i)
                sp.wait_ge(diff0_done, i)
                sp.dma_start(x_in[:, :, :], x_d[:, bass.ds(2 * i, 2), :]).then_inc(x_loaded, 16)
            with sp.Fori(0, PAIRS) as i:
                sp.wait_ge(y_done, i + 1)
                sp.dma_start(out_d[:, bass.ds(2 * i, 2), :], y[:, bass.ds(i * PX, PX)]
                             .rearrange("p (m x) -> p m x", m=2)).then_inc(y_stored, 16)
            sp.wait_ge(y_stored, 16 * PAIRS)

        @block.gpsimd
        def _(pool):
            pool.memset(pow_half[:, :], -0.5).then_inc(pool_set, 1)
            pool.memset(red[:, :, :], 0.0).then_inc(pool_set, 1)
            pool.memset(pad_hi[:, :, :, :, :].bitcast(F32), 0.0).then_inc(pool_set, 1)
            pool.memset(pad_lo[:, :, :, :, :].bitcast(F32), 0.0).then_inc(pool_set, 1)
            pool.memset(nmax2[:, :, :, :, :], 0.0).then_inc(pool_set, 1)
            pool.memset(v_t[:, :, :, :, :], 1.0).then_inc(pool_set, 1)
            pool.wait_ge(vec_pre, 1)
            pool.wait_ge(pool_set, 1)
            pool.tensor_tensor(bn_tmp[:, 1:2], bn_tmp[:, 0:1], pow_half[:, 0:1], ALU.pow).then_inc(bn_pow, 1)

            def split_weights(k):
                hi = w_hi[:, k, :, :].rearrange("p t c -> p (t c)")
                lo = w_lo[:, k, :, :].rearrange("p t c -> p (t c)")
                pool.wait_ge(wst_loaded, 16 * (k + 1))
                pool.tensor_copy(hi, w_stage[:, :]).then_inc(w_split_hi, 1)
                pool.wait_ge(w_split_hi, k + 1)
                pool.tensor_tensor(lo, w_stage[:, :], hi.bitcast(F32), ALU.subtract).then_inc(w_split, 1)

            def pair(i):
                pool.wait_ge(o0_scaled, 2 * i + 2)
                pool.wait_ge(x_loaded, 16 * i + 16)
                pool.tensor_tensor(diff0[:, :, :], x_in[:, :, :], o0[:, :, :], ALU.subtract).then_inc(diff0_done, 1)
                pool.wait_ge(n2m_done, i + 1)
                pool.tensor_tensor(rn[:, :], n2m[:, :], pow_half[:, 0:1], ALU.pow).then_inc(rn_done, 1)
                pool.wait_ge(ab_copied, i + 1)
                pool.tensor_tensor(b_signed[:, :], ab[:, 1, :], c("sign_b").to_broadcast([P, P]), ALU.mult).then_inc(b_signed_done, 1)
                pool.tensor_tensor(ab_sq[:, :, :], ab[:, :, :], ab[:, :, :], ALU.mult).then_inc(squares_done, 1)
                pool.tensor_tensor(a_times_b[:, :], ab[:, 0, :], ab[:, 1, :], ALU.mult).then_inc(squares_done, 1)
                pool.wait_ge(gvar_done, i + 1)
                pool.tensor_tensor(grstd[:, :], gvar[:, :], pow_half[:, 0:2], ALU.pow).then_inc(grstd_done, 1)
                for m in range(2):
                    x3_m = x3_pair[:, m, :].rearrange("p (h w) -> p h w", w=W)
                    hi = pad_hi[:, 0, m, 1:H + 1, 1:W + 1]
                    pool.wait_ge(pad_hi_done, 2 * i + m + 1)
                    pool.tensor_tensor(pad_lo[:, 0, m, 1:H + 1, 1:W + 1], x3_m, hi.bitcast(F32),
                                       ALU.subtract).then_inc(pad_lo_done, 1)
                pool.tensor_copy(x3[:, bass.ds(i * PX, PX)],
                                 x3_pair[:, :, :].rearrange("p m x -> p (m x)")).then_inc(x3_kept, 1)

            for k in range(3):
                split_weights(k)
            pool.wait_ge(pool_set, 6)
            pair(0)
            split_weights(3)
            with pool.Fori(1, PAIRS) as i:
                pair(i)
            pool.wait_ge(var3_done, 1)
            pool.tensor_tensor(rstd3[:, :], var3[:, :], pow_half[:, :], ALU.pow).then_inc(rstd3_done, 1)

        @block.scalar
        def _(act):
            def conv_copy(i, w):
                act.wait_ge(conv_done, 3 * i + w + 1)
                act.activation(tiled(qkv3[w])[:, bass.ds(2 * i, 2), :, :],
                               bank[CONV + w][:, :].rearrange("p (m t x) -> p m t x", m=2, x=GPX),
                               ACT.Copy).then_inc(conv_copied, 1)

            def pair(i, convs_of=None):
                act.wait_ge(e_min_done, i + 1)
                for m in range(2):
                    act.activation(att0[:, m, :], bank[1][:, m * C:(m + 1) * C], ACT.Exp, bias=e_min[:, m:m + 1],
                                   scale=-1.0, accum_out=att0_sum[:, m:m + 1]).then_inc(att0_exp, 1)
                act.wait_ge(att0t_done, i + 1)
                act.activation(att0_t[:, :, :], bank[2][:, 0:2 * C], ACT.Copy).then_inc(att0t_copied, 1)
                act.wait_ge(o0_done, i + 1)
                act.wait_ge(att0_inv_done, i + 1)
                after(act, x1_done, 2 * i)
                for m in range(2):
                    act.activation(o0[:, m, :], bank[3][:, m * HW:(m + 1) * HW], ACT.Identity,
                                   scale=att0_inv[:, m:m + 1], accum_out=sum_o0[:, m:m + 1]).then_inc(o0_scaled, 1)
                act.wait_ge(hid0_done, i + 1)
                act.activation(hid0[:, :], bank[4][0:HID0, 0:2], ACT.Relu, bias=c("b1", HID0),
                               scale=1.0 / HW).then_inc(hid0_relu, 1)
                act.wait_ge(z0_done, i + 1)
                act.activation(z0[:, :], bank[0][:, 0:2], ACT.Exp, bias=neg_b2[:, :], scale=-1.0).then_inc(z0_exp, 1)
                act.wait_ge(red_done, i + 1)
                act.activation(red[:, 1:H + 1, 1:W + 1], bank[1][:, 0:HW].rearrange("p (h w) -> p h w", w=W),
                               ACT.Identity, bias=c("reduce_b")).then_inc(red_copied, 1)
                if convs_of is not None:
                    conv_copy(convs_of, 0)
                act.wait_ge(dw_tap, TAPS * i + TAPS)
                act.activation(xr[:, :], dwa[:, :, :].rearrange("p h w -> p (h w)"), ACT.Relu, bias=bn_shift[:, :],
                               scale=bn_scale[:, :], accum_out=sum_xr[:, :]).then_inc(xr_done, 1)
                act.wait_ge(xr_done, i + 1)
                act.activation(sq_junk[:, :], xr[:, :], ACT.Square, accum_out=n2[:, :]).then_inc(n2_done, 1)
                act.wait_ge(hid1_done, i + 1)
                act.activation(hid1[:, :], bank[4][0:2 * HID1, 0:1], ACT.Relu, bias=c("gb1", 2 * HID1),
                               scale=1.0 / HW).then_inc(hid1_relu, 1)
                act.wait_ge(z1_done, i + 1)
                act.activation(z1[:, :], bank[4][:, 0:1], ACT.Exp, bias=neg_gb2[:, :], scale=-1.0).then_inc(z1_exp, 1)
                act.wait_ge(dft_done, i + 1)
                act.activation(ab[:, :, :], bank[3][:, 0:2 * P], ACT.Copy).then_inc(ab_copied, 1)
                act.wait_ge(even_done, i + 1)
                act.activation(even[:, :], bank[1][:, 0:HW], ACT.Copy).then_inc(even_copied, 1)
                act.wait_ge(nmax1_done, i + 1)
                act.activation(att1[:, :], logit1[:, :], ACT.Exp, bias=nmax1[:, :],
                               accum_out=att1_sum[:, :]).then_inc(att1_exp, 1)
                act.wait_ge(filt_done, i + 1)
                act.wait_ge(z1_chain, 3 * i + 3)
                act.activation(filt[:, :], bank[2][:, 0:HW], ACT.Identity, scale=fscale[:, :]).then_inc(filt_scaled, 1)
                for q in range(QUADS):
                    act.wait_ge(qk_done, 4 * i + q + 1)
                    act.activation(q_hm[:, q, :], bank[q][:, :], ACT.Identity, bias=bq_lo[:, q:q + 1],
                                   scale=c("lo_rows")).then_inc(qk_high, 1)
                for q in range(QUADS):
                    act.wait_ge(qk_done, 4 * i + QUADS + q + 1)
                    act.activation(k_hi[:, q, :], bank[QUADS + q][:, :], ACT.Identity,
                                   bias=c("bk")[:, q:q + 1]).then_inc(qk_high, 1)
                if convs_of is not None:
                    conv_copy(convs_of, 1)
                for m in range(2):
                    act.wait_ge(maxt_done, 2 * i + m + 1)
                    act.activation(nmax2_t[:, :, :], bank[4][:, :], ACT.Copy).then_inc(maxt_copied, 1)
                    for h in range(HEADS):
                        n = HEADS * m + h
                        act.wait_ge(st_done, 2 * HEADS * i + n + 1)
                        if n >= 3:
                            act.wait_ge(pv_done, 2 * HEADS * i + n - 2)
                        act.activation(prob[:, n % 3, :, :], bank[2 + h % 2][:, :], ACT.Exp,
                                       scale=L2_SCALE).then_inc(st_exp, 1)
                    if m == 1 and convs_of is not None:
                        conv_copy(convs_of, 2)
                    act.wait_ge(ht_done, 2 * i + m + 1)
                    act.activation(h_c[:, m, :], bank[0][:, 0:HW], ACT.Copy).then_inc(ht_copied, 1)

            act.wait_ge(vec_set, 5)
            act.wait_ge(cst_loaded, 16)
            act.wait_ge(pool_set, 6)
            pair(0)
            with act.Fori(1, PAIRS) as i:
                pair(i, convs_of=i - 1)
            for w in range(3):
                conv_copy(PAIRS - 1, w)
            for b in range(BATCHES):
                act.wait_ge(nmax3_done, b + 1)
                if b:
                    act.wait_ge(att3_scaled, b)
                for g in range(BATCH):
                    act.activation(att3[:, g, :], logit3[:, g, :], ACT.Exp, bias=nmax3[:, g:g + 1],
                                   accum_out=att3_sum[:, g:g + 1]).then_inc(att3_exp, 1)
                act.wait_ge(v3t_done, b + 1)
                if b >= 2:
                    act.wait_ge(virt_done, b - 1)
                act.activation(v3_t[:, b % 2, :, :], bank[2 + b % 2][:, :], ACT.Copy).then_inc(v3t_copied, 1)
                act.wait_ge(att3t_done, b + 1)
                act.activation(att3_t[:, b % 2, :, :], bank[4 + b % 2][:, :], ACT.Copy).then_inc(att3t_copied, 1)
            act.wait_ge(ln_ready, 1)
            with act.Fori(0, N) as n:
                act.activation(act3[:, bass.ds(n * HW, HW)].rearrange("p (t x) -> p t x", x=GPX),
                               tiled(virt)[:, bass.ds(n, 1), :, :], ACT.Relu, bias=lb[:, bass.ds(n, 1)],
                               scale=la[:, bass.ds(n, 1)]).then_inc(act3_done, 1)

        @block.vector
        def _(dve):
            dve.memset(ones_r[:, :].bitcast(F32), 1.0).then_inc(vec_set, 1)
            dve.wait_ge(cst_loaded, 16)
            dve.tensor_scalar(bn_tmp[:, 0:1], c("bn_var"), 1e-5, None, ALU.add).then_inc(vec_pre, 1)
            dve.tensor_scalar(neg_b2[:, :], c("b2"), -1.0, None, ALU.mult).then_inc(vec_set, 1)
            dve.tensor_scalar(neg_gb2[:, :], c("gb2"), -1.0, None, ALU.mult).then_inc(vec_set, 1)
            dve.tensor_scalar(bq_lo[:, :], c("bq"), c("lo_rows"), None, ALU.mult).then_inc(vec_set, 1)
            dve.tensor_tensor(bn_shift[:, :], c("dw_b"), c("bn_mean"), ALU.subtract).then_inc(vec_pre, 1)
            dve.wait_ge(bn_pow, 1)
            dve.tensor_tensor(bn_scale[:, :], bn_tmp[:, 1:2], c("bn_gamma"), ALU.mult).then_inc(vec_pre, 1)
            dve.wait_ge(vec_pre, 3)
            dve.scalar_tensor_tensor(bn_shift[:, :], bn_shift[:, :], bn_scale[:, :], c("bn_beta"),
                                     ALU.mult, ALU.add).then_inc(vec_set, 1)
            dve.wait_ge(bias_mm, 1)
            dve.tensor_tensor(proj_bias[:, :], bank[7][:, 0:1], c("bproj"), ALU.add).then_inc(vec_set, 1)
            dve.wait_ge(vec_set, 6)
            dve.wait_ge(pool_set, 6)

            def pair(i):
                dve.wait_ge(xt_done, i + 1)
                dve.tensor_copy(x_t[:, :, :, :].rearrange("p m k c -> p (m k c)"), bank[0][:, :]).then_inc(xt_copied, 1)
                dve.wait_ge(x_loaded, 16 * i + 16)
                dve.tensor_reduce(sum_x[:, :], x_in[:, :, :], X, ALU.add).then_inc(sum_x_done, 1)
                dve.wait_ge(energy_done, i + 1)
                dve.tensor_reduce(e_min[:, :], bank[1][:, 0:2 * C].rearrange("p (m c) -> p m c", m=2), X,
                                  ALU.min).then_inc(e_min_done, 1)
                dve.wait_ge(att0_exp, 2 * i + 2)
                dve.reciprocal(att0_inv[:, :], att0_sum[:, :]).then_inc(att0_inv_done, 1)
                dve.wait_ge(z0_exp, i + 1)
                dve.tensor_scalar(z0p[:, :], z0[:, :], 1.0, None, ALU.add).then_inc(z0_chain, 1)
                dve.wait_ge(z0_chain, 2 * i + 1)
                dve.reciprocal(se[:, :], z0p[:, :]).then_inc(z0_chain, 1)
                dve.wait_ge(z0_chain, 2 * i + 2)
                dve.wait_ge(diff0_done, i + 1)
                for m in range(2):
                    dve.scalar_tensor_tensor(x1[:, m, :], diff0[:, m, :], se[:, m:m + 1], o0[:, m, :],
                                             ALU.mult, ALU.add).then_inc(x1_done, 1)
                dve.wait_ge(red_copied, i + 1)
                for t in range(TAPS):
                    tap = red[:, t // 3:t // 3 + H, t % 3:t % 3 + W]
                    wt = c("dw")[:, t:t + 1]
                    if t == 0:
                        dve.tensor_scalar(dwa[:, :, :], tap, wt, None, ALU.mult).then_inc(dw_tap, 1)
                    else:
                        dve.wait_ge(dw_tap, TAPS * i + t)
                        dve.scalar_tensor_tensor(dwa[:, :, :], tap, wt, dwa[:, :, :], ALU.mult,
                                                 ALU.add).then_inc(dw_tap, 1)
                dve.wait_ge(n2_done, i + 1)
                dve.tensor_scalar(n2m[:, :], n2[:, :], 1e-24, None, ALU.max).then_inc(n2m_done, 1)
                dve.wait_ge(rn_done, i + 1)
                dve.tensor_scalar(xh[:, :], xr[:, :], rn[:, :], None, ALU.mult).then_inc(xh_done, 1)
                dve.wait_ge(n2m_done, i + 1)
                dve.tensor_tensor(nrm[:, :], n2m[:, :], rn[:, :], ALU.mult).then_inc(xh_done, 1)
                dve.wait_ge(xht_done, i + 1)
                dve.tensor_copy(xh_t[:, :, :].rearrange("p k c -> p (k c)"), bank[2][:, 0:HW]).then_inc(xht_copied, 1)
                dve.wait_ge(z1_exp, i + 1)
                dve.tensor_scalar(z1p[:, :], z1[:, :], 1.0, None, ALU.add).then_inc(z1_chain, 1)
                dve.wait_ge(z1_chain, 3 * i + 1)
                dve.reciprocal(gate1[:, :], z1p[:, :]).then_inc(z1_chain, 1)
                dve.wait_ge(z1_chain, 3 * i + 2)
                dve.tensor_tensor(fscale[:, :], gate1[:, :], n2m[:, :], ALU.mult).then_inc(z1_chain, 1)
                dve.wait_ge(dot1_done, i + 1)
                dve.scalar_tensor_tensor(logit1[:, :], bank[0][:, 0:P], c("temp"), c("mask1"), ALU.mult,
                                         ALU.add).then_inc(logit1_done, 1)
                dve.wait_ge(logit1_done, i + 1)
                dve.tensor_reduce(nmax1[:, :], logit1[:, :], X, ALU.max, negate=True).then_inc(nmax1_done, 1)
                dve.wait_ge(att1_exp, i + 1)
                dve.reciprocal(att1_inv[:, :], att1_sum[:, :]).then_inc(att1_chain, 1)
                dve.wait_ge(att1_chain, 2 * i + 1)
                dve.tensor_scalar(att1_n[:, :], att1[:, :], att1_inv[:, :], None, ALU.mult).then_inc(att1_chain, 1)
                dve.wait_ge(patt_done, i + 1)
                dve.wait_ge(xh_done, 2 * i + 2)
                dve.tensor_scalar(post_att[:, :], bank[3][:, 0:C], nrm[:, :], None, ALU.mult).then_inc(patt_copied, 1)
                dve.wait_ge(y1_done, i + 1)
                dve.wait_ge(x1_done, 2 * i + 2)
                for m in range(2):
                    dve.scalar_tensor_tensor(x2[:, m, :], bank[Y_BANK[m]][:, 0:HW], c("post_b"), x1[:, m, :],
                                             ALU.add, ALU.add).then_inc(x2_done, 1)
                for m in range(2):
                    dve.wait_ge(x2_done, 2 * i + m + 1)
                    dve.bn_stats(stats[:, m, :], x2[:, m, :]).then_inc(gn_chain, 1)
                dve.wait_ge(gn_chain, 7 * i + 2)
                dve.tensor_tensor(msq[:, :, :], halves(stats)[:, :, :, 1], halves(stats)[:, :, :, 1],
                                  ALU.mult).then_inc(gn_chain, 1)
                dve.wait_ge(gn_chain, 7 * i + 3)
                dve.scalar_tensor_tensor(halves(stats)[:, :, :, 2], halves(stats)[:, :, :, 2], 2.0 / HW,
                                         msq[:, :, :], ALU.mult, ALU.add).then_inc(gn_chain, 1)
                dve.wait_ge(gsum_done, i + 1)
                dve.tensor_copy(gmv[:, :, :].rearrange("p m k -> p (m k)"), bank[0][:, 0:4]).then_inc(gn_chain, 1)
                dve.wait_ge(gn_chain, 7 * i + 5)
                dve.tensor_tensor(gm2[:, :], gmv[:, :, 0], gmv[:, :, 0], ALU.mult).then_inc(gn_chain, 1)
                dve.wait_ge(gn_chain, 7 * i + 6)
                dve.tensor_tensor(gm2[:, :], gmv[:, :, 1], gm2[:, :], ALU.subtract).then_inc(gn_chain, 1)
                dve.wait_ge(gn_chain, 7 * i + 7)
                dve.tensor_scalar(gvar[:, :], gm2[:, :], 1e-5, None, ALU.add).then_inc(gvar_done, 1)
                dve.wait_ge(grstd_done, i + 1)
                dve.tensor_scalar(ga[:, :], grstd[:, :], c("gn_gamma"), None, ALU.mult).then_inc(xn_done, 1)
                dve.wait_ge(xn_done, 5 * i + 1)
                dve.tensor_tensor(gma[:, :], gmv[:, :, 0], ga[:, :], ALU.mult).then_inc(xn_done, 1)
                dve.wait_ge(xn_done, 5 * i + 2)
                dve.tensor_scalar(gb[:, :], gma[:, :], -1.0, c("gn_beta"), ALU.mult, ALU.add).then_inc(xn_done, 1)
                dve.wait_ge(xn_done, 5 * i + 3)
                for m in range(2):
                    dve.tensor_scalar(xn[:, m, :], x2[:, m, :], ga[:, m:m + 1], gb[:, m:m + 1], ALU.mult,
                                      ALU.add).then_inc(xn_done, 1)
                for q in range(QUADS):
                    dve.wait_ge(qk_high, 4 * i + q + 1)
                    dve.scalar_tensor_tensor(q_hl[:, q, :], bank[q][:, :], c("bq")[:, q:q + 1],
                                             q_hm[:, q, :].bitcast(F32), ALU.add, ALU.subtract).then_inc(qk_low, 1)
                for q in range(QUADS):
                    dve.wait_ge(qk_high, 4 * i + QUADS + q + 1)
                    dve.scalar_tensor_tensor(k_lo[:, q, :], bank[QUADS + q][:, :], c("bk")[:, q:q + 1],
                                             k_hi[:, q, :].bitcast(F32), ALU.add, ALU.subtract).then_inc(qk_low, 1)
                dve.wait_ge(v_done, i + 1)
                for m in range(2):
                    dve.tensor_copy(v_t[:, m, :, :, 0:DH].rearrange("p k h d -> p (k h) d"),
                                    bank[4][:, m * HW:(m + 1) * HW].rearrange("p (n d) -> p n d", d=DH)
                                    ).then_inc(v_copied, 1)

                def row_max(n):
                    m, h = n // HEADS, n % HEADS
                    dve.wait_ge(s_done, 2 * HEADS * i + n + 1)
                    col = SLOT * (h % 4)
                    dve.tensor_reduce(nmax2[:, m, :, h // 4, col:col + 1],
                                      bank[h % 2][:, :].rearrange("p (k s) -> p k s", k=CH), X, ALU.max,
                                      negate=True).then_inc(s_max, 1)

                for h in range(HEADS):
                    row_max(h)
                for m in range(2):
                    if m == 0:
                        for h in range(HEADS):
                            row_max(HEADS + h)
                    out_h = bank[4][:, 0:CH * HEADS * VW].rearrange("p (n w) -> p n w", w=VW)
                    dve.wait_ge(pv_done, 2 * HEADS * i + HEADS * (m + 1))
                    dve.reciprocal(den2[:, :, :].rearrange("p k h -> p (k h)"), out_h[:, :, DH]).then_inc(den_done, 1)
                    dve.wait_ge(den_done, 2 * i + m + 1)
                    dve.tensor_tensor(h_t[:, :, :].rearrange("p k (h d) -> p (k h) d", d=DH), out_h[:, :, 0:DH],
                                      den2[:, :, :].rearrange("p k h -> p (k h)").unsqueeze(2)
                                      .to_broadcast([P, CH * HEADS, DH]), ALU.mult).then_inc(h_scaled, 1)
                dve.wait_ge(proj_done, i + 1)
                after(dve, x3_kept, i)
                for m in range(2):
                    dve.scalar_tensor_tensor(x3_pair[:, m, :], bank[1][:, m * HW:(m + 1) * HW],
                                             proj_bias[:, :], x2[:, m, :], ALU.add, ALU.add).then_inc(x3_done, 1)
                after(dve, conv_done, 3 * i)
                for m in range(2):
                    dve.wait_ge(x3_done, 2 * i + m + 1)
                    dve.tensor_copy(pad_hi[:, 0, m, 1:H + 1, 1:W + 1],
                                    x3_pair[:, m, :].rearrange("p (h w) -> p h w", w=W)).then_inc(pad_hi_done, 1)

            pair(0)
            with dve.Fori(1, PAIRS) as i:
                pair(i)
            mask = c("mask3").unsqueeze(1).to_broadcast([P, BATCH, P])
            for b in range(BATCHES):
                dve.wait_ge(dot3_done, b + 1)
                if b:
                    dve.wait_ge(att3_exp, BATCH * b)
                dve.scalar_tensor_tensor(logit3[:, :, :], bank[b % 2][:, :].rearrange("p (g x) -> p g x", g=BATCH),
                                         L3_SCALE, mask, ALU.mult, ALU.add).then_inc(logit3_done, 1)
                dve.wait_ge(logit3_done, b + 1)
                dve.tensor_reduce(nmax3[:, :], logit3[:, :, :], X, ALU.max, negate=True).then_inc(nmax3_done, 1)
                dve.wait_ge(att3_exp, BATCH * (b + 1))
                dve.reciprocal(att3_inv[:, :], att3_sum[:, :]).then_inc(att3_inv_done, 1)
                dve.wait_ge(att3_inv_done, b + 1)
                if b:
                    dve.wait_ge(att3t_done, b)
                dve.tensor_tensor(att3_n[:, :, :], att3[:, :, :],
                                  att3_inv[:, :].unsqueeze(2).to_broadcast([P, BATCH, P]),
                                  ALU.mult).then_inc(att3_scaled, 1)
                dve.wait_ge(virt_done, b + 1)
                dve.tensor_copy(virt[:, b * BATCH * P:(b + 1) * BATCH * P], bank[6 + b % 2][:, :]).then_inc(virt_copied, 1)
            dve.wait_ge(virt_copied, BATCHES)
            for n in range(N):
                dve.bn_stats(stats3[:, n, :], tiled(virt)[:, n, :, :]).then_inc(ln_chain, 1)
            k = N
            dve.wait_ge(ln_chain, k)
            dve.tensor_tensor(msq3[:, :, :], halves(stats3)[:, :, :, 1], halves(stats3)[:, :, :, 1],
                              ALU.mult).then_inc(ln_chain, 1)
            dve.wait_ge(ln_chain, k + 1)
            dve.scalar_tensor_tensor(halves(stats3)[:, :, :, 2], halves(stats3)[:, :, :, 2], 2.0 / HW,
                                     msq3[:, :, :], ALU.mult, ALU.add).then_inc(ln_chain, 1)
            dve.wait_ge(tot3_done, 1)
            dve.tensor_copy(tmv3[:, :, :].rearrange("p n k -> p (n k)"), bank[0][:, 0:2 * N]).then_inc(ln_chain, 1)
            dve.wait_ge(ln_chain, k + 3)
            dve.tensor_tensor(tm3[:, :], tmv3[:, :, 0], tmv3[:, :, 0], ALU.mult).then_inc(ln_chain, 1)
            dve.wait_ge(ln_chain, k + 4)
            dve.tensor_tensor(tm3[:, :], tmv3[:, :, 1], tm3[:, :], ALU.subtract).then_inc(ln_chain, 1)
            dve.wait_ge(ln_chain, k + 5)
            dve.tensor_scalar(var3[:, :], tm3[:, :], 1e-5, None, ALU.add).then_inc(var3_done, 1)
            dve.wait_ge(rstd3_done, 1)
            dve.tensor_scalar(la[:, :], rstd3[:, :], c("ln_gamma"), None, ALU.mult).then_inc(ln_chain, 1)
            dve.wait_ge(ln_chain, k + 6)
            dve.tensor_tensor(lma[:, :], tmv3[:, :, 0], la[:, :], ALU.mult).then_inc(ln_chain, 1)
            dve.wait_ge(ln_chain, k + 7)
            dve.tensor_scalar(lb[:, :], lma[:, :], -1.0, c("ln_beta"), ALU.mult, ALU.add).then_inc(ln_ready, 1)

            def split_act(i, s):
                dve.wait_ge(act3_done, 4 * i + 2 * s + 2)
                after(dve, last_conv, 2 * i + s - 1)
                r = act3[:, bass.ds((2 * i + s) * PX, PX)].rearrange("p (m h w) -> p m h w", m=2, w=W)
                for m in range(2):
                    dve.tensor_copy(pad_hi[:, s, m, 1:H + 1, 1:W + 1], r[:, m, :, :]).then_inc(last_hi, 1)
                dve.wait_ge(last_hi, 4 * i + 2 * s + 2)
                for m in range(2):
                    ins = dve.tensor_tensor(pad_lo[:, s, m, 1:H + 1, 1:W + 1], r[:, m, :, :],
                                            pad_hi[:, s, m, 1:H + 1, 1:W + 1].bitcast(F32), ALU.subtract)
                ins.then_inc(last_lo, 1)

            def add_residual(i, s):
                dve.wait_ge(last_conv, 2 * i + s + 1)
                dve.tensor_tensor(y[:, bass.ds((2 * i + s) * PX, PX)], bank[s][:, :],
                                  x3[:, bass.ds((2 * i + s) * PX, PX)], ALU.add).then_inc(y_done, 1)

            def last_round(i):
                split_act(i, 0)
                if not (isinstance(i, int) and i == 0):
                    add_residual(i - 1, 1)
                split_act(i, 1)
                add_residual(i, 0)

            dve.wait_ge(x3_kept, PAIRS)
            dve.wait_ge(conv_done, 3 * PAIRS)
            last_round(0)
            with dve.Fori(1, PAIRS // 2) as i:
                last_round(i)
            add_residual(PAIRS // 2 - 1, 1)

        @block.tensor
        def _(pe):
            mm, tr = pe.matmul, pe.transpose
            ident = c("ident")

            def conv_taps(w, slot, dst, t0, t1, s=None):
                last = None
                for t in range(t0, t1):
                    r = [p[:, slot, :, t // 3:t // 3 + H, t % 3:t % 3 + W] for p in (pad_hi, pad_lo)]
                    mm(dst, w_hi[:, w, t, :], r[0], start=(t == 0), stop=False)
                    mm(dst, w_hi[:, w, t, :], r[1], start=False, stop=False)
                    last = mm(dst, w_lo[:, w, t, :], r[0], start=False, stop=(t == TAPS - 1))
                if s is not None and t1 == TAPS:
                    last.then_inc(s, 1)

            def fill(j, w, t0, t1):
                if j is None:
                    return
                if t0 == 0 and w == 0:
                    pe.wait_ge(pad_lo_done, 2 * j + 2)
                conv_taps(w, 0, bank[CONV + w][:, :], t0, t1, conv_done)

            def pair(i, j=None):
                pe.wait_ge(x_loaded, 16 * i + 16)
                after(pe, ht_copied, 2 * i)
                for m in range(2):
                    for k in range(CH):
                        o = (m * CH + k) * C
                        ins = tr(bank[0][:, o:o + C], x_in[:, m, k * P:(k + 1) * P], ident)
                ins.then_inc(xt_done, 1)
                fill(j, 0, 0, 2)
                pe.wait_ge(xt_copied, i + 1)
                after(pe, x3_done, 2 * i)
                for m in range(2):
                    for k in range(CH):
                        ins = mm(bank[1][:, m * C:(m + 1) * C], x_t[:, m, k, :], x_t[:, m, k, :],
                                 start=(k == 0), stop=(k == CH - 1))
                ins.then_inc(energy_done, 1)
                fill(j, 0, 2, 5)
                pe.wait_ge(att0_exp, 2 * i + 2)
                for m in range(2):
                    ins = tr(bank[2][:, m * C:(m + 1) * C], att0[:, m, :], ident)
                ins.then_inc(att0t_done, 1)
                fill(j, 0, 5, 7)
                pe.wait_ge(att0t_copied, i + 1)
                for m in range(2):
                    ins = mm(bank[3][:, m * HW:(m + 1) * HW], att0_t[:, m, :], x_in[:, m, :], start=True, stop=True)
                ins.then_inc(o0_done, 1)
                fill(j, 0, 7, 9)
                pe.wait_ge(sum_x_done, i + 1)
                pe.wait_ge(o0_scaled, 2 * i + 2)
                after(pe, h_scaled, 2 * i)
                mm(bank[4][0:HID0, 0:2], c("w1x"), sum_x[:, :], start=True, stop=False)
                mm(bank[4][0:HID0, 0:2], c("w1o"), sum_o0[:, :], start=False, stop=True).then_inc(hid0_done, 1)
                fill(j, 1, 0, 1)
                pe.wait_ge(hid0_relu, i + 1)
                mm(bank[0][:, 0:2], c("w2", HID0), hid0[:, :], start=True, stop=True).then_inc(z0_done, 1)
                fill(j, 1, 1, 3)
                pe.wait_ge(x1_done, 2 * i + 2)
                for m in range(2):
                    ins = mm(bank[1][m * MID:(m + 1) * MID, 0:HW], c("reduce_w"), x1[:, m, :], start=True, stop=True)
                ins.then_inc(red_done, 1)
                fill(j, 1, 3, 8)
                pe.wait_ge(xr_done, i + 1)
                mm(bank[4][0:2 * HID1, 0:1], c("gw1"), sum_xr[:, :], start=True, stop=True).then_inc(hid1_done, 1)
                pe.wait_ge(hid1_relu, i + 1)
                mm(bank[4][:, 0:1], c("gw2", 2 * HID1), hid1[:, :], start=True, stop=True).then_inc(z1_done, 1)
                fill(j, 1, 8, 9)
                pe.wait_ge(xh_done, 2 * i + 1)
                for k in range(CH):
                    ins = tr(bank[2][:, k * P:(k + 1) * P], xh[:, k * P:(k + 1) * P], ident)
                ins.then_inc(xht_done, 1)
                fill(j, 2, 0, 1)
                pe.wait_ge(xht_copied, i + 1)
                fwd = c("fwd").rearrange("p (k r f) -> p k r f", k=CH, r=2)
                for r in range(2):
                    for k in range(CH):
                        ins = mm(bank[3][:, r * P:(r + 1) * P], fwd[:, k, r, :], xh_t[:, k, :],
                                 start=(k == 0), stop=(k == CH - 1))
                ins.then_inc(dft_done, 1)
                fill(j, 2, 1, 2)
                pe.wait_ge(ab_copied, i + 1)
                pe.wait_ge(b_signed_done, i + 1)
                pe.wait_ge(z0_exp, i + 1)
                mm(bank[0][:, 0:P], ab[:, 0, :], ab[:, 0, :], start=True, stop=False)
                mm(bank[0][:, 0:P], ab[:, 1, :], b_signed[:, :], start=False, stop=True).then_inc(dot1_done, 1)
                mm(bank[1][:, 0:HW], ab[:, 0, :], c("even_a"), start=True, stop=False)
                mm(bank[1][:, 0:HW], ab[:, 1, :], c("even_b"), start=False, stop=True).then_inc(even_done, 1)
                pe.wait_ge(squares_done, 2 * i + 2)
                mm(bank[2][:, 0:HW], ab_sq[:, 0, :], c("inv_aa"), start=True, stop=False)
                mm(bank[2][:, 0:HW], ab_sq[:, 1, :], c("inv_bb"), start=False, stop=False)
                mm(bank[2][:, 0:HW], a_times_b[:, :], c("inv_ab"), start=False, stop=True).then_inc(filt_done, 1)
                pe.wait_ge(att1_chain, 2 * i + 2)
                mm(bank[3][:, 0:C], att1_n[:, :], c("post1"), start=True, stop=True).then_inc(patt_done, 1)
                fill(j, 2, 2, 3)
                pe.wait_ge(patt_copied, i + 1)
                pe.wait_ge(even_copied, i + 1)
                pe.wait_ge(filt_scaled, i + 1)
                pe.wait_ge(z1_exp, i + 1)
                for m in range(2):
                    r0 = m * MID
                    mm(bank[Y_BANK[m]][:, 0:HW], post_att[r0:r0 + MID, :], even[r0:r0 + MID, :],
                       start=True, stop=False)
                    ins = mm(bank[Y_BANK[m]][:, 0:HW], c("post2", MID, r0), filt[r0:r0 + MID, :],
                             start=False, stop=True)
                ins.then_inc(y1_done, 1)
                fill(j, 2, 3, 5)
                pe.wait_ge(gn_chain, 7 * i + 4)
                mm(bank[0][:, 0:4], c("group"), halves(stats)[:, :, 0, 1:3], start=True, stop=False)
                mm(bank[0][:, 0:4], c("group"), halves(stats)[:, :, 1, 1:3], start=False, stop=True).then_inc(gsum_done, 1)
                fill(j, 2, 5, 6)
                pe.wait_ge(xn_done, 5 * i + 5)
                xn_all = xn[:, :, :].rearrange("p m x -> p (m x)")
                for q in range(QUADS):
                    mm(bank[q][:, :], c("wq")[:, q * P:(q + 1) * P], xn_all, start=True, stop=True).then_inc(qk_done, 1)
                for q in range(QUADS):
                    mm(bank[QUADS + q][:, :], c("wk")[:, q * P:(q + 1) * P], xn_all, start=True,
                       stop=True).then_inc(qk_done, 1)
                pe.wait_ge(x2_done, 2 * i + 2)
                for m in range(2):
                    for k in range(CH):
                        o = (m * CH + k) * C
                        ins = mm(bank[4][:, o:o + C], xn[:, m, k * P:(k + 1) * P], c("wv"), start=True, stop=True)
                ins.then_inc(v_done, 1)

                def scores(n):
                    m, h = n // HEADS, n % HEADS
                    r = slice(SLOT * (h % 4), SLOT * (h % 4) + SLOT)
                    if n < 2:
                        pe.wait_ge(qk_low, 4 * i + 4)
                    else:
                        pe.wait_ge(s_max, 2 * HEADS * i + n - 1)
                    for k in range(CH):
                        ins = mm(bank[h % 2][:, k * HW:(k + 1) * HW],
                                 q_hl[r, h // 4, m * HW + k * P:m * HW + (k + 1) * P],
                                 k_hi[r, h // 4, m * HW:(m + 1) * HW], start=True, stop=True)
                    ins.then_inc(s_done, 1)

                def scores_t(n):
                    m, h = n // HEADS, n % HEADS
                    r = slice(SLOT * (h % 4), SLOT * (h % 4) + SLOT)
                    if n >= 2:
                        pe.wait_ge(st_exp, 2 * HEADS * i + n - 1)
                    q_m = q_hl[r, h // 4, m * HW:(m + 1) * HW]
                    for k in range(CH):
                        dst = bank[2 + h % 2][:, k * HW:(k + 1) * HW]
                        key = slice(m * HW + k * P, m * HW + (k + 1) * P)
                        mm(dst, k_hi[r, h // 4, key], q_m, start=True, stop=False)
                        mm(dst, k_lo[r, h // 4, key], q_m, start=False, stop=False)
                        ins = mm(dst, ones_r[r, :], nmax2_t[r, h // 4, :], start=False, stop=True)
                    ins.then_inc(st_done, 1)

                def values(n):
                    m, h = n // HEADS, n % HEADS
                    pe.wait_ge(st_exp, 2 * HEADS * i + n + 1)
                    for t in range(CH):
                        o = (t * HEADS + h) * VW
                        for k in range(CH):
                            ins = mm(bank[4][:, o:o + VW], prob[:, n % 3, k, t * P:(t + 1) * P],
                                     v_t[:, m, k, h, :], start=(k == 0), stop=(k == CH - 1))
                    ins.then_inc(pv_done, 1)

                for h in range(HEADS):
                    scores(h)
                    if h == 3:
                        fill(j, 2, 6, 7)
                    if h == 5:
                        fill(j, 2, 7, 9)
                for m in range(2):
                    pe.wait_ge(s_max, 2 * HEADS * i + HEADS * (m + 1))
                    if m == 0:
                        pe.wait_ge(v_copied, 2 * i + 2)
                    else:
                        pe.wait_ge(h_scaled, 2 * i + 1)
                    for q in range(QUADS):
                        for k in range(CH):
                            o = q * HW + k * P
                            ins = tr(bank[4][:, o:o + P], nmax2[:, m, k, q, :], ident)
                    ins.then_inc(maxt_done, 1)
                    pe.wait_ge(maxt_copied, 2 * i + m + 1)
                    for h in range(HEADS):
                        scores_t(HEADS * m + h)
                        if m == 0:
                            scores(HEADS + h)
                        if h:
                            values(HEADS * m + h - 1)
                    values(HEADS * m + HEADS - 1)
                    pe.wait_ge(h_scaled, 2 * i + m + 1)
                    if m == 0:
                        pe.wait_ge(s_max, 2 * HEADS * (i + 1))
                    else:
                        pe.wait_ge(ht_copied, 2 * i + 1)
                    for k in range(CH):
                        ins = tr(bank[0][:, k * P:(k + 1) * P], h_t[:, k, :], ident)
                    ins.then_inc(ht_done, 1)
                if j is not None:
                    pe.wait_ge(conv_copied, 3 * i)
                pe.wait_ge(ht_copied, 2 * i + 2)
                mm(bank[1][:, :], c("wproj"), h_c[:, :, :].rearrange("p m x -> p (m x)"), start=True,
                   stop=True).then_inc(proj_done, 1)

            pe.wait_ge(cst_loaded, 16)
            mm(bank[7][:, 0:1], c("wproj"), c("bv"), start=True, stop=True).then_inc(bias_mm, 1)
            pe.wait_ge(vec_set, 6)
            pair(0)
            pe.wait_ge(w_split, 3)
            with pe.Fori(1, PAIRS) as i:
                pair(i, i - 1)
            for w in range(3):
                fill(PAIRS - 1, w, 0, TAPS)
            pe.wait_ge(conv_copied, 3 * PAIRS)
            pe.wait_ge(x3_done, 2 * PAIRS)
            q3, k3, v3 = qkv3

            def dots(b):
                if b >= 2:
                    pe.wait_ge(logit3_done, b - 1)
                for g in range(BATCH):
                    px = slice((b * BATCH + g) * P, (b * BATCH + g + 1) * P)
                    ins = mm(bank[b % 2][:, g * P:(g + 1) * P], q3[:, px], k3[:, px], start=True, stop=True)
                ins.then_inc(dot3_done, 1)
                if b >= 2:
                    pe.wait_ge(v3t_copied, b - 1)
                for g in range(BATCH):
                    px = slice((b * BATCH + g) * P, (b * BATCH + g + 1) * P)
                    ins = tr(bank[2 + b % 2][:, g * C:(g + 1) * C], v3[:, px], ident)
                ins.then_inc(v3t_done, 1)

            dots(0)
            for b in range(BATCHES):
                if b + 1 < BATCHES:
                    dots(b + 1)
                pe.wait_ge(att3_scaled, b + 1)
                if b >= 2:
                    pe.wait_ge(att3t_copied, b - 1)
                for g in range(BATCH):
                    ins = tr(bank[4 + b % 2][:, g * P:(g + 1) * P], att3_n[:, g, :], ident)
                ins.then_inc(att3t_done, 1)
                pe.wait_ge(att3t_copied, b + 1)
                pe.wait_ge(v3t_copied, b + 1)
                if b >= 2:
                    pe.wait_ge(virt_copied, b - 1)
                for g in range(BATCH):
                    ins = mm(bank[6 + b % 2][:, g * P:(g + 1) * P], v3_t[:, b % 2, g, :], att3_t[:, b % 2, g, :],
                             start=True, stop=True)
                ins.then_inc(virt_done, 1)
            pe.wait_ge(ln_chain, N + 2)
            mm(bank[0][:, 0:2 * N], c("mean_all"), halves(stats3)[:, :, 0, 1:3], start=True, stop=False)
            mm(bank[0][:, 0:2 * N], c("mean_all"), halves(stats3)[:, :, 1, 1:3], start=False, stop=True).then_inc(tot3_done, 1)
            pe.wait_ge(ln_ready, 1)
            pe.wait_ge(w_split, 4)

            def last_convs(i):
                for s in range(2):
                    pe.wait_ge(last_lo, 2 * i + s + 1)
                    after(pe, y_done, 2 * i + s - 1)
                    conv_taps(3, s, bank[s][:, :], 0, TAPS, last_conv)

            last_convs(0)
            with pe.Fori(1, PAIRS // 2) as i:
                last_convs(i)


def constants():
    t = {"ident": np.eye(P, dtype=np.float32)}
    r = np.arange(P)
    t["mask1"] = np.where(r[:, None] // HID1 == r[None, :] // HID1, 0.0, FAR)
    t["mask3"] = np.where(r[:, None] % GPX == r[None, :] % GPX, 0.0, FAR)
    t["group"] = np.where(r[:, None] // GC == r[None, :] // GC, 0.5 / GC, 0.0)
    t["mean_all"] = np.full((P, P), 0.5 / P)
    half = [(0, 0), (0, W // 2), (H // 2, 0), (H // 2, W // 2)]
    pairs, seen = [], set(half)
    for u in range(H):
        for v in range(W):
            if (u, v) not in seen:
                pairs.append((u, v))
                seen |= {(u, v), (-u % H, -v % W)}
    h, w = np.divmod(np.arange(HW), W)
    angle = lambda f: 2 * np.pi * ((f[0] * h + f[1] * w) % H) / H
    root = float(np.sqrt(HW))
    a = [np.cos(angle(f)) / root for f in half[:2]] + [np.sqrt(2) * np.cos(angle(f)) / root for f in pairs]
    b = [np.cos(angle(f)) / root for f in half[2:]] + [np.sqrt(2) * np.sin(angle(f)) / root for f in pairs]
    a, b = np.array(a), np.array(b)
    t["fwd"] = np.stack([a.T.reshape(CH, P, P), b.T.reshape(CH, P, P)], 1).transpose(2, 0, 1, 3).reshape(P, -1)
    t["even_a"] = a
    t["even_b"] = np.where(r[:, None] < 2, b, 0.0)
    t["inv_aa"] = np.array([np.cos(angle(f)) / root for f in half[:2] + pairs])
    t["inv_bb"] = np.array([np.cos(angle(f)) / root for f in half[2:]] + [-np.cos(angle(f)) / root for f in pairs])
    t["inv_ab"] = np.array([0 * h for f in half[2:]] + [2 * np.sin(angle(f)) / root for f in pairs])
    t["sign_b"] = np.where(r < 2, 1.0, -1.0)[:, None]
    t["lo_rows"] = np.where(r % SLOT >= DH, 1.0, 0.0)[:, None]
    return {k: v.astype(np.float32) for k, v in t.items()}


_OUT = ((N, C, H, W), "float32")


def kernel(**inputs):
    import numpy as _np
    import concourse.bacc as _bacc
    from concourse import mybir as _mybir
    from concourse.bass_utils import run_bass_kernel_spmd as _run

    a = {k: _np.asarray(v) for k, v in inputs.items()}
    col = lambda v: v.reshape(-1, 1)
    twice = lambda v: _np.concatenate([v, v], 0)
    q_rows = _np.array([[3 * DH * (4 * q + s // SLOT) + s % DH for s in range(P)] for q in range(QUADS)])
    v_rows = _np.array([3 * DH * h + 2 * DH + d for h in range(HEADS) for d in range(DH)])
    wqkv, bqkv = a["L2_conv_w_qkv"], a["L2_conv_b_qkv"]
    gw1 = _np.zeros((P, 2 * HID1), _np.float32)
    gw2 = _np.zeros((2 * HID1, P), _np.float32)
    for m in range(2):
        gw1[m * MID:(m + 1) * MID, m * HID1:(m + 1) * HID1] = a["L1_conv_gate_w1"].T
        gw2[m * HID1:(m + 1) * HID1, m * MID:(m + 1) * MID] = a["L1_conv_gate_w2"].T
    t = constants()
    t["w1x"], t["w1o"] = a["L0_conv_w1"].T[:C], a["L0_conv_w1"].T[C:]
    t["w2"], t["b1"], t["b2"] = a["L0_conv_w2"].T, col(a["L0_conv_b1"]), col(a["L0_conv_b2"])
    t["reduce_w"] = a["L1_conv_reduce_w"].T
    t["reduce_b"] = twice(col(a["L1_conv_reduce_b"]))
    t["dw"] = twice(a["L1_conv_dw_w"].reshape(MID, TAPS))
    for k in ("dw_b", "bn_gamma", "bn_beta", "bn_mean", "bn_var"):
        t[k] = twice(col(a["L1_conv_" + k]))
    t["gw1"], t["gw2"] = gw1, gw2
    t["gb1"], t["gb2"] = twice(col(a["L1_conv_gate_b1"])), twice(col(a["L1_conv_gate_b2"]))
    t["temp"] = twice(_np.repeat(col(a["L1_conv_temperature"]), MID // 8, 0))
    post = a["L1_conv_post_w"].T
    t["post1"], t["post2"], t["post_b"] = twice(post[:MID]), twice(post[MID:]), col(a["L1_conv_post_b"])
    t["gn_gamma"], t["gn_beta"] = col(a["L2_conv_gamma"]), col(a["L2_conv_beta"])
    t["wq"] = _np.concatenate([wqkv[q_rows[q]].T for q in range(QUADS)], 1)
    t["wk"] = _np.concatenate([wqkv[q_rows[q] + DH].T for q in range(QUADS)], 1)
    t["bq"] = bqkv[q_rows].T
    t["bk"] = bqkv[q_rows + DH].T
    t["wv"], t["bv"] = wqkv[v_rows].T, col(bqkv[v_rows])
    t["wproj"], t["bproj"] = a["L2_conv_w_proj"].T, col(a["L2_conv_b_proj"])
    t["ln_gamma"], t["ln_beta"] = col(a["L3_conv_gamma"]), col(a["L3_conv_beta"])
    small = _np.zeros((P, SMALL_W), _np.float32)
    for k, (b, e) in AT.items():
        small[:t[k].shape[0], b:e] = t[k]
    convs = _np.concatenate([a["L3_conv_W" + k].transpose(1, 2, 3, 0).reshape(C, TAPS * C) for k in "qkvc"], 1)
    arrays = {"x": _np.ascontiguousarray(a["x"]), "small": small, "convs": _np.ascontiguousarray(convs)}

    nc = _bacc.Bacc("TRN2", target_bir_lowering=False, num_devices=1)
    ap = {k: nc.dram_tensor(k, v.shape, _mybir.dt.from_np(v.dtype), kind="ExternalInput").ap()
          for k, v in arrays.items()}
    out = nc.dram_tensor("out", _OUT[0], _mybir.dt.from_np(_np.dtype(_OUT[1])), kind="ExternalOutput").ap()
    program(nc, ap["x"], ap["small"], ap["convs"], out)
    r = _run(nc, [arrays], core_ids=[0])
    return r.results[0]["out"]
```

```python
from contextlib import ExitStack

import numpy as np

import concourse.bass as bass
from concourse import mybir


N, C, H, W = 16, 128, 16, 16
HW = H * W
PAIRS = N // 2
PX = 2 * HW
P = 128
CH = HW // P
HID0 = 2 * C // 16
MID = C // 2
HID1 = MID // 8
HEADS = 8
DH = C // HEADS
SLOT = 32
QUADS = HEADS * SLOT // P
TAPS = 9
PW = W + 2
GC = C // 32
GPX = P // N
BATCH = 4
BATCHES = HW // GPX // BATCH
L2_SCALE = DH ** -0.5
L3_SCALE = float(1.0 / np.sqrt(np.float32(C)))
FAR = -1e30
STAGE = {0: 0, 2: 1, 5: 2, 7: 3, **{s: s - 4 for s in range(8, 21)}}
STAGES = 17
SLOTS = 3 * HEADS
TAPS_IN = [0, 0, 1, 1, 1, 1, 1, 1, 2, 1, 1, 2, 1, 1, 2, 1, 1, 2, 1, 1, 2, 1, 2, 0]
CONV_OUT = {9: 0, 16: 1, 22: 2}

F32 = mybir.dt.float32
F32R = mybir.dt.float32r
ALU = mybir.AluOpType
ACT = mybir.ActivationFunctionType
X = mybir.AxisListType.X

SMALL = [("ident", P), ("mask1", P), ("mask3", P), ("group", P), ("mean_all", P),
         ("fwd", CH * 2 * P), ("inv_aa", HW), ("inv_bb", HW), ("inv_ab", HW),
         ("even_a", HW), ("even_b", HW), ("sign_b", 1), ("lo_rows", 1),
         ("w1x", HID0), ("w1o", HID0), ("w2", C), ("b1", 1), ("b2", 1),
         ("reduce_w", MID), ("reduce_b", 1), ("dw", TAPS), ("dw_b", 1), ("bn_gamma", 1), ("bn_beta", 1),
         ("bn_mean", 1), ("bn_var", 1), ("gw1", 2 * HID1), ("gb1", 1), ("gw2", P), ("gb2", 1),
         ("temp", 1), ("post1", C), ("post2", C), ("post_b", 1),
         ("gn_gamma", 1), ("gn_beta", 1), ("wq", QUADS * P), ("wk", QUADS * P), ("bq", QUADS),
         ("bk", QUADS), ("wv", C), ("bv", 1), ("wproj", C), ("bproj", 1), ("ln_gamma", 1), ("ln_beta", 1)]
AT, _o = {}, 0
for _n, _w in SMALL:
    AT[_n] = (_o, _o + _w)
    _o += _w
SMALL_W = _o


def program(nc, x, small, convs, out):
    with ExitStack() as ctx:
        def sb(name, shape, dt=F32):
            return ctx.enter_context(nc.sbuf_tensor(name, shape, dt))

        def sem(name):
            return ctx.enter_context(nc.semaphore(name))

        cst = sb("cst", [P, SMALL_W])

        def c(name, rows=P, r0=0):
            a, b = AT[name]
            return cst[r0:r0 + rows, a:b]

        w_stage = sb("w_stage", [P, TAPS * C])
        w_hi = sb("w_hi", [P, 4, TAPS, C], F32R)
        w_lo = sb("w_lo", [P, 4, TAPS, C], F32R)
        neg_b2 = sb("neg_b2", [P, 1])
        neg_gb2 = sb("neg_gb2", [P, 1])
        bn_scale = sb("bn_scale", [P, 1])
        bn_shift = sb("bn_shift", [P, 1])
        bn_tmp = sb("bn_tmp", [P, 2])
        bq_lo = sb("bq_lo", [P, QUADS])
        proj_bias = sb("proj_bias", [P, 1])
        pow_half = sb("pow_half", [P, N])
        ones_r = sb("ones_r", [P, P], F32R)
        x_in = sb("x_in", [P, 2, HW])
        x_t = sb("x_t", [P, 2, CH, C])
        e_min = sb("e_min", [P, 2])
        att0 = sb("att0", [P, 2, C])
        att0_t = sb("att0_t", [P, 2, C])
        att0_sum = sb("att0_sum", [P, 2])
        att0_inv = sb("att0_inv", [P, 2])
        o0 = sb("o0", [P, 2, HW])
        diff0 = sb("diff0", [P, 2, HW])
        sum_o0 = sb("sum_o0", [P, 2])
        sum_x = sb("sum_x", [P, 2])
        hid0 = sb("hid0", [HID0, 2])
        z0 = sb("z0", [P, 2])
        z0p = sb("z0p", [P, 2])
        se = sb("se", [P, 2])
        x1 = sb("x1", [P, 2, HW])
        red = sb("red", [P, H + 2, PW])
        dwa = sb("dwa", [P, H, W])
        xr = sb("xr", [P, HW])
        sq_junk = sb("sq_junk", [P, HW])
        sum_xr = sb("sum_xr", [P, 1])
        n2 = sb("n2", [P, 1])
        n2m = sb("n2m", [P, 1])
        rn = sb("rn", [P, 1])
        nrm = sb("nrm", [P, 1])
        xh = sb("xh", [P, HW])
        xh_t = sb("xh_t", [P, CH, P])
        hid1 = sb("hid1", [2 * HID1, 1])
        z1 = sb("z1", [P, 1])
        z1p = sb("z1p", [P, 1])
        gate1 = sb("gate1", [P, 1])
        fscale = sb("fscale", [P, 1])
        ab = sb("ab", [P, 2, P])
        b_signed = sb("b_signed", [P, P])
        ab_sq = sb("ab_sq", [P, 2, P])
        a_times_b = sb("a_times_b", [P, P])
        logit1 = sb("logit1", [P, P])
        nmax1 = sb("nmax1", [P, 1])
        att1 = sb("att1", [P, P])
        att1_sum = sb("att1_sum", [P, 1])
        att1_inv = sb("att1_inv", [P, 1])
        att1_n = sb("att1_n", [P, P])
        even = sb("even", [P, HW])
        filt = sb("filt", [P, HW])
        post_att = sb("post_att", [P, C])
        x2 = sb("x2", [P, 2, HW])
        stats = sb("stats", [P, 2, 6])
        msq = sb("msq", [P, 2, 2])
        gmv = sb("gmv", [P, 2, 2])
        gm2 = sb("gm2", [P, 2])
        gvar = sb("gvar", [P, 2])
        grstd = sb("grstd", [P, 2])
        ga = sb("ga", [P, 2])
        gma = sb("gma", [P, 2])
        gb = sb("gb", [P, 2])
        xn = sb("xn", [P, 2, HW])
        q_hm = sb("q_hm", [P, QUADS, PX], F32R)
        q_hl = sb("q_hl", [P, QUADS, PX], F32R)
        k_hi = sb("k_hi", [P, QUADS, PX], F32R)
        k_lo = sb("k_lo", [P, QUADS, PX], F32R)
        v_t = sb("v_t", [P, 2, CH, HEADS, SLOT])
        nmax2 = sb("nmax2", [P, 2, CH, QUADS, P])
        nmax2_t = sb("nmax2_t", [P, QUADS, HW], F32R)
        prob = sb("prob", [P, 3, CH, HW])
        den2 = sb("den2", [P, CH, HEADS])
        o2 = sb("o2", [P, QUADS, HW])
        h_t = sb("h_t", [P, CH, C])
        x2_res = sb("x2_res", [P, 2, HW])
        h_c = sb("h_c", [P, 2, HW])
        x3 = sb("x3", [P, N * HW])
        x3_pair = sb("x3_pair", [P, 2, HW])
        pad_hi = sb("pad_hi", [P, 2, 2, H + 2, PW], F32R)
        pad_lo = sb("pad_lo", [P, 2, 2, H + 2, PW], F32R)
        qkv3 = [sb(n, [P, N * HW]) for n in ("q3", "k3", "v3")]
        nmax3 = sb("nmax3", [P, 2, BATCH])
        att3_sum = sb("att3_sum", [P, 2, BATCH])
        att3_inv = sb("att3_inv", [P, BATCH])
        logit3 = [prob[:, n, :, :].rearrange("p k x -> p (k x)") for n in range(2)]
        att3 = [x1[:, :, :].rearrange("p m x -> p (m x)"), x2[:, :, :].rearrange("p m x -> p (m x)")]
        att3_n = [x_in[:, :, :].rearrange("p m x -> p (m x)"), xn[:, :, :].rearrange("p m x -> p (m x)")]
        att3_t = [o0[:, :, :].rearrange("p m x -> p (m x)"), diff0[:, :, :].rearrange("p m x -> p (m x)")]
        v3_t = w_stage[:, 0:2 * BATCH * C].rearrange("p (s g c) -> p s g c", s=2, g=BATCH)
        virt = qkv3[0]
        act3 = qkv3[1]
        y = qkv3[2]
        stats3 = sb("stats3", [P, N, 6])
        msq3 = sb("msq3", [P, N, 2])
        tm3 = sb("tm3", [P, N])
        tmv3 = sb("tmv3", [P, N, 2])
        var3 = sb("var3", [P, N])
        rstd3 = sb("rstd3", [P, N])
        la = sb("la", [P, N])
        lma = sb("lma", [P, N])
        lb = sb("lb", [P, N])

        bank = [ctx.enter_context(nc.psum_tensor(f"bank{n}", [P, 512], F32)) for n in range(8)]
        FRONT = (0, 1)
        S_BANK = 2
        ST_BANK = (3, 4)
        O_BANK = 5
        H_BANK = 6
        CONV = 7

        cst_loaded, x_loaded = sem("cst_loaded"), sem("x_loaded")
        wst_loaded = sem("wst_loaded")
        w_split_hi, w_split, w_ready = sem("w_split_hi"), sem("w_split"), sem("w_ready")
        pool_set, vec_set, vec_pre, bias_mm = sem("pool_set"), sem("vec_set"), sem("vec_pre"), sem("bias_mm")
        bn_pow = sem("bn_pow")
        xt_done, xt_copied, energy_done, e_min_done = sem("xt_done"), sem("xt_copied"), sem("energy_done"), sem("e_min_done")
        att0_exp, att0_inv_done, att0t_done, att0t_copied = sem("att0_exp"), sem("att0_inv_done"), sem("att0t_done"), sem("att0t_copied")
        o0_done, o0_scaled, diff0_done, sum_x_done = sem("o0_done"), sem("o0_scaled"), sem("diff0_done"), sem("sum_x_done")
        hid0_done, hid0_relu, z0_done, z0_exp = sem("hid0_done"), sem("hid0_relu"), sem("z0_done"), sem("z0_exp")
        z0_chain, x1_done = sem("z0_chain"), sem("x1_done")
        red_done, red_copied, dw_tap, xr_done, n2_done = sem("red_done"), sem("red_copied"), sem("dw_tap"), sem("xr_done"), sem("n2_done")
        n2m_done, rn_done, xh_done = sem("n2m_done"), sem("rn_done"), sem("xh_done")
        hid1_done, hid1_relu, z1_done, z1_exp, z1_chain = sem("hid1_done"), sem("hid1_relu"), sem("z1_done"), sem("z1_exp"), sem("z1_chain")
        xht_done, xht_copied, dft_done, ab_copied = sem("xht_done"), sem("xht_copied"), sem("dft_done"), sem("ab_copied")
        b_signed_done, squares_done = sem("b_signed_done"), sem("squares_done")
        dot1_done, even_done, filt_done = sem("dot1_done"), sem("even_done"), sem("filt_done")
        logit1_done, nmax1_done, att1_exp, att1_chain = sem("logit1_done"), sem("nmax1_done"), sem("att1_exp"), sem("att1_chain")
        even_copied, filt_scaled, patt_done, patt_copied = sem("even_copied"), sem("filt_scaled"), sem("patt_done"), sem("patt_copied")
        y1_done, x2_done = sem("y1_done"), sem("x2_done")
        gn_chain, gsum_done, gvar_done, grstd_done, xn_done = sem("gn_chain"), sem("gsum_done"), sem("gvar_done"), sem("grstd_done"), sem("xn_done")
        qk_done, v_done, qk_high, qk_low, v_copied = sem("qk_done"), sem("v_done"), sem("qk_high"), sem("qk_low"), sem("v_copied")
        s_done, s_max, maxt_done, maxt_copied = sem("s_done"), sem("s_max"), sem("maxt_done"), sem("maxt_copied")
        st_done, st_exp, pv_done, den_done, h_scaled = sem("st_done"), sem("st_exp"), sem("pv_done"), sem("den_done"), sem("h_scaled")
        o2_copied, ot_done, x2_res_done = sem("o2_copied"), sem("ot_done"), sem("x2_res_done")
        ht_done, ht_copied, proj_done, x3_done = sem("ht_done"), sem("ht_copied"), sem("proj_done"), sem("x3_done")
        x3_kept = sem("x3_kept")
        pad_hi_done, pad_lo_done, conv_done, conv_copied = sem("pad_hi_done"), sem("pad_lo_done"), sem("conv_done"), sem("conv_copied")
        dot3_done, v3t_done, logit3_done, nmax3_done = sem("dot3_done"), sem("v3t_done"), sem("logit3_done"), sem("nmax3_done")
        att3_exp, att3_inv_done, att3_scaled, att3t_done = sem("att3_exp"), sem("att3_inv_done"), sem("att3_scaled"), sem("att3t_done")
        att3t_copied, v3t_copied, virt_done, virt_copied = sem("att3t_copied"), sem("v3t_copied"), sem("virt_done"), sem("virt_copied")
        ln_chain, tot3_done, var3_done, rstd3_done, ln_ready = sem("ln_chain"), sem("tot3_done"), sem("var3_done"), sem("rstd3_done"), sem("ln_ready")
        act3_done, last_hi, last_lo, last_conv = sem("act3_done"), sem("last_hi"), sem("last_lo"), sem("last_conv")
        y_done, y_stored = sem("y_done"), sem("y_stored")

        def tiled(t):
            return t[:, :].rearrange("p (t n x) -> p n t x", n=N, x=GPX)

        def halves(t):
            return t[:, :, :].rearrange("p m (e k) -> p m e k", e=2)

        def after(eng, s, value):
            if not (isinstance(value, int) and value <= 0):
                eng.wait_ge(s, value)

        x_d = x.rearrange("n c h w -> c n (h w)")
        out_d = out.rearrange("n c h w -> c n (h w)")

        block = ctx.enter_context(nc.Block())

        @block.sync
        def _(sp):
            sp.dma_start(x_in[:, :, :], x_d[:, 0:2, :]).then_inc(x_loaded, 16)
            sp.dma_start(cst[:, :], small).then_inc(cst_loaded, 16)
            for k in range(4):
                if k:
                    sp.wait_ge(w_split, k)
                sp.dma_start(w_stage[:, :], convs[:, k * TAPS * C:(k + 1) * TAPS * C]).then_inc(wst_loaded, 16)
            with sp.Fori(1, PAIRS) as i:
                sp.wait_ge(xt_done, i)
                sp.wait_ge(o0_done, i)
                sp.wait_ge(sum_x_done, i)
                sp.wait_ge(diff0_done, i)
                sp.dma_start(x_in[:, :, :], x_d[:, bass.ds(2 * i, 2), :]).then_inc(x_loaded, 16)
            with sp.Fori(0, PAIRS) as i:
                sp.wait_ge(y_done, i + 1)
                sp.dma_start(out_d[:, bass.ds(2 * i, 2), :], y[:, bass.ds(i * PX, PX)]
                             .rearrange("p (m x) -> p m x", m=2)).then_inc(y_stored, 16)
            sp.wait_ge(y_stored, 16 * PAIRS)

        @block.gpsimd
        def _(pool):
            pool.memset(pow_half[:, :], -0.5).then_inc(pool_set, 1)
            pool.memset(red[:, :, :], 0.0).then_inc(pool_set, 1)
            pool.memset(pad_hi[:, :, :, :, :].bitcast(F32), 0.0).then_inc(pool_set, 1)
            pool.memset(pad_lo[:, :, :, :, :].bitcast(F32), 0.0).then_inc(pool_set, 1)
            pool.memset(nmax2[:, :, :, :, :], 0.0).then_inc(pool_set, 1)
            pool.memset(v_t[:, :, :, :, :], 1.0).then_inc(pool_set, 1)
            pool.wait_ge(vec_pre, 1)
            pool.wait_ge(pool_set, 1)
            pool.tensor_tensor(bn_tmp[:, 1:2], bn_tmp[:, 0:1], pow_half[:, 0:1], ALU.pow).then_inc(bn_pow, 1)

            def split_weights(k):
                hi = w_hi[:, k, :, :].rearrange("p t c -> p (t c)")
                lo = w_lo[:, k, :, :].rearrange("p t c -> p (t c)")
                pool.wait_ge(wst_loaded, 16 * (k + 1))
                pool.tensor_copy(hi, w_stage[:, :]).then_inc(w_split_hi, 1)
                pool.wait_ge(w_split_hi, k + 1)
                pool.tensor_tensor(lo, w_stage[:, :], hi.bitcast(F32), ALU.subtract).then_inc(w_split, 1)

            def front(i):
                pool.wait_ge(o0_scaled, 2 * i + 2)
                pool.wait_ge(x_loaded, 16 * i + 16)
                pool.tensor_tensor(diff0[:, :, :], x_in[:, :, :], o0[:, :, :], ALU.subtract).then_inc(diff0_done, 1)
                pool.wait_ge(n2m_done, i + 1)
                pool.tensor_tensor(rn[:, :], n2m[:, :], pow_half[:, 0:1], ALU.pow).then_inc(rn_done, 1)
                pool.wait_ge(ab_copied, i + 1)
                pool.tensor_tensor(b_signed[:, :], ab[:, 1, :], c("sign_b").to_broadcast([P, P]),
                                   ALU.mult).then_inc(b_signed_done, 1)
                pool.tensor_tensor(ab_sq[:, :, :], ab[:, :, :], ab[:, :, :], ALU.mult).then_inc(squares_done, 1)
                pool.tensor_tensor(a_times_b[:, :], ab[:, 0, :], ab[:, 1, :], ALU.mult).then_inc(squares_done, 1)
                pool.wait_ge(gvar_done, i + 1)
                pool.tensor_tensor(grstd[:, :], gvar[:, :], pow_half[:, 0:2], ALU.pow).then_inc(grstd_done, 1)

            def residual(i):
                pool.wait_ge(x2_done, 2 * i + 2)
                after(pool, x3_done, 2 * i)
                pool.tensor_tensor(x2_res[:, :, :].rearrange("p m x -> p (m x)"),
                                   x2[:, :, :].rearrange("p m x -> p (m x)"),
                                   proj_bias[:, :].to_broadcast([P, PX]), ALU.add).then_inc(x2_res_done, 1)

            def low_part(j):
                for m in range(2):
                    pool.wait_ge(pad_hi_done, 2 * j + m + 1)
                    pool.tensor_tensor(pad_lo[:, 0, m, 1:H + 1, 1:W + 1],
                                       x3_pair[:, m, :].rearrange("p (h w) -> p h w", w=W),
                                       pad_hi[:, 0, m, 1:H + 1, 1:W + 1].bitcast(F32),
                                       ALU.subtract).then_inc(pad_lo_done, 1)
                pool.tensor_copy(x3[:, bass.ds(j * PX, PX)],
                                 x3_pair[:, :, :].rearrange("p m x -> p (m x)")).then_inc(x3_kept, 1)

            pool.wait_ge(pool_set, 6)
            split_weights(0)
            front(0)
            split_weights(1)
            split_weights(2)
            pool.wait_ge(vec_set, 6)
            residual(0)
            front(1)
            low_part(0)
            residual(1)
            split_weights(3)
            with pool.Fori(2, PAIRS) as i:
                front(i)
                low_part(i - 1)
                residual(i)
            low_part(PAIRS - 1)
            pool.wait_ge(var3_done, 1)
            pool.tensor_tensor(rstd3[:, :], var3[:, :], pow_half[:, :], ALU.pow).then_inc(rstd3_done, 1)

        @block.scalar
        def _(act):
            def conv_copy(i, w):
                act.wait_ge(conv_done, 3 * i + w + 1)
                act.activation(tiled(qkv3[w])[:, bass.ds(2 * i, 2), :, :],
                               bank[CONV][:, :].rearrange("p (m t x) -> p m t x", m=2, x=GPX),
                               ACT.Copy).then_inc(conv_copied, 1)

            def stage(k, i):
                if k == 1:
                    act.wait_ge(e_min_done, i + 1)
                    for m in range(2):
                        act.activation(att0[:, m, :], bank[1][:, m * C:(m + 1) * C], ACT.Exp, bias=e_min[:, m:m + 1],
                                       scale=-1.0, accum_out=att0_sum[:, m:m + 1]).then_inc(att0_exp, 1)
                if k == 2:
                    act.wait_ge(att0t_done, i + 1)
                    act.activation(att0_t[:, :, :], bank[0][:, 0:2 * C], ACT.Copy).then_inc(att0t_copied, 1)
                if k == 3:
                    act.wait_ge(o0_done, i + 1)
                    act.wait_ge(att0_inv_done, i + 1)
                    after(act, x1_done, 2 * i)
                    for m in range(2):
                        act.activation(o0[:, m, :], bank[1][:, m * HW:(m + 1) * HW], ACT.Identity,
                                       scale=att0_inv[:, m:m + 1], accum_out=sum_o0[:, m:m + 1]).then_inc(o0_scaled, 1)
                if k == 4:
                    act.wait_ge(hid0_done, i + 1)
                    act.activation(hid0[:, :], bank[0][0:HID0, 0:2], ACT.Relu, bias=c("b1", HID0),
                                   scale=1.0 / HW).then_inc(hid0_relu, 1)
                if k == 5:
                    act.wait_ge(z0_done, i + 1)
                    act.activation(z0[:, :], bank[1][:, 0:2], ACT.Exp, bias=neg_b2[:, :], scale=-1.0).then_inc(z0_exp, 1)
                if k == 6:
                    act.wait_ge(red_done, i + 1)
                    act.activation(red[:, 1:H + 1, 1:W + 1], bank[0][:, 0:HW].rearrange("p (h w) -> p h w", w=W),
                                   ACT.Identity, bias=c("reduce_b")).then_inc(red_copied, 1)
                if k == 8:
                    act.wait_ge(dw_tap, TAPS * i + TAPS)
                    act.activation(xr[:, :], dwa[:, :, :].rearrange("p h w -> p (h w)"), ACT.Relu, bias=bn_shift[:, :],
                                   scale=bn_scale[:, :], accum_out=sum_xr[:, :]).then_inc(xr_done, 1)
                    act.wait_ge(xr_done, i + 1)
                    act.activation(sq_junk[:, :], xr[:, :], ACT.Square, accum_out=n2[:, :]).then_inc(n2_done, 1)
                if k == 9:
                    act.wait_ge(hid1_done, i + 1)
                    act.activation(hid1[:, :], bank[1][0:2 * HID1, 0:1], ACT.Relu, bias=c("gb1", 2 * HID1),
                                   scale=1.0 / HW).then_inc(hid1_relu, 1)
                if k == 10:
                    act.wait_ge(z1_done, i + 1)
                    act.activation(z1[:, :], bank[0][:, 0:1], ACT.Exp, bias=neg_gb2[:, :], scale=-1.0).then_inc(z1_exp, 1)
                if k == 11:
                    act.wait_ge(dft_done, i + 1)
                    act.activation(ab[:, :, :], bank[0][:, 0:2 * P], ACT.Copy).then_inc(ab_copied, 1)
                if k == 12:
                    act.wait_ge(even_done, i + 1)
                    act.activation(even[:, :], bank[0][:, 0:HW], ACT.Copy).then_inc(even_copied, 1)
                    act.wait_ge(nmax1_done, i + 1)
                    act.activation(att1[:, :], logit1[:, :], ACT.Exp, bias=nmax1[:, :],
                                   accum_out=att1_sum[:, :]).then_inc(att1_exp, 1)
                if k == 13:
                    act.wait_ge(filt_done, i + 1)
                    act.wait_ge(z1_chain, 3 * i + 3)
                    act.activation(filt[:, :], bank[1][:, 0:HW], ACT.Identity, scale=fscale[:, :]).then_inc(filt_scaled, 1)

            def o2_copy(j, m):
                act.wait_ge(pv_done, 2 * HEADS * j + HEADS * (m + 1))
                act.activation(o2[:, :, :].rearrange("p q x -> p (q x)"), bank[O_BANK][:, :], ACT.Copy).then_inc(o2_copied, 1)

            def h_copy(j, m):
                act.wait_ge(ht_done, 2 * j + m + 1)
                act.activation(h_c[:, m, :], bank[H_BANK][:, 0:HW], ACT.Copy).then_inc(ht_copied, 1)

            def qk_high_parts(i, what):
                for q in range(QUADS):
                    if what == "q":
                        act.wait_ge(qk_done, 4 * i + q + 1)
                        act.activation(q_hm[:, q, :], bank[FRONT[q]][:, :], ACT.Identity, bias=bq_lo[:, q:q + 1],
                                       scale=c("lo_rows")).then_inc(qk_high, 1)
                    else:
                        act.wait_ge(qk_done, 4 * i + QUADS + q + 1)
                        act.activation(k_hi[:, q, :], bank[ST_BANK[q]][:, :], ACT.Identity,
                                       bias=c("bk")[:, q:q + 1]).then_inc(qk_high, 1)

            def slots(j, i=None, cj=None):
                for s in range(SLOTS):
                    n = s - HEADS
                    if n in (0, HEADS):
                        act.wait_ge(maxt_done, 2 * j + n // HEADS + 1)
                        act.activation(nmax2_t[:, :, :], bank[ST_BANK[0]][:, :], ACT.Copy).then_inc(maxt_copied, 1)
                    if n >= 0:
                        act.wait_ge(st_done, 2 * HEADS * j + n + 1)
                        if n >= 3:
                            act.wait_ge(pv_done, 2 * HEADS * j + n - 2)
                        act.activation(prob[:, n % 3, :, :], bank[ST_BANK[n % 2]][:, :], ACT.Exp,
                                       scale=L2_SCALE).then_inc(st_exp, 1)
                    if n == HEADS:
                        o2_copy(j, 0)
                    if n == HEADS + 2:
                        h_copy(j, 0)
                    if s in CONV_OUT and cj is not None:
                        conv_copy(cj, CONV_OUT[s])
                    if s in STAGE and i is not None:
                        stage(STAGE[s], i)
                o2_copy(j, 1)
                if i is not None:
                    qk_high_parts(i, "q")
                h_copy(j, 1)
                if i is not None:
                    qk_high_parts(i, "k")

            act.wait_ge(vec_set, 5)
            act.wait_ge(cst_loaded, 16)
            act.wait_ge(pool_set, 6)
            for k in range(STAGES):
                stage(k, 0)
            qk_high_parts(0, "q")
            qk_high_parts(0, "k")
            slots(0, 1)
            with act.Fori(2, PAIRS) as i:
                slots(i - 1, i, i - 2)
            slots(PAIRS - 1, None, PAIRS - 2)
            for w in range(3):
                conv_copy(PAIRS - 1, w)
            for b in range(BATCHES + 1):
                if b < BATCHES:
                    act.wait_ge(nmax3_done, b + 1)
                    if b >= 2:
                        act.wait_ge(att3_scaled, b - 1)
                    for g in range(BATCH):
                        act.activation(att3[b % 2][:, g * P:(g + 1) * P], logit3[b % 2][:, g * P:(g + 1) * P], ACT.Exp,
                                       bias=nmax3[:, b % 2, g:g + 1],
                                       accum_out=att3_sum[:, b % 2, g:g + 1]).then_inc(att3_exp, 1)
                    act.wait_ge(v3t_done, b + 1)
                    if b >= 2:
                        act.wait_ge(virt_done, b - 1)
                    act.activation(v3_t[:, b % 2, :, :], bank[2 + b % 2][:, :], ACT.Copy).then_inc(v3t_copied, 1)
                if b >= 1:
                    act.wait_ge(att3t_done, b)
                    act.activation(att3_t[(b - 1) % 2], bank[4 + (b - 1) % 2][:, :], ACT.Copy).then_inc(att3t_copied, 1)
            act.wait_ge(ln_ready, 1)
            with act.Fori(0, N) as n:
                act.activation(act3[:, bass.ds(n * HW, HW)].rearrange("p (t x) -> p t x", x=GPX),
                               tiled(virt)[:, bass.ds(n, 1), :, :], ACT.Relu, bias=lb[:, bass.ds(n, 1)],
                               scale=la[:, bass.ds(n, 1)]).then_inc(act3_done, 1)

        @block.vector
        def _(dve):
            dve.memset(ones_r[:, :].bitcast(F32), 1.0).then_inc(vec_set, 1)
            dve.wait_ge(cst_loaded, 16)
            dve.tensor_scalar(bn_tmp[:, 0:1], c("bn_var"), 1e-5, None, ALU.add).then_inc(vec_pre, 1)
            dve.tensor_scalar(neg_b2[:, :], c("b2"), -1.0, None, ALU.mult).then_inc(vec_set, 1)
            dve.tensor_scalar(neg_gb2[:, :], c("gb2"), -1.0, None, ALU.mult).then_inc(vec_set, 1)
            dve.tensor_scalar(bq_lo[:, :], c("bq"), c("lo_rows"), None, ALU.mult).then_inc(vec_set, 1)
            dve.tensor_tensor(bn_shift[:, :], c("dw_b"), c("bn_mean"), ALU.subtract).then_inc(vec_pre, 1)
            dve.wait_ge(bn_pow, 1)
            dve.tensor_tensor(bn_scale[:, :], bn_tmp[:, 1:2], c("bn_gamma"), ALU.mult).then_inc(vec_pre, 1)
            dve.wait_ge(vec_pre, 3)
            dve.scalar_tensor_tensor(bn_shift[:, :], bn_shift[:, :], bn_scale[:, :], c("bn_beta"),
                                     ALU.mult, ALU.add).then_inc(vec_set, 1)
            dve.wait_ge(bias_mm, 1)
            dve.tensor_tensor(proj_bias[:, :], bank[CONV][:, 0:1], c("bproj"), ALU.add).then_inc(vec_set, 1)
            dve.wait_ge(vec_set, 6)
            dve.wait_ge(pool_set, 6)

            def stage(k, i):
                if k == 0:
                    dve.wait_ge(xt_done, i + 1)
                    dve.tensor_copy(x_t[:, :, :, :].rearrange("p m k c -> p (m k c)"), bank[0][:, :]).then_inc(xt_copied, 1)
                    dve.wait_ge(x_loaded, 16 * i + 16)
                    dve.tensor_reduce(sum_x[:, :], x_in[:, :, :], X, ALU.add).then_inc(sum_x_done, 1)
                if k == 1:
                    dve.wait_ge(energy_done, i + 1)
                    dve.tensor_reduce(e_min[:, :], bank[1][:, 0:2 * C].rearrange("p (m c) -> p m c", m=2), X,
                                      ALU.min).then_inc(e_min_done, 1)
                    dve.wait_ge(att0_exp, 2 * i + 2)
                    dve.reciprocal(att0_inv[:, :], att0_sum[:, :]).then_inc(att0_inv_done, 1)
                if k == 5:
                    dve.wait_ge(z0_exp, i + 1)
                    dve.tensor_scalar(z0p[:, :], z0[:, :], 1.0, None, ALU.add).then_inc(z0_chain, 1)
                    dve.wait_ge(z0_chain, 2 * i + 1)
                    dve.reciprocal(se[:, :], z0p[:, :]).then_inc(z0_chain, 1)
                    dve.wait_ge(z0_chain, 2 * i + 2)
                    dve.wait_ge(diff0_done, i + 1)
                    for m in range(2):
                        dve.scalar_tensor_tensor(x1[:, m, :], diff0[:, m, :], se[:, m:m + 1], o0[:, m, :],
                                                 ALU.mult, ALU.add).then_inc(x1_done, 1)
                if k in (6, 7, 8):
                    dve.wait_ge(red_copied, i + 1)
                    for t in range(3 * (k - 6), 3 * (k - 5)):
                        tap = red[:, t // 3:t // 3 + H, t % 3:t % 3 + W]
                        wt = c("dw")[:, t:t + 1]
                        if t == 0:
                            dve.tensor_scalar(dwa[:, :, :], tap, wt, None, ALU.mult).then_inc(dw_tap, 1)
                        else:
                            dve.wait_ge(dw_tap, TAPS * i + t)
                            dve.scalar_tensor_tensor(dwa[:, :, :], tap, wt, dwa[:, :, :], ALU.mult,
                                                     ALU.add).then_inc(dw_tap, 1)
                if k == 8:
                    dve.wait_ge(n2_done, i + 1)
                    dve.tensor_scalar(n2m[:, :], n2[:, :], 1e-24, None, ALU.max).then_inc(n2m_done, 1)
                if k == 9:
                    dve.wait_ge(rn_done, i + 1)
                    dve.tensor_scalar(xh[:, :], xr[:, :], rn[:, :], None, ALU.mult).then_inc(xh_done, 1)
                    dve.wait_ge(n2m_done, i + 1)
                    dve.tensor_tensor(nrm[:, :], n2m[:, :], rn[:, :], ALU.mult).then_inc(xh_done, 1)
                if k == 10:
                    dve.wait_ge(xht_done, i + 1)
                    dve.tensor_copy(xh_t[:, :, :].rearrange("p k c -> p (k c)"), bank[1][:, 0:HW]).then_inc(xht_copied, 1)
                    dve.wait_ge(z1_exp, i + 1)
                    dve.tensor_scalar(z1p[:, :], z1[:, :], 1.0, None, ALU.add).then_inc(z1_chain, 1)
                    dve.wait_ge(z1_chain, 3 * i + 1)
                    dve.reciprocal(gate1[:, :], z1p[:, :]).then_inc(z1_chain, 1)
                    dve.wait_ge(z1_chain, 3 * i + 2)
                    dve.tensor_tensor(fscale[:, :], gate1[:, :], n2m[:, :], ALU.mult).then_inc(z1_chain, 1)
                if k == 12:
                    dve.wait_ge(dot1_done, i + 1)
                    dve.scalar_tensor_tensor(logit1[:, :], bank[1][:, 0:P], c("temp"), c("mask1"), ALU.mult,
                                             ALU.add).then_inc(logit1_done, 1)
                    dve.wait_ge(logit1_done, i + 1)
                    dve.tensor_reduce(nmax1[:, :], logit1[:, :], X, ALU.max, negate=True).then_inc(nmax1_done, 1)
                    dve.wait_ge(att1_exp, i + 1)
                    dve.reciprocal(att1_inv[:, :], att1_sum[:, :]).then_inc(att1_chain, 1)
                    dve.wait_ge(att1_chain, 2 * i + 1)
                    dve.tensor_scalar(att1_n[:, :], att1[:, :], att1_inv[:, :], None, ALU.mult).then_inc(att1_chain, 1)
                if k == 14:
                    dve.wait_ge(patt_done, i + 1)
                    dve.wait_ge(xh_done, 2 * i + 2)
                    dve.tensor_scalar(post_att[:, :], bank[0][:, 0:C], nrm[:, :], None, ALU.mult).then_inc(patt_copied, 1)
                if k == 15:
                    dve.wait_ge(y1_done, i + 1)
                    dve.wait_ge(x1_done, 2 * i + 2)
                    after(dve, x2_res_done, i)
                    for m in range(2):
                        dve.scalar_tensor_tensor(x2[:, m, :], bank[m][:, 0:HW], c("post_b"), x1[:, m, :],
                                                 ALU.add, ALU.add).then_inc(x2_done, 1)
                    for m in range(2):
                        dve.wait_ge(x2_done, 2 * i + m + 1)
                        dve.bn_stats(stats[:, m, :], x2[:, m, :]).then_inc(gn_chain, 1)
                    dve.wait_ge(gn_chain, 7 * i + 2)
                    dve.tensor_tensor(msq[:, :, :], halves(stats)[:, :, :, 1], halves(stats)[:, :, :, 1],
                                      ALU.mult).then_inc(gn_chain, 1)
                    dve.wait_ge(gn_chain, 7 * i + 3)
                    dve.scalar_tensor_tensor(halves(stats)[:, :, :, 2], halves(stats)[:, :, :, 2], 2.0 / HW,
                                             msq[:, :, :], ALU.mult, ALU.add).then_inc(gn_chain, 1)
                if k == 16:
                    dve.wait_ge(gsum_done, i + 1)
                    dve.tensor_copy(gmv[:, :, :].rearrange("p m k -> p (m k)"), bank[0][:, 0:4]).then_inc(gn_chain, 1)
                    dve.wait_ge(gn_chain, 7 * i + 5)
                    dve.tensor_tensor(gm2[:, :], gmv[:, :, 0], gmv[:, :, 0], ALU.mult).then_inc(gn_chain, 1)
                    dve.wait_ge(gn_chain, 7 * i + 6)
                    dve.tensor_tensor(gm2[:, :], gmv[:, :, 1], gm2[:, :], ALU.subtract).then_inc(gn_chain, 1)
                    dve.wait_ge(gn_chain, 7 * i + 7)
                    dve.tensor_scalar(gvar[:, :], gm2[:, :], 1e-5, None, ALU.add).then_inc(gvar_done, 1)
                    dve.wait_ge(grstd_done, i + 1)
                    dve.tensor_scalar(ga[:, :], grstd[:, :], c("gn_gamma"), None, ALU.mult).then_inc(xn_done, 1)
                    dve.wait_ge(xn_done, 5 * i + 1)
                    dve.tensor_tensor(gma[:, :], gmv[:, :, 0], ga[:, :], ALU.mult).then_inc(xn_done, 1)
                    dve.wait_ge(xn_done, 5 * i + 2)
                    dve.tensor_scalar(gb[:, :], gma[:, :], -1.0, c("gn_beta"), ALU.mult, ALU.add).then_inc(xn_done, 1)
                    dve.wait_ge(xn_done, 5 * i + 3)
                    for m in range(2):
                        dve.tensor_scalar(xn[:, m, :], x2[:, m, :], ga[:, m:m + 1], gb[:, m:m + 1], ALU.mult,
                                          ALU.add).then_inc(xn_done, 1)

            def qkv_parts(i):
                for q in range(QUADS):
                    dve.wait_ge(qk_high, 4 * i + q + 1)
                    dve.scalar_tensor_tensor(q_hl[:, q, :], bank[FRONT[q]][:, :], c("bq")[:, q:q + 1],
                                             q_hm[:, q, :].bitcast(F32), ALU.add, ALU.subtract).then_inc(qk_low, 1)
                for q in range(QUADS):
                    dve.wait_ge(qk_high, 4 * i + QUADS + q + 1)
                    dve.scalar_tensor_tensor(k_lo[:, q, :], bank[ST_BANK[q]][:, :], c("bk")[:, q:q + 1],
                                             k_hi[:, q, :].bitcast(F32), ALU.add, ALU.subtract).then_inc(qk_low, 1)
                dve.wait_ge(v_done, i + 1)
                for m in range(2):
                    dve.tensor_copy(v_t[:, m, :, :, 0:DH].rearrange("p k h d -> p (k h) d"),
                                    bank[0][:, m * HW:(m + 1) * HW].rearrange("p (n d) -> p n d", d=DH)
                                    ).then_inc(v_copied, 1)

            def row_max(j, n):
                m, h = n // HEADS, n % HEADS
                dve.wait_ge(s_done, 2 * HEADS * j + n + 1)
                col = SLOT * (h % 4)
                dve.tensor_reduce(nmax2[:, m, :, h // 4, col:col + 1],
                                  bank[S_BANK][:, :].rearrange("p (k s) -> p k s", k=CH), X, ALU.max,
                                  negate=True).then_inc(s_max, 1)

            def normalise(j, m):
                out_h = bank[S_BANK][:, :].rearrange("p (n w) -> p n w", w=SLOT)
                dve.wait_ge(ot_done, 2 * j + m + 1)
                dve.reciprocal(den2[:, :, :].rearrange("p k h -> p (k h)"), out_h[:, :, DH]).then_inc(den_done, 1)
                dve.wait_ge(den_done, 2 * j + m + 1)
                dve.tensor_tensor(h_t[:, :, :].rearrange("p k (h d) -> p (k h) d", d=DH), out_h[:, :, 0:DH],
                                  den2[:, :, :].rearrange("p k h -> p (k h)").unsqueeze(2)
                                  .to_broadcast([P, CH * HEADS, DH]), ALU.mult).then_inc(h_scaled, 1)

            def add_x2(j, m):
                dve.wait_ge(proj_done, 2 * j + m + 1)
                dve.wait_ge(x2_res_done, j + 1)
                after(dve, x3_kept, j)
                dve.tensor_tensor(x3_pair[:, m, :], bank[H_BANK][:, HW:2 * HW], x2_res[:, m, :],
                                  ALU.add).then_inc(x3_done, 1)

            def high_part(j):
                after(dve, conv_done, 3 * j)
                for m in range(2):
                    dve.wait_ge(x3_done, 2 * j + m + 1)
                    dve.tensor_copy(pad_hi[:, 0, m, 1:H + 1, 1:W + 1],
                                    x3_pair[:, m, :].rearrange("p (h w) -> p h w", w=W)).then_inc(pad_hi_done, 1)

            def slots(j, i=None):
                for s in range(SLOTS):
                    if s < 2 * HEADS:
                        row_max(j, s)
                    if s == 2 * HEADS + 1:
                        normalise(j, 0)
                    if s == 2 * HEADS + 3:
                        add_x2(j, 0)
                    if s in STAGE and i is not None:
                        stage(STAGE[s], i)
                normalise(j, 1)
                if i is not None:
                    qkv_parts(i)
                add_x2(j, 1)
                high_part(j)

            for k in range(STAGES):
                stage(k, 0)
            qkv_parts(0)
            slots(0, 1)
            with dve.Fori(2, PAIRS) as i:
                slots(i - 1, i)
            slots(PAIRS - 1)
            mask = c("mask3").unsqueeze(1).to_broadcast([P, BATCH, P])
            for b in range(BATCHES + 2):
                if b < BATCHES:
                    dve.wait_ge(dot3_done, b + 1)
                    if b >= 2:
                        dve.wait_ge(att3_exp, BATCH * (b - 1))
                    logits = logit3[b % 2].rearrange("p (g x) -> p g x", g=BATCH)
                    dve.scalar_tensor_tensor(logits, bank[b % 2][:, :].rearrange("p (g x) -> p g x", g=BATCH),
                                             L3_SCALE, mask, ALU.mult, ALU.add).then_inc(logit3_done, 1)
                    dve.wait_ge(logit3_done, b + 1)
                    dve.tensor_reduce(nmax3[:, b % 2, :], logits, X, ALU.max, negate=True).then_inc(nmax3_done, 1)
                a = b - 1
                if 0 <= a < BATCHES:
                    dve.wait_ge(att3_exp, BATCH * (a + 1))
                    after(dve, att3_scaled, a)
                    dve.reciprocal(att3_inv[:, :], att3_sum[:, a % 2, :]).then_inc(att3_inv_done, 1)
                    dve.wait_ge(att3_inv_done, a + 1)
                    if a >= 2:
                        dve.wait_ge(att3t_done, a - 1)
                    dve.tensor_tensor(att3_n[a % 2].rearrange("p (g x) -> p g x", g=BATCH),
                                      att3[a % 2].rearrange("p (g x) -> p g x", g=BATCH),
                                      att3_inv[:, :].unsqueeze(2).to_broadcast([P, BATCH, P]),
                                      ALU.mult).then_inc(att3_scaled, 1)
                a = b - 2
                if a >= 0:
                    dve.wait_ge(virt_done, a + 1)
                    dve.tensor_copy(virt[:, a * BATCH * P:(a + 1) * BATCH * P], bank[6 + a % 2][:, :]).then_inc(virt_copied, 1)
            dve.wait_ge(virt_copied, BATCHES)
            for n in range(N):
                dve.bn_stats(stats3[:, n, :], tiled(virt)[:, n, :, :]).then_inc(ln_chain, 1)
            k = N
            dve.wait_ge(ln_chain, k)
            dve.tensor_tensor(msq3[:, :, :], halves(stats3)[:, :, :, 1], halves(stats3)[:, :, :, 1],
                              ALU.mult).then_inc(ln_chain, 1)
            dve.wait_ge(ln_chain, k + 1)
            dve.scalar_tensor_tensor(halves(stats3)[:, :, :, 2], halves(stats3)[:, :, :, 2], 2.0 / HW,
                                     msq3[:, :, :], ALU.mult, ALU.add).then_inc(ln_chain, 1)
            dve.wait_ge(tot3_done, 1)
            dve.tensor_copy(tmv3[:, :, :].rearrange("p n k -> p (n k)"), bank[0][:, 0:2 * N]).then_inc(ln_chain, 1)
            dve.wait_ge(ln_chain, k + 3)
            dve.tensor_tensor(tm3[:, :], tmv3[:, :, 0], tmv3[:, :, 0], ALU.mult).then_inc(ln_chain, 1)
            dve.wait_ge(ln_chain, k + 4)
            dve.tensor_tensor(tm3[:, :], tmv3[:, :, 1], tm3[:, :], ALU.subtract).then_inc(ln_chain, 1)
            dve.wait_ge(ln_chain, k + 5)
            dve.tensor_scalar(var3[:, :], tm3[:, :], 1e-5, None, ALU.add).then_inc(var3_done, 1)
            dve.wait_ge(rstd3_done, 1)
            dve.tensor_scalar(la[:, :], rstd3[:, :], c("ln_gamma"), None, ALU.mult).then_inc(ln_chain, 1)
            dve.wait_ge(ln_chain, k + 6)
            dve.tensor_tensor(lma[:, :], tmv3[:, :, 0], la[:, :], ALU.mult).then_inc(ln_chain, 1)
            dve.wait_ge(ln_chain, k + 7)
            dve.tensor_scalar(lb[:, :], lma[:, :], -1.0, c("ln_beta"), ALU.mult, ALU.add).then_inc(ln_ready, 1)

            def split_act(i, s):
                dve.wait_ge(act3_done, 4 * i + 2 * s + 2)
                after(dve, last_conv, 2 * i + s - 1)
                r = act3[:, bass.ds((2 * i + s) * PX, PX)].rearrange("p (m h w) -> p m h w", m=2, w=W)
                for m in range(2):
                    dve.tensor_copy(pad_hi[:, s, m, 1:H + 1, 1:W + 1], r[:, m, :, :]).then_inc(last_hi, 1)
                dve.wait_ge(last_hi, 4 * i + 2 * s + 2)
                for m in range(2):
                    ins = dve.tensor_tensor(pad_lo[:, s, m, 1:H + 1, 1:W + 1], r[:, m, :, :],
                                            pad_hi[:, s, m, 1:H + 1, 1:W + 1].bitcast(F32), ALU.subtract)
                ins.then_inc(last_lo, 1)

            def add_residual(i, s):
                dve.wait_ge(last_conv, 2 * i + s + 1)
                dve.tensor_tensor(y[:, bass.ds((2 * i + s) * PX, PX)], bank[s][:, :],
                                  x3[:, bass.ds((2 * i + s) * PX, PX)], ALU.add).then_inc(y_done, 1)

            def last_round(i):
                split_act(i, 0)
                if not (isinstance(i, int) and i == 0):
                    add_residual(i - 1, 1)
                split_act(i, 1)
                add_residual(i, 0)

            dve.wait_ge(x3_kept, PAIRS)
            dve.wait_ge(conv_done, 3 * PAIRS)
            last_round(0)
            with dve.Fori(1, PAIRS // 2) as i:
                last_round(i)
            add_residual(PAIRS // 2 - 1, 1)

        @block.tensor
        def _(pe):
            mm, tr = pe.matmul, pe.transpose
            ident = c("ident")

            def conv_taps(w, slot, dst, t0, t1, s=None):
                last = None
                for t in range(t0, t1):
                    r = [p[:, slot, :, t // 3:t // 3 + H, t % 3:t % 3 + W] for p in (pad_hi, pad_lo)]
                    mm(dst, w_hi[:, w, t, :], r[0], start=(t == 0), stop=False)
                    mm(dst, w_hi[:, w, t, :], r[1], start=False, stop=False)
                    last = mm(dst, w_lo[:, w, t, :], r[0], start=False, stop=(t == TAPS - 1))
                if s is not None and t1 == TAPS:
                    last.then_inc(s, 1)

            def stage(k, i):
                if k == 0:
                    pe.wait_ge(x_loaded, 16 * i + 16)
                    after(pe, v_copied, 2 * i)
                    for m in range(2):
                        for q in range(CH):
                            o = (m * CH + q) * C
                            ins = tr(bank[0][:, o:o + C], x_in[:, m, q * P:(q + 1) * P], ident)
                    ins.then_inc(xt_done, 1)
                if k == 1:
                    pe.wait_ge(xt_copied, i + 1)
                    after(pe, qk_low, 4 * i)
                    for m in range(2):
                        for q in range(CH):
                            ins = mm(bank[1][:, m * C:(m + 1) * C], x_t[:, m, q, :], x_t[:, m, q, :],
                                     start=(q == 0), stop=(q == CH - 1))
                    ins.then_inc(energy_done, 1)
                if k == 2:
                    pe.wait_ge(att0_exp, 2 * i + 2)
                    for m in range(2):
                        ins = tr(bank[0][:, m * C:(m + 1) * C], att0[:, m, :], ident)
                    ins.then_inc(att0t_done, 1)
                if k == 3:
                    pe.wait_ge(att0t_copied, i + 1)
                    for m in range(2):
                        ins = mm(bank[1][:, m * HW:(m + 1) * HW], att0_t[:, m, :], x_in[:, m, :], start=True, stop=True)
                    ins.then_inc(o0_done, 1)
                if k == 4:
                    pe.wait_ge(sum_x_done, i + 1)
                    pe.wait_ge(o0_scaled, 2 * i + 2)
                    mm(bank[0][0:HID0, 0:2], c("w1x"), sum_x[:, :], start=True, stop=False)
                    mm(bank[0][0:HID0, 0:2], c("w1o"), sum_o0[:, :], start=False, stop=True).then_inc(hid0_done, 1)
                if k == 5:
                    pe.wait_ge(hid0_relu, i + 1)
                    mm(bank[1][:, 0:2], c("w2", HID0), hid0[:, :], start=True, stop=True).then_inc(z0_done, 1)
                if k == 6:
                    pe.wait_ge(x1_done, 2 * i + 2)
                    for m in range(2):
                        ins = mm(bank[0][m * MID:(m + 1) * MID, 0:HW], c("reduce_w"), x1[:, m, :], start=True, stop=True)
                    ins.then_inc(red_done, 1)
                if k == 9:
                    pe.wait_ge(xr_done, i + 1)
                    mm(bank[1][0:2 * HID1, 0:1], c("gw1"), sum_xr[:, :], start=True, stop=True).then_inc(hid1_done, 1)
                if k == 10:
                    pe.wait_ge(hid1_relu, i + 1)
                    mm(bank[0][:, 0:1], c("gw2", 2 * HID1), hid1[:, :], start=True, stop=True).then_inc(z1_done, 1)
                    pe.wait_ge(xh_done, 2 * i + 1)
                    for q in range(CH):
                        ins = tr(bank[1][:, q * P:(q + 1) * P], xh[:, q * P:(q + 1) * P], ident)
                    ins.then_inc(xht_done, 1)
                if k == 11:
                    pe.wait_ge(xht_copied, i + 1)
                    pe.wait_ge(z1_exp, i + 1)
                    fwd = c("fwd").rearrange("p (k r f) -> p k r f", k=CH, r=2)
                    for r in range(2):
                        for q in range(CH):
                            ins = mm(bank[0][:, r * P:(r + 1) * P], fwd[:, q, r, :], xh_t[:, q, :],
                                     start=(q == 0), stop=(q == CH - 1))
                    ins.then_inc(dft_done, 1)
                if k == 12:
                    pe.wait_ge(ab_copied, i + 1)
                    pe.wait_ge(b_signed_done, i + 1)
                    mm(bank[1][:, 0:P], ab[:, 0, :], ab[:, 0, :], start=True, stop=False)
                    mm(bank[1][:, 0:P], ab[:, 1, :], b_signed[:, :], start=False, stop=True).then_inc(dot1_done, 1)
                    mm(bank[0][:, 0:HW], ab[:, 0, :], c("even_a"), start=True, stop=False)
                    mm(bank[0][:, 0:HW], ab[:, 1, :], c("even_b"), start=False, stop=True).then_inc(even_done, 1)
                if k == 13:
                    pe.wait_ge(squares_done, 2 * i + 2)
                    pe.wait_ge(logit1_done, i + 1)
                    mm(bank[1][:, 0:HW], ab_sq[:, 0, :], c("inv_aa"), start=True, stop=False)
                    mm(bank[1][:, 0:HW], ab_sq[:, 1, :], c("inv_bb"), start=False, stop=False)
                    mm(bank[1][:, 0:HW], a_times_b[:, :], c("inv_ab"), start=False, stop=True).then_inc(filt_done, 1)
                if k == 14:
                    pe.wait_ge(att1_chain, 2 * i + 2)
                    pe.wait_ge(even_copied, i + 1)
                    mm(bank[0][:, 0:C], att1_n[:, :], c("post1"), start=True, stop=True).then_inc(patt_done, 1)
                if k == 15:
                    pe.wait_ge(patt_copied, i + 1)
                    pe.wait_ge(filt_scaled, i + 1)
                    for m in range(2):
                        r0 = m * MID
                        mm(bank[m][:, 0:HW], post_att[r0:r0 + MID, :], even[r0:r0 + MID, :], start=True, stop=False)
                        ins = mm(bank[m][:, 0:HW], c("post2", MID, r0), filt[r0:r0 + MID, :], start=False, stop=True)
                    ins.then_inc(y1_done, 1)
                if k == 16:
                    pe.wait_ge(gn_chain, 7 * i + 4)
                    mm(bank[0][:, 0:4], c("group"), halves(stats)[:, :, 0, 1:3], start=True, stop=False)
                    mm(bank[0][:, 0:4], c("group"), halves(stats)[:, :, 1, 1:3], start=False, stop=True).then_inc(gsum_done, 1)

            def project(i, what):
                xn_all = xn[:, :, :].rearrange("p m x -> p (m x)")
                if what == "q":
                    pe.wait_ge(xn_done, 5 * i + 5)
                if what in "qk":
                    for q in range(QUADS):
                        dst = bank[(FRONT if what == "q" else ST_BANK)[q]][:, :]
                        mm(dst, c("w" + what)[:, q * P:(q + 1) * P], xn_all, start=True, stop=True).then_inc(qk_done, 1)
                if what == "v":
                    pe.wait_ge(qk_low, 4 * i + 1)
                    for m in range(2):
                        for k in range(CH):
                            o = (m * CH + k) * C
                            ins = mm(bank[0][:, o:o + C], xn[:, m, k * P:(k + 1) * P], c("wv"), start=True, stop=True)
                    ins.then_inc(v_done, 1)

            def scores(j, n):
                m, h = n // HEADS, n % HEADS
                r = slice(SLOT * (h % 4), SLOT * (h % 4) + SLOT)
                if n == 0:
                    pe.wait_ge(qk_low, 4 * j + 4)
                else:
                    pe.wait_ge(s_max, 2 * HEADS * j + n)
                for k in range(CH):
                    ins = mm(bank[S_BANK][:, k * HW:(k + 1) * HW],
                             q_hl[r, h // 4, m * HW + k * P:m * HW + (k + 1) * P],
                             k_hi[r, h // 4, m * HW:(m + 1) * HW], start=True, stop=True)
                ins.then_inc(s_done, 1)

            def scores_t(j, n):
                m, h = n // HEADS, n % HEADS
                r = slice(SLOT * (h % 4), SLOT * (h % 4) + SLOT)
                if n % HEADS == 0:
                    pe.wait_ge(maxt_copied, 2 * j + m + 1)
                if n >= 2:
                    pe.wait_ge(st_exp, 2 * HEADS * j + n - 1)
                q_m = q_hl[r, h // 4, m * HW:(m + 1) * HW]
                for k in range(CH):
                    dst = bank[ST_BANK[n % 2]][:, k * HW:(k + 1) * HW]
                    key = slice(m * HW + k * P, m * HW + (k + 1) * P)
                    mm(dst, k_hi[r, h // 4, key], q_m, start=True, stop=False)
                    mm(dst, k_lo[r, h // 4, key], q_m, start=False, stop=False)
                    ins = mm(dst, ones_r[r, :], nmax2_t[r, h // 4, :], start=False, stop=True)
                ins.then_inc(st_done, 1)

            def maxima_t(j, m):
                pe.wait_ge(s_max, 2 * HEADS * j + HEADS * (m + 1))
                if m:
                    pe.wait_ge(st_exp, 2 * HEADS * j + HEADS)
                for q in range(QUADS):
                    for k in range(CH):
                        o = q * HW + k * P
                        ins = tr(bank[ST_BANK[0]][:, o:o + P], nmax2[:, m, k, q, :], ident)
                ins.then_inc(maxt_done, 1)

            def values(j, n):
                m, h = n // HEADS, n % HEADS
                pe.wait_ge(st_exp, 2 * HEADS * j + n + 1)
                if h == 0:
                    after(pe, o2_copied, 2 * j + m)
                dst = bank[O_BANK][SLOT * (h % 4):SLOT * (h % 4) + SLOT, h // 4 * HW:(h // 4 + 1) * HW]
                for k in range(CH):
                    ins = mm(dst, v_t[:, m, k, h, :], prob[:, n % 3, k, :], start=(k == 0), stop=(k == CH - 1))
                ins.then_inc(pv_done, 1)

            def result_t(j, m):
                pe.wait_ge(o2_copied, 2 * j + m + 1)
                pe.wait_ge(s_max, 2 * HEADS * (j + 1))
                for k in range(CH):
                    for q in range(QUADS):
                        o = (k * QUADS + q) * P
                        ins = tr(bank[S_BANK][:, o:o + P], o2[:, q, k * P:(k + 1) * P], ident)
                ins.then_inc(ot_done, 1)

            def heads_t(j, m):
                pe.wait_ge(h_scaled, 2 * j + m + 1)
                after(pe, x3_done, 2 * j + m)
                for k in range(CH):
                    ins = tr(bank[H_BANK][:, k * P:(k + 1) * P], h_t[:, k, :], ident)
                ins.then_inc(ht_done, 1)

            def project_out(j, m):
                pe.wait_ge(ht_copied, 2 * j + m + 1)
                mm(bank[H_BANK][:, HW:2 * HW], c("wproj"), h_c[:, m, :], start=True, stop=True).then_inc(proj_done, 1)

            def convolve(j, t0, t1):
                for t in range(t0, t1):
                    if t == 0:
                        pe.wait_ge(pad_lo_done, 2 * j + 2)
                    elif t % TAPS == 0:
                        pe.wait_ge(conv_copied, 3 * j + t // TAPS)
                    conv_taps(t // TAPS, 0, bank[CONV][:, :], t % TAPS, t % TAPS + 1, conv_done)

            def slots(j, i=None, cj=None):
                for s in range(SLOTS):
                    n = s - HEADS
                    if n < 0:
                        scores(j, s)
                    elif n % HEADS == 0:
                        maxima_t(j, n // HEADS)
                    if cj is not None:
                        convolve(cj, sum(TAPS_IN[:s]), sum(TAPS_IN[:s + 1]))
                    if n >= 0:
                        scores_t(j, n)
                        if n < HEADS:
                            scores(j, HEADS + n)
                        if n:
                            values(j, n - 1)
                    if n == HEADS + 1:
                        result_t(j, 0)
                    if n == HEADS + 2:
                        heads_t(j, 0)
                    if n == HEADS + 3:
                        project_out(j, 0)
                    if s in STAGE and i is not None:
                        stage(STAGE[s], i)
                values(j, 2 * HEADS - 1)
                if cj is not None:
                    pe.wait_ge(conv_copied, 3 * cj + 3)
                if i is not None:
                    project(i, "q")
                result_t(j, 1)
                if i is not None:
                    project(i, "k")
                heads_t(j, 1)
                if i is not None:
                    project(i, "v")
                project_out(j, 1)

            pe.wait_ge(cst_loaded, 16)
            mm(bank[CONV][:, 0:1], c("wproj"), c("bv"), start=True, stop=True).then_inc(bias_mm, 1)
            pe.wait_ge(vec_set, 6)
            for k in range(STAGES):
                stage(k, 0)
            for what in "qkv":
                project(0, what)
            slots(0, 1)
            pe.wait_ge(w_split, 3)
            with pe.Fori(2, PAIRS) as i:
                slots(i - 1, i, i - 2)
            slots(PAIRS - 1, None, PAIRS - 2)
            convolve(PAIRS - 1, 0, 3 * TAPS)
            pe.wait_ge(conv_copied, 3 * PAIRS)
            pe.wait_ge(x3_done, 2 * PAIRS)
            q3, k3, v3 = qkv3

            def dots(b):
                if b >= 2:
                    pe.wait_ge(logit3_done, b - 1)
                for g in range(BATCH):
                    px = slice((b * BATCH + g) * P, (b * BATCH + g + 1) * P)
                    ins = mm(bank[b % 2][:, g * P:(g + 1) * P], q3[:, px], k3[:, px], start=True, stop=True)
                ins.then_inc(dot3_done, 1)
                if b >= 2:
                    pe.wait_ge(v3t_copied, b - 1)
                for g in range(BATCH):
                    px = slice((b * BATCH + g) * P, (b * BATCH + g + 1) * P)
                    ins = tr(bank[2 + b % 2][:, g * C:(g + 1) * C], v3[:, px], ident)
                ins.then_inc(v3t_done, 1)

            for b in range(BATCHES + 2):
                if b < BATCHES:
                    dots(b)
                a = b - 2
                if a >= 0:
                    pe.wait_ge(att3t_copied, a + 1)
                    pe.wait_ge(v3t_copied, a + 1)
                    if a >= 2:
                        pe.wait_ge(virt_copied, a - 1)
                    for g in range(BATCH):
                        ins = mm(bank[6 + a % 2][:, g * P:(g + 1) * P], v3_t[:, a % 2, g, :],
                                 att3_t[a % 2][:, g * P:(g + 1) * P], start=True, stop=True)
                    ins.then_inc(virt_done, 1)
                a = b - 1
                if 0 <= a < BATCHES:
                    pe.wait_ge(att3_scaled, a + 1)
                    if a >= 2:
                        pe.wait_ge(att3t_copied, a - 1)
                    for g in range(BATCH):
                        ins = tr(bank[4 + a % 2][:, g * P:(g + 1) * P], att3_n[a % 2][:, g * P:(g + 1) * P], ident)
                    ins.then_inc(att3t_done, 1)
            pe.wait_ge(ln_chain, N + 2)
            mm(bank[0][:, 0:2 * N], c("mean_all"), halves(stats3)[:, :, 0, 1:3], start=True, stop=False)
            mm(bank[0][:, 0:2 * N], c("mean_all"), halves(stats3)[:, :, 1, 1:3], start=False, stop=True).then_inc(tot3_done, 1)
            pe.wait_ge(ln_ready, 1)
            pe.wait_ge(w_split, 4)

            def last_convs(i):
                for s in range(2):
                    pe.wait_ge(last_lo, 2 * i + s + 1)
                    after(pe, y_done, 2 * i + s - 1)
                    conv_taps(3, s, bank[s][:, :], 0, TAPS, last_conv)

            last_convs(0)
            with pe.Fori(1, PAIRS // 2) as i:
                last_convs(i)


def constants():
    t = {"ident": np.eye(P, dtype=np.float32)}
    r = np.arange(P)
    t["mask1"] = np.where(r[:, None] // HID1 == r[None, :] // HID1, 0.0, FAR)
    t["mask3"] = np.where(r[:, None] % GPX == r[None, :] % GPX, 0.0, FAR)
    t["group"] = np.where(r[:, None] // GC == r[None, :] // GC, 0.5 / GC, 0.0)
    t["mean_all"] = np.full((P, P), 0.5 / P)
    half = [(0, 0), (0, W // 2), (H // 2, 0), (H // 2, W // 2)]
    pairs, seen = [], set(half)
    for u in range(H):
        for v in range(W):
            if (u, v) not in seen:
                pairs.append((u, v))
                seen |= {(u, v), (-u % H, -v % W)}
    h, w = np.divmod(np.arange(HW), W)
    angle = lambda f: 2 * np.pi * ((f[0] * h + f[1] * w) % H) / H
    root = float(np.sqrt(HW))
    a = [np.cos(angle(f)) / root for f in half[:2]] + [np.sqrt(2) * np.cos(angle(f)) / root for f in pairs]
    b = [np.cos(angle(f)) / root for f in half[2:]] + [np.sqrt(2) * np.sin(angle(f)) / root for f in pairs]
    a, b = np.array(a), np.array(b)
    t["fwd"] = np.stack([a.T.reshape(CH, P, P), b.T.reshape(CH, P, P)], 1).transpose(2, 0, 1, 3).reshape(P, -1)
    t["even_a"] = a
    t["even_b"] = np.where(r[:, None] < 2, b, 0.0)
    t["inv_aa"] = np.array([np.cos(angle(f)) / root for f in half[:2] + pairs])
    t["inv_bb"] = np.array([np.cos(angle(f)) / root for f in half[2:]] + [-np.cos(angle(f)) / root for f in pairs])
    t["inv_ab"] = np.array([0 * h for f in half[2:]] + [2 * np.sin(angle(f)) / root for f in pairs])
    t["sign_b"] = np.where(r < 2, 1.0, -1.0)[:, None]
    t["lo_rows"] = np.where(r % SLOT >= DH, 1.0, 0.0)[:, None]
    return {k: v.astype(np.float32) for k, v in t.items()}


_OUT = ((N, C, H, W), "float32")


def kernel(**inputs):
    import numpy as _np
    import concourse.bacc as _bacc
    from concourse import mybir as _mybir
    from concourse.bass_utils import run_bass_kernel_spmd as _run

    a = {k: _np.asarray(v) for k, v in inputs.items()}
    col = lambda v: v.reshape(-1, 1)
    twice = lambda v: _np.concatenate([v, v], 0)
    q_rows = _np.array([[3 * DH * (4 * q + s // SLOT) + s % DH for s in range(P)] for q in range(QUADS)])
    v_rows = _np.array([3 * DH * h + 2 * DH + d for h in range(HEADS) for d in range(DH)])
    wqkv, bqkv = a["L2_conv_w_qkv"], a["L2_conv_b_qkv"]
    gw1 = _np.zeros((P, 2 * HID1), _np.float32)
    gw2 = _np.zeros((2 * HID1, P), _np.float32)
    for m in range(2):
        gw1[m * MID:(m + 1) * MID, m * HID1:(m + 1) * HID1] = a["L1_conv_gate_w1"].T
        gw2[m * HID1:(m + 1) * HID1, m * MID:(m + 1) * MID] = a["L1_conv_gate_w2"].T
    t = constants()
    t["w1x"], t["w1o"] = a["L0_conv_w1"].T[:C], a["L0_conv_w1"].T[C:]
    t["w2"], t["b1"], t["b2"] = a["L0_conv_w2"].T, col(a["L0_conv_b1"]), col(a["L0_conv_b2"])
    t["reduce_w"] = a["L1_conv_reduce_w"].T
    t["reduce_b"] = twice(col(a["L1_conv_reduce_b"]))
    t["dw"] = twice(a["L1_conv_dw_w"].reshape(MID, TAPS))
    for k in ("dw_b", "bn_gamma", "bn_beta", "bn_mean", "bn_var"):
        t[k] = twice(col(a["L1_conv_" + k]))
    t["gw1"], t["gw2"] = gw1, gw2
    t["gb1"], t["gb2"] = twice(col(a["L1_conv_gate_b1"])), twice(col(a["L1_conv_gate_b2"]))
    t["temp"] = twice(_np.repeat(col(a["L1_conv_temperature"]), MID // 8, 0))
    post = a["L1_conv_post_w"].T
    t["post1"], t["post2"], t["post_b"] = twice(post[:MID]), twice(post[MID:]), col(a["L1_conv_post_b"])
    t["gn_gamma"], t["gn_beta"] = col(a["L2_conv_gamma"]), col(a["L2_conv_beta"])
    t["wq"] = _np.concatenate([wqkv[q_rows[q]].T for q in range(QUADS)], 1)
    t["wk"] = _np.concatenate([wqkv[q_rows[q] + DH].T for q in range(QUADS)], 1)
    t["bq"] = bqkv[q_rows].T
    t["bk"] = bqkv[q_rows + DH].T
    t["wv"], t["bv"] = wqkv[v_rows].T, col(bqkv[v_rows])
    t["wproj"], t["bproj"] = a["L2_conv_w_proj"].T, col(a["L2_conv_b_proj"])
    t["ln_gamma"], t["ln_beta"] = col(a["L3_conv_gamma"]), col(a["L3_conv_beta"])
    small = _np.zeros((P, SMALL_W), _np.float32)
    for k, (b, e) in AT.items():
        small[:t[k].shape[0], b:e] = t[k]
    convs = _np.concatenate([a["L3_conv_W" + k].transpose(1, 2, 3, 0).reshape(C, TAPS * C) for k in "qkvc"], 1)
    arrays = {"x": _np.ascontiguousarray(a["x"]), "small": small, "convs": _np.ascontiguousarray(convs)}

    nc = _bacc.Bacc("TRN2", target_bir_lowering=False, num_devices=1)
    ap = {k: nc.dram_tensor(k, v.shape, _mybir.dt.from_np(v.dtype), kind="ExternalInput").ap()
          for k, v in arrays.items()}
    out = nc.dram_tensor("out", _OUT[0], _mybir.dt.from_np(_np.dtype(_OUT[1])), kind="ExternalOutput").ap()
    program(nc, ap["x"], ap["small"], ap["convs"], out)
    r = _run(nc, [arrays], core_ids=[0])
    return r.results[0]["out"]
```

```python
from contextlib import ExitStack

import numpy as np

import concourse.bass as bass
from concourse import mybir


N, C, H, W = 16, 128, 16, 16
HW = H * W
PAIRS = N // 2
PX = 2 * HW
P = 128
CH = HW // P
HID0 = 2 * C // 16
MID = C // 2
HID1 = MID // 8
HEADS = 8
DH = C // HEADS
SLOT = 32
QUADS = HEADS * SLOT // P
TAPS = 9
PW = W + 2
MIXES = 4
KH = 3
KC = KH * C
WC = MIXES * KC
POS = (2, 0, 1, 3)
HT = W // 2
GC = C // 32
GPX = P // N
BATCH = 4
BATCHES = HW // GPX // BATCH
L2_SCALE = DH ** -0.5
L3_SCALE = float(1.0 / np.sqrt(np.float32(C)))
FAR = -1e30
STAGE_SLOTS = (2, 5, 6, 7, 8, 9, 10, 11, 12, 13, 14, 15, 16, 17, 18, 19, 21)
STAGE = {s: k for k, s in enumerate(STAGE_SLOTS)}
STAGES = len(STAGE_SLOTS)
SLOTS = 3 * HEADS
UNITS = 6
GROUPS = 6
UNITS_IN = (0, 0, 0, 0, 2, 2, 2, 2, 3, 1, 3, 3, 2, 2, 2, 0, 2, 1, 1, 0, 0, 2, 0, 0)
UNITS_LATE = (2, 2, 2)
DONE_IN = [next(s for s in range(SLOTS) if sum(UNITS_IN[:s + 1]) >= UNITS * (g + 1)) for g in range(GROUPS - 1)]
FIRST_OUT = {DONE_IN[2 * w]: w for w in range(3)}
SECOND_OUT = {DONE_IN[2 * w + 1]: w for w in range(2)}
K_LOW_SLOT, V_HIGH_SLOT, V_LOW_SLOT, WINDOW_SLOT, ONES_SLOT = 4, 3, 7, 2, 4
LN_GROUPS = (slice(0, 2), slice(2, N))
UNITS_V = (2, 2, 2, 2, 2, 2)
UNITS_END = (1, 2, 3, 3)
LAG = 2
OUT_SLOT = 2 * HEADS + LAG

F32 = mybir.dt.float32
F32R = mybir.dt.float32r
ALU = mybir.AluOpType
ACT = mybir.ActivationFunctionType
X = mybir.AxisListType.X
XY = mybir.AxisListType.XY

SMALL = [("ident", P), ("lo_rows", 1), ("hi_rows", 1), ("one_row", 1), ("sign_b", 1),
         ("w1x", HID0), ("w1o", HID0), ("w2", C), ("b1", 1), ("b2", 1),
         ("reduce_w", MID), ("reduce_b", 1), ("dw", TAPS), ("dw_b", 1), ("bn_gamma", 1), ("bn_beta", 1),
         ("bn_mean", 1), ("bn_var", 1), ("gb1", 1), ("gb2", 1), ("bq", QUADS), ("bv", 1), ("bproj", 1),
         ("wproj", C),
         ("gw1", 2 * HID1), ("gw2", P), ("fwd", CH * 2 * P), ("mask1", P), ("mask3", P), ("group", P),
         ("mean_all", P), ("inv_aa", HW), ("inv_bb", HW), ("inv_ab", HW), ("even_a", HW), ("even_b", HW),
         ("temp", 1), ("post1", C), ("post2", C), ("post_b", 1), ("combine", 2 * SLOT),
         ("gn_gamma", 1), ("gn_beta", 1), ("wq", QUADS * P), ("wk", QUADS * P),
         ("bk", QUADS), ("wv", C), ("ln_gamma", 1), ("ln_beta", 1)]
AT, _o = {}, 0
for _n, _w in SMALL:
    AT[_n] = (_o, _o + _w)
    _o += _w
SMALL_W = _o
FIRST_W = AT["gw1"][0]


def program(nc, x, small, convs, out):
    with ExitStack() as ctx:
        def sb(name, shape, dt=F32):
            return ctx.enter_context(nc.sbuf_tensor(name, shape, dt))

        def sem(name):
            return ctx.enter_context(nc.semaphore(name))

        cst = sb("cst", [P, SMALL_W])

        def c(name, rows=P, r0=0):
            a, b = AT[name]
            return cst[r0:r0 + rows, a:b]

        w_stage = sb("w_stage", [P, TAPS * C])
        w_hi = sb("w_hi", [P, 3, WC], F32R)
        w_lo = sb("w_lo", [P, 3, WC], F32R)
        neg_b2 = sb("neg_b2", [P, 1])
        neg_gb2 = sb("neg_gb2", [P, 1])
        bn_scale = sb("bn_scale", [P, 1])
        bn_shift = sb("bn_shift", [P, 1])
        bn_tmp = sb("bn_tmp", [P, 2])
        bq_lo = sb("bq_lo", [P, QUADS])
        proj_bias = sb("proj_bias", [P, 1])
        pow_half = sb("pow_half", [P, N])
        ones_r = sb("ones_r", [P, P], F32R)
        x_in = sb("x_in", [P, 2, HW])
        e_min = sb("e_min", [P, 2])
        att0_sum = sb("att0_sum", [P, 2])
        att0_inv = sb("att0_inv", [P, 2])
        o0 = sb("o0", [P, 2, HW])
        diff0 = sb("diff0", [P, 2, HW])
        sum_o0 = sb("sum_o0", [P, 2])
        sum_x = sb("sum_x", [P, 2])
        hid0 = sb("hid0", [HID0, 2])
        z0 = sb("z0", [P, 2])
        z0p = sb("z0p", [P, 2])
        se = sb("se", [P, 2])
        x1 = sb("x1", [P, 2, HW])
        red = sb("red", [P, H + 2, PW])
        xr = sb("xr", [P, HW])
        att0_t = xr[:, :].rearrange("p (m c) -> p m c", m=2)
        sum_xr = sb("sum_xr", [P, 1])
        n2 = sb("n2", [P, 1])
        n2m = sb("n2m", [P, 1])
        rn = sb("rn", [P, 1])
        nrm = sb("nrm", [P, 1])
        xh_ab = sb("xh_ab", [P, 2 * HW])
        xh = xh_ab[:, 0:HW]
        ab = xh_ab[:, HW:2 * HW].rearrange("p (r f) -> p r f", r=2)
        x_t = xh_ab[:, :].rearrange("p (m k c) -> p m k c", m=2, k=CH)
        xh_t = sb("xh_t", [P, CH, P])
        att0 = xh_t
        hid1 = sb("hid1", [2 * HID1, 1])
        z1 = sb("z1", [P, 1])
        z1p = sb("z1p", [P, 1])
        gate1 = sb("gate1", [P, 1])
        fscale = sb("fscale", [P, 1])
        b_signed = sb("b_signed", [P, P])
        ab_sq = sb("ab_sq", [P, 2, P])
        a_times_b = sb("a_times_b", [P, P])
        logit1 = sb("logit1", [P, P])
        nmax1 = sb("nmax1", [P, 1])
        att1 = sb("att1", [P, P])
        att1_sum = sb("att1_sum", [P, 1])
        att1_inv = sb("att1_inv", [P, 1])
        att1_n = sb("att1_n", [P, P])
        even = sb("even", [P, HW])
        dwa = even[:, :].rearrange("p (h w) -> p h w", w=W)
        filt = sb("filt", [P, HW])
        sq_junk = filt
        post_att = sb("post_att", [P, C])
        x2 = sb("x2", [P, 2, HW])
        stats = sb("stats", [P, 2, 6])
        msq = sb("msq", [P, 2, 2])
        gmv = sb("gmv", [P, 2, 2])
        gm2 = sb("gm2", [P, 2])
        gvar = sb("gvar", [P, 2])
        grstd = sb("grstd", [P, 2])
        ga = sb("ga", [P, 2])
        gma = sb("gma", [P, 2])
        gb = sb("gb", [P, 2])
        xn = sb("xn", [P, 2, HW])
        qk = sb("qk", [P, 4, QUADS, PX], F32R)
        q_hm = qk[:, 0, :, :]
        q_hl = qk[:, 1, :, :]
        k_hi = qk[:, 2, :, :]
        k_lo = qk[:, 3, :, :]
        v_t = sb("v_t", [P, 2, CH, HEADS // 2, 6 * SLOT], F32R)
        nmax2 = sb("nmax2", [P, 2, CH, QUADS, P])
        q_max = sb("q_max", [P, QUADS, HW], F32R)
        prob = sb("prob", [P, 2, CH, HW])
        p_hi = sb("p_hi", [P, 3, CH, HW], F32R)
        p_lo = sb("p_lo", [P, 3, CH, HW], F32R)
        den2 = sb("den2", [P, CH, HEADS])
        o2 = sb("o2", [P, 2 * QUADS, HW])
        h_t = sb("h_t", [P, CH, C])
        x2_res = sb("x2_res", [P, 2, HW])
        h_c = sb("h_c", [P, 2, HW])
        x3_pair = sb("x3_pair", [P, 2, HW])
        windows = sb("windows", [P, 2, MIXES, H, HT])
        win_0 = sb("win_0", [P, 2, MIXES, 2, H + 2, HT], F32R)
        v_flat = v_t[:, :, :, :, :].rearrange("p m k t c -> p (m k t c)")[:, 0:4 * MIXES * (H + 2) * HT]
        win_1 = v_flat.rearrange("p (e a m h t) -> p e a m h t", e=2, a=MIXES, m=2, t=HT)
        win_hi = [w[:, 0, :, :, :, :] for w in (win_0, win_1)]
        win_lo = [w[:, 1, :, :, :, :] for w in (win_0, win_1)]
        first = sb("first", [P, 2, HW])
        qkv3 = [sb(n, [P, N * HW]) for n in ("q3", "k3", "v3")]
        nmax3 = sb("nmax3", [P, 2, BATCH])
        att3_sum = sb("att3_sum", [P, 2, BATCH])
        att3_inv = sb("att3_inv", [P, 2, BATCH])
        logit3 = [prob[:, n, :, :].rearrange("p k x -> p (k x)") for n in range(2)]
        att3 = [x1[:, :, :].rearrange("p m x -> p (m x)"), x2[:, :, :].rearrange("p m x -> p (m x)")]
        att3_n = [x_in[:, :, :].rearrange("p m x -> p (m x)"), xn[:, :, :].rearrange("p m x -> p (m x)")]
        sq3 = [o0[:, :, :].rearrange("p m x -> p (m x)"), diff0[:, :, :].rearrange("p m x -> p (m x)")]
        v3_t = nmax2[:, :, :, :, :].rearrange("p s k q c -> p s (k q) c")
        w3 = qk[:, :, :, :].rearrange("p s q x -> p (s q x)")
        w3_hi, w3_lo = w3[:, 0:WC], w3[:, WC:2 * WC]
        w_mix = prob[:, :, :, :].rearrange("p n k x -> p (n k x)")[:, 0:2 * KC]
        att3_t = qkv3[0]
        virt = qkv3[1]
        x3_back = qkv3[0]
        act3 = [t[:, :, :].rearrange("p m (h w) -> p m h w", w=W) for t in (x1, x2)]
        windows3 = [t.rearrange("p (a m h t) -> p a m h t", a=MIXES, m=2, t=HT) for t in
                    (prob[:, :, :, :].rearrange("p n k x -> p (n k x)"),
                     nmax2[:, :, :, :, :].rearrange("p s k q c -> p (s k q c)"))]
        joined3 = [t[:, :, :].rearrange("p m (h w) -> p m h w", w=W) for t in (x_in, xn)]
        partial3 = [o2[:, n, :] for n in range(2)]
        y = qkv3[2]
        sum3 = sb("sum3", [P, 2, 2, N])
        tm3 = sb("tm3", [P, N])
        tmv3 = sb("tmv3", [P, 2, N])
        var3 = sb("var3", [P, N])
        rstd3 = sb("rstd3", [P, N])
        la = sb("la", [P, N])
        lma = sb("lma", [P, N])
        lb = sb("lb", [P, N])

        bank = [ctx.enter_context(nc.psum_tensor(f"bank{n}", [P, 512], F32)) for n in range(8)]
        FRONT = (0, 1)
        S_BANK = 2
        ST_BANK = (3, 4)
        O_BANK = (5, 6)
        CONV = 7

        def h_bank(m):
            return (S_BANK, FRONT[1])[m]

        def s_bank(n):
            if n < HEADS:
                return O_BANK[n % 2]
            return O_BANK[1] if n < HEADS + HEADS // 2 + LAG and n % 2 else S_BANK

        def s_before(n):
            return max([k + 1 for k in range(n) if s_bank(k) == s_bank(n)], default=0)

        cst_loaded, cst2_loaded, x_loaded = sem("cst_loaded"), sem("cst2_loaded"), sem("x_loaded")
        wst_loaded = sem("wst_loaded")
        w_mixed, w_halved, w_split_hi, w_split = sem("w_mixed"), sem("w_halved"), sem("w_split_hi"), sem("w_split")
        pool_set, vec_set, vec_pre, bias_mm = sem("pool_set"), sem("vec_set"), sem("vec_pre"), sem("bias_mm")
        bn_pow, table_loaded = sem("bn_pow"), sem("table_loaded")
        xt_done, xt_copied, energy_done, e_min_done = sem("xt_done"), sem("xt_copied"), sem("energy_done"), sem("e_min_done")
        att0_exp, att0_inv_done, att0t_done, att0t_copied = sem("att0_exp"), sem("att0_inv_done"), sem("att0t_done"), sem("att0t_copied")
        o0_done, o0_scaled, diff0_done, sum_x_done = sem("o0_done"), sem("o0_scaled"), sem("diff0_done"), sem("sum_x_done")
        hid0_done, hid0_relu, z0_done, z0_exp = sem("hid0_done"), sem("hid0_relu"), sem("z0_done"), sem("z0_exp")
        z0_chain, x1_done = sem("z0_chain"), sem("x1_done")
        red_done, red_copied, dw_tap, xr_done, n2_done = sem("red_done"), sem("red_copied"), sem("dw_tap"), sem("xr_done"), sem("n2_done")
        n2m_done, rn_done, xh_done = sem("n2m_done"), sem("rn_done"), sem("xh_done")
        hid1_done, hid1_relu, z1_done, z1_exp, z1_chain = sem("hid1_done"), sem("hid1_relu"), sem("z1_done"), sem("z1_exp"), sem("z1_chain")
        xht_done, xht_copied, dft_done, ab_copied = sem("xht_done"), sem("xht_copied"), sem("dft_done"), sem("ab_copied")
        b_signed_done, squares_done = sem("b_signed_done"), sem("squares_done")
        dot1_done, even_done, filt_done = sem("dot1_done"), sem("even_done"), sem("filt_done")
        logit1_done, nmax1_done, att1_exp, att1_chain = sem("logit1_done"), sem("nmax1_done"), sem("att1_exp"), sem("att1_chain")
        even_copied, filt_scaled, patt_done, patt_copied = sem("even_copied"), sem("filt_scaled"), sem("patt_done"), sem("patt_copied")
        y1_done, x2_done = sem("y1_done"), sem("x2_done")
        gn_chain, gsum_done, gvar_done, grstd_done, xn_done = sem("gn_chain"), sem("gsum_done"), sem("gvar_done"), sem("grstd_done"), sem("xn_done")
        qk_done, v_done, qk_high, qk_low, v_copied = sem("qk_done"), sem("v_done"), sem("qk_high"), sem("qk_low"), sem("v_copied")
        k_rows, v_high, p_split = sem("k_rows"), sem("v_high"), sem("p_split")
        s_done, s_max, maxt_done, maxt_copied = sem("s_done"), sem("s_max"), sem("maxt_done"), sem("maxt_copied")
        st_done, st_exp, pv_done, den_done, h_scaled = sem("st_done"), sem("st_exp"), sem("pv_done"), sem("den_done"), sem("h_scaled")
        o2_copied, ot_done, x2_res_done = sem("o2_copied"), sem("ot_done"), sem("x2_res_done")
        ht_done, ht_copied, proj_done, x3_done = sem("ht_done"), sem("ht_copied"), sem("proj_done"), sem("x3_done")
        x3_kept = sem("x3_kept")
        win_done, win_high, win_low = sem("win_done"), sem("win_high"), sem("win_low")
        group_done, first_copied, first_summed = sem("group_done"), sem("first_copied"), sem("first_summed")
        join_chain, joined = sem("join_chain"), sem("joined")
        dot3_done, v3t_done, logit3_done, nmax3_done = sem("dot3_done"), sem("v3t_done"), sem("logit3_done"), sem("nmax3_done")
        att3_exp, att3_inv_done, att3_scaled, att3t_done = sem("att3_exp"), sem("att3_inv_done"), sem("att3_scaled"), sem("att3t_done")
        att3t_copied, v3t_copied, virt_done, virt_copied = sem("att3t_copied"), sem("v3t_copied"), sem("virt_done"), sem("virt_copied")
        sq3_done, sum3_done = sem("sq3_done"), sem("sum3_done")
        ln_chain, tot3_done, var3_done, rstd3_done, ln_ready = sem("ln_chain"), sem("tot3_done"), sem("var3_done"), sem("rstd3_done"), sem("ln_ready")
        act3_done, last_win, last_high, last_low = sem("act3_done"), sem("last_win"), sem("last_high"), sem("last_low")
        last_conv, last_chain, x3_back_in = sem("last_conv"), sem("last_chain"), sem("x3_back_in")
        y_done, y_stored = sem("y_done"), sem("y_stored")

        def tiled(t):
            return t[:, :].rearrange("p (t n x) -> p n t x", n=N, x=GPX)

        def batch(b):
            return slice(b * BATCH * P, (b + 1) * BATCH * P)

        def v_views(m):
            v_m = v_t[:, m, :, :, :].rearrange("p k t (a e z) -> p (k t) a e z", a=3, e=2)
            return (bank[S_BANK][:, m * HW:(m + 1) * HW].rearrange("p (n a d) -> p n a d", a=2, d=DH),
                    v_m[:, :, 0:3:2, 0, 0:DH], v_m[:, :, 0:3:2, 1, 0:DH])

        def conv_bank(j, g):
            return ST_BANK[0] if isinstance(j, int) and j == PAIRS - 1 and g % 2 else CONV

        def make_windows(dve, src, dst):
            even, odd = src[:, :, :, 0:W:2], src[:, :, :, 1:W:2]
            dve.tensor_scalar(dst[:, 0, :, :, 0:1], odd[:, :, :, 0:1], -1.0, None, ALU.mult)
            dve.tensor_tensor(dst[:, 0, :, :, 1:HT], odd[:, :, :, 0:HT - 1], odd[:, :, :, 1:HT], ALU.subtract)
            half = dve.tensor_tensor(dst[:, 1, :, :, :], even, odd, ALU.add)
            dve.tensor_tensor(dst[:, 2, :, :, :], odd, even, ALU.subtract)
            dve.tensor_copy(dst[:, 3, :, :, HT - 1:HT], even[:, :, :, HT - 1:HT])
            return half, dve.tensor_tensor(dst[:, 3, :, :, 0:HT - 1], even[:, :, :, 0:HT - 1], even[:, :, :, 1:HT],
                                           ALU.subtract)

        def halves(t):
            return t[:, :, :].rearrange("p m (e k) -> p m e k", e=2)

        def after(eng, s, value):
            if not (isinstance(value, int) and value <= 0):
                eng.wait_ge(s, value)

        x_d = x.rearrange("n c h w -> c n (h w)")
        out_d = out.rearrange("n c h w -> c n (h w)")

        block = ctx.enter_context(nc.Block())

        @block.sync
        def _(sp):
            sp.dma_start(x_in[:, :, :], x_d[:, 0:2, :]).then_inc(x_loaded, 16)
            sp.dma_start(cst[:, 0:FIRST_W], small[:, 0:FIRST_W]).then_inc(cst_loaded, 16)
            sp.dma_start(cst[:, FIRST_W:], small[:, FIRST_W:]).then_inc(cst2_loaded, 16)

            def load_weights(k):
                if k:
                    sp.wait_ge(w_split, k)
                sp.dma_start(w_stage[:, :], convs[:, k * 3 * KC:(k + 1) * 3 * KC]).then_inc(wst_loaded, 16)

            def load_x(i):
                sp.wait_ge(xt_done, i)
                sp.wait_ge(o0_done, i)
                sp.wait_ge(sum_x_done, i)
                sp.wait_ge(diff0_done, i)
                sp.dma_start(x_in[:, :, :], x_d[:, bass.ds(2 * i, 2), :]).then_inc(x_loaded, 16)

            def store_x3(j):
                sp.wait_ge(x3_done, 2 * j + 2)
                sp.dma_start(out_d[:, bass.ds(2 * j, 2), :], x3_pair[:, :, :]).then_inc(x3_kept, 16)

            load_weights(0)
            load_weights(1)
            load_x(1)
            load_weights(2)
            load_x(2)
            load_weights(3)
            with sp.Fori(3, PAIRS) as i:
                store_x3(i - 3)
                load_x(i)
            for j in (PAIRS - 3, PAIRS - 2, PAIRS - 1):
                store_x3(j)
            sp.wait_ge(x3_kept, 16 * PAIRS)
            sp.wait_ge(tot3_done, BATCHES)
            sp.dma_start(x3_back[:, :].rearrange("p (n x) -> p n x", x=HW), out_d).then_inc(x3_back_in, 16)
            with sp.Fori(0, PAIRS) as i:
                sp.wait_ge(y_done, i + 1)
                sp.dma_start(out_d[:, bass.ds(2 * i, 2), :], y[:, bass.ds(i * PX, PX)]
                             .rearrange("p (m x) -> p m x", m=2)).then_inc(y_stored, 16)
            sp.wait_ge(y_stored, 16 * PAIRS)

        @block.gpsimd
        def _(pool):
            pool.memset(pow_half[:, :], -0.5).then_inc(pool_set, 1)
            pool.memset(red[:, :, :], 0.0).then_inc(pool_set, 1)
            pool.memset(win_0[:, :, :, :, :, :].bitcast(F32), 0.0).then_inc(pool_set, 1)
            pool.memset(nmax2[:, :, :, :, :], 0.0).then_inc(pool_set, 1)
            pool.wait_ge(vec_pre, 1)
            pool.wait_ge(pool_set, 1)
            pool.tensor_tensor(bn_tmp[:, 1:2], bn_tmp[:, 0:1], pow_half[:, 0:1], ALU.pow).then_inc(bn_pow, 1)
            pool.memset(v_t[:, :, :, :, :].bitcast(F32), 0.0).then_inc(pool_set, 1)

            def mix_weights(k):
                g = [w_stage[:, x * KC:(x + 1) * KC] for x in range(3)]
                u1, u2 = w_mix[:, 0:KC], w_mix[:, KC:2 * KC]
                pool.wait_ge(wst_loaded, 16 * (k + 1))
                pool.tensor_tensor(u1, g[0], g[2], ALU.add).then_inc(w_mixed, 1)
                pool.wait_ge(w_mixed, 3 * k + 1)
                pool.tensor_tensor(u2, u1, g[1], ALU.subtract).then_inc(w_mixed, 1)
                pool.wait_ge(w_mixed, 3 * k + 2)
                pool.tensor_tensor(u1, u1, g[1], ALU.add).then_inc(w_mixed, 1)

            def weights_low(k, hi, lo):
                pool.wait_ge(w_split_hi, 2 * k + 2)
                pool.tensor_tensor(lo[:, 0:2 * KC], w_mix, hi[:, 0:2 * KC].bitcast(F32), ALU.subtract)
                for x in range(2):
                    o = (2 + x) * KC
                    ins = pool.tensor_tensor(lo[:, o:o + KC], w_stage[:, 2 * x * KC:(2 * x + 1) * KC],
                                             hi[:, o:o + KC].bitcast(F32), ALU.subtract)
                ins.then_inc(w_split, 1)

            def stage(k, i):
                if k == 3:
                    pool.wait_ge(o0_scaled, 2 * i + 2)
                    pool.wait_ge(x_loaded, 16 * i + 16)
                    pool.tensor_tensor(diff0[:, :, :], x_in[:, :, :], o0[:, :, :], ALU.subtract).then_inc(diff0_done, 1)
                if k == 8:
                    pool.wait_ge(n2m_done, i + 1)
                    pool.tensor_tensor(rn[:, :], n2m[:, :], pow_half[:, 0:1], ALU.pow).then_inc(rn_done, 1)
                if k == 11:
                    pool.wait_ge(ab_copied, i + 1)
                    pool.tensor_tensor(b_signed[:, :], ab[:, 1, :], c("sign_b").to_broadcast([P, P]),
                                       ALU.mult).then_inc(b_signed_done, 1)
                    pool.tensor_tensor(ab_sq[:, :, :], ab[:, :, :], ab[:, :, :], ALU.mult).then_inc(squares_done, 1)
                    pool.tensor_tensor(a_times_b[:, :], ab[:, 0, :], ab[:, 1, :], ALU.mult).then_inc(squares_done, 1)
                if k == 16:
                    pool.wait_ge(gvar_done, i + 1)
                    pool.tensor_tensor(grstd[:, :], gvar[:, :], pow_half[:, 0:2], ALU.pow).then_inc(grstd_done, 1)

            def residual(i):
                pool.wait_ge(x2_done, 2 * i + 2)
                after(pool, x3_done, 2 * i)
                pool.tensor_tensor(x2_res[:, :, :].rearrange("p m x -> p (m x)"),
                                   x2[:, :, :].rearrange("p m x -> p (m x)"),
                                   proj_bias[:, :].to_broadcast([P, PX]), ALU.add).then_inc(x2_res_done, 1)

            def window_low(j, m):
                pool.wait_ge(win_high, 2 * j + m + 1)
                pool.tensor_tensor(win_lo[0][:, :, m, 1:H + 1, :], windows[:, m, :, :, :],
                                   win_hi[0][:, :, m, 1:H + 1, :].bitcast(F32), ALU.subtract).then_inc(win_low, 1)

            def first_sum(j, w):
                pool.wait_ge(first_copied, 3 * j + w + 1)
                pool.tensor_tensor(first[:, 0, :], first[:, 0, :], first[:, 1, :], ALU.add).then_inc(first_summed, 1)

            def prob_low(j, n):
                pool.wait_ge(st_exp, 2 * HEADS * j + n + 1)
                if n >= 3:
                    pool.wait_ge(pv_done, 2 * HEADS * j + n - 2)
                pool.tensor_tensor(p_lo[:, n % 3, :, :], prob[:, n % 2, :, :], p_hi[:, n % 3, :, :].bitcast(F32),
                                   ALU.subtract).then_inc(p_split, 1)

            def slots(j, i=None, cj=None):
                residual(j)
                if not (isinstance(j, int) and j == 0):
                    window_low(j - 1, 1)
                for s in range(SLOTS):
                    if s == 0 and cj is None:
                        mix_weights(2)
                        weights_low(2, w_hi[:, 2, :], w_lo[:, 2, :])
                    if s - 1 in FIRST_OUT and cj is not None and not (i is None and FIRST_OUT[s - 1] == 2):
                        first_sum(cj, FIRST_OUT[s - 1])
                    if s >= HEADS:
                        prob_low(j, s - HEADS)
                    if s in STAGE and i is not None:
                        stage(STAGE[s], i)

            pool.wait_ge(pool_set, 5)
            for a in range(2):
                o = 4 * SLOT * a + DH
                pool.memset(v_t[:, :, :, :, o:o + 1].bitcast(F32), 1.0).then_inc(pool_set, 1)
            mix_weights(0)
            for k in range(STAGES):
                stage(k, 0)
                if k == 3:
                    weights_low(0, w_hi[:, 0, :], w_lo[:, 0, :])
                if k == 8:
                    mix_weights(1)
                if k == 11:
                    weights_low(1, w_hi[:, 1, :], w_lo[:, 1, :])
            pool.wait_ge(vec_set, 6)
            slots(0, 1)
            slots(1, 2, 0)
            with pool.Fori(3, PAIRS) as i:
                slots(i - 1, i, i - 2)
            slots(PAIRS - 1, None, PAIRS - 2)
            first_sum(PAIRS - 2, 2)
            mix_weights(3)
            pool.wait_ge(pv_done, 2 * HEADS * PAIRS)
            weights_low(3, w3_hi, w3_lo)
            for w in range(2):
                first_sum(PAIRS - 1, w)
            for b in range(BATCHES):
                pool.wait_ge(att3_inv_done, b + 1)
                if b >= 2:
                    pool.wait_ge(att3t_done, b - 1)
                pool.tensor_tensor(att3_n[b % 2].rearrange("p (g x) -> p g x", g=BATCH),
                                   att3[b % 2].rearrange("p (g x) -> p g x", g=BATCH),
                                   att3_inv[:, b % 2, :].unsqueeze(2).to_broadcast([P, BATCH, P]),
                                   ALU.mult).then_inc(att3_scaled, 1)
                if b == UNITS // UNITS_V[0]:
                    first_sum(PAIRS - 1, 2)
            pool.memset(v_flat.bitcast(F32), 0.0).then_inc(pool_set, 1)
            for g, cols in enumerate(LN_GROUPS):
                pool.wait_ge(var3_done, 1)
                pool.tensor_tensor(rstd3[:, cols], var3[:, cols], pow_half[:, cols], ALU.pow).then_inc(rstd3_done, 1)

            def low_half(i, s, h):
                pool.wait_ge(last_high, 4 * i + 2 * s + h + 1)
                for m in range(2):
                    ins = pool.tensor_tensor(win_lo[s][:, 2 * h:2 * h + 2, m, 1:H + 1, :],
                                             windows3[s][:, 2 * h:2 * h + 2, m, :, :],
                                             win_hi[s][:, 2 * h:2 * h + 2, m, 1:H + 1, :].bitcast(F32), ALU.subtract)
                ins.then_inc(last_low, 1)

            pool.wait_ge(last_low, 2)
            low_half(0, 1, 0)
            low_half(0, 1, 1)
            with pool.Fori(1, PAIRS // 2) as i:
                for s in range(2):
                    low_half(i, s, 0)
                    low_half(i, s, 1)

        @block.scalar
        def _(act):
            def split_weights(k, hi):
                act.wait_ge(w_mixed, 3 * k + 3)
                act.activation(w_mix, w_mix, ACT.Copy, scale=0.5).then_inc(w_halved, 1)
                act.activation(hi[:, 2 * KC:].rearrange("p (x c) -> p x c", x=2),
                               w_stage[:, :].rearrange("p (x c) -> p x c", x=3)[:, 0:3:2, :],
                               ACT.Copy).then_inc(w_split_hi, 1)
                act.wait_ge(w_halved, k + 1)
                act.activation(hi[:, 0:2 * KC], w_mix, ACT.Copy).then_inc(w_split_hi, 1)

            def values(i):
                act.wait_ge(v_done, i + 1)
                for m in range(2):
                    v, v_h, v_l = v_views(m)
                    act.activation(v_h, v, ACT.Copy).then_inc(v_high, 1)

            def ones_rows(i):
                for q in range(QUADS):
                    act.wait_ge(qk_low, 4 * i + QUADS + q + 1)
                    act.activation(k_lo[:, q, :], k_lo[:, q, :].bitcast(F32), ACT.Identity, scale=c("hi_rows"),
                                   bias=c("one_row")).then_inc(k_rows, 1)

            def window_high(j, m):
                after(act, group_done, GROUPS * j)
                act.wait_ge(win_done, 2 * j + m + 1)
                act.activation(win_hi[0][:, :, m, 1:H + 1, :], windows[:, m, :, :, :], ACT.Copy).then_inc(win_high, 1)

            def first_copy(j, w):
                act.wait_ge(group_done, GROUPS * j + 2 * w + 1)
                if w:
                    act.wait_ge(joined, 3 * j + w)
                act.activation(first[:, :, :].rearrange("p a x -> p (a x)"), bank[conv_bank(j, 2 * w)][:, :],
                               ACT.Copy).then_inc(first_copied, 1)

            def stage(k, i):
                if k == 0:
                    act.wait_ge(xt_done, i + 1)
                    act.activation(xh_ab[:, :], bank[0][:, :], ACT.Copy).then_inc(xt_copied, 1)
                    act.wait_ge(x_loaded, 16 * i + 16)
                    for m in range(2):
                        ins = act.activation((filt, even)[m][:, :], x_in[:, m, :], ACT.Copy, accum_out=sum_x[:, m:m + 1])
                    ins.then_inc(sum_x_done, 1)
                if k == 1:
                    act.wait_ge(e_min_done, i + 1)
                    for m in range(2):
                        act.activation(att0[:, m, :], bank[1][:, m * C:(m + 1) * C], ACT.Exp, bias=e_min[:, m:m + 1],
                                       scale=-1.0, accum_out=att0_sum[:, m:m + 1]).then_inc(att0_exp, 1)
                if k == 2:
                    act.wait_ge(att0t_done, i + 1)
                    act.activation(att0_t[:, :, :], bank[0][:, 0:2 * C], ACT.Copy).then_inc(att0t_copied, 1)
                if k == 3:
                    act.wait_ge(o0_done, i + 1)
                    act.wait_ge(att0_inv_done, i + 1)
                    after(act, x1_done, 2 * i)
                    for m in range(2):
                        act.activation(o0[:, m, :], bank[1][:, m * HW:(m + 1) * HW], ACT.Identity,
                                       scale=att0_inv[:, m:m + 1], accum_out=sum_o0[:, m:m + 1]).then_inc(o0_scaled, 1)
                if k == 4:
                    act.wait_ge(hid0_done, i + 1)
                    act.activation(hid0[:, :], bank[0][0:HID0, 0:2], ACT.Relu, bias=c("b1", HID0),
                                   scale=1.0 / HW).then_inc(hid0_relu, 1)
                if k == 5:
                    act.wait_ge(z0_done, i + 1)
                    act.activation(z0[:, :], bank[1][:, 0:2], ACT.Exp, bias=neg_b2[:, :], scale=-1.0).then_inc(z0_exp, 1)
                if k == 6:
                    act.wait_ge(red_done, i + 1)
                    act.activation(red[:, 1:H + 1, 1:W + 1], bank[0][:, 0:HW].rearrange("p (h w) -> p h w", w=W),
                                   ACT.Identity, bias=c("reduce_b")).then_inc(red_copied, 1)
                if k == 8:
                    act.wait_ge(dw_tap, TAPS * i + TAPS)
                    act.activation(xr[:, :], even[:, :], ACT.Relu, bias=bn_shift[:, :],
                                   scale=bn_scale[:, :], accum_out=sum_xr[:, :]).then_inc(xr_done, 1)
                    act.wait_ge(xr_done, i + 1)
                    act.activation(sq_junk[:, :], xr[:, :], ACT.Square, accum_out=n2[:, :]).then_inc(n2_done, 1)
                if k == 9:
                    act.wait_ge(hid1_done, i + 1)
                    act.activation(hid1[:, :], bank[1][0:2 * HID1, 0:1], ACT.Relu, bias=c("gb1", 2 * HID1),
                                   scale=1.0 / HW).then_inc(hid1_relu, 1)
                if k == 10:
                    act.wait_ge(z1_done, i + 1)
                    act.activation(z1[:, :], bank[0][:, 0:1], ACT.Exp, bias=neg_gb2[:, :], scale=-1.0).then_inc(z1_exp, 1)
                if k == 11:
                    act.wait_ge(dft_done, i + 1)
                    act.activation(ab[:, :, :], bank[0][:, 0:2 * P], ACT.Copy).then_inc(ab_copied, 1)
                if k == 12:
                    act.wait_ge(even_done, i + 1)
                    act.activation(even[:, :], bank[0][:, 0:HW], ACT.Copy).then_inc(even_copied, 1)
                    act.wait_ge(nmax1_done, i + 1)
                    act.activation(att1[:, :], logit1[:, :], ACT.Exp, bias=nmax1[:, :],
                                   accum_out=att1_sum[:, :]).then_inc(att1_exp, 1)
                if k == 13:
                    act.wait_ge(filt_done, i + 1)
                    act.wait_ge(z1_chain, 3 * i + 3)
                    act.activation(filt[:, :], bank[1][:, 0:HW], ACT.Identity, scale=fscale[:, :]).then_inc(filt_scaled, 1)

            def o2_copy(j, m, half):
                act.wait_ge(pv_done, 2 * HEADS * j + HEADS * m + HEADS // 2 * (half + 1))
                after(act, ot_done, 2 * j + m)
                act.activation(o2[:, QUADS * half:QUADS * (half + 1), :].rearrange("p q x -> p (q x)"),
                               bank[O_BANK[half]][:, :], ACT.Copy).then_inc(o2_copied, 1)

            def h_copy(j, m):
                act.wait_ge(ht_done, 2 * j + m + 1)
                act.activation(h_c[:, m, :], bank[h_bank(m)][:, 0:HW], ACT.Copy).then_inc(ht_copied, 1)

            def qk_high_parts(i, what):
                for q in range(QUADS):
                    if what == "q":
                        act.wait_ge(qk_done, 4 * i + q + 1)
                        act.activation(q_hm[:, q, :], bank[FRONT[q]][:, :], ACT.Identity, bias=bq_lo[:, q:q + 1],
                                       scale=c("lo_rows")).then_inc(qk_high, 1)
                    else:
                        act.wait_ge(qk_done, 4 * i + QUADS + q + 1)
                        act.activation(k_hi[:, q, :], bank[ST_BANK[q]][:, :], ACT.Identity,
                                       bias=c("bk")[:, q:q + 1]).then_inc(qk_high, 1)

            def slots(j, i=None, cj=None):
                for s in range(SLOTS):
                    n = s - HEADS
                    before = not (isinstance(j, int) and j == 0)
                    if s == 1 and before:
                        h_copy(j - 1, 1)
                    if s == V_HIGH_SLOT:
                        values(j)
                    if s == ONES_SLOT:
                        ones_rows(j)
                    if s == WINDOW_SLOT and before:
                        window_high(j - 1, 0)
                        window_high(j - 1, 1)
                    if s == 2 and cj is None:
                        split_weights(2, w_hi[:, 2, :])
                    if n >= 0:
                        scores = bank[ST_BANK[n % 2]][:, :]
                        act.wait_ge(st_done, 2 * HEADS * j + n + 1)
                        if n >= 3:
                            act.wait_ge(pv_done, 2 * HEADS * j + n - 2)
                        act.activation(p_hi[:, n % 3, :, :], scores, ACT.Exp, scale=L2_SCALE)
                        if n >= 2:
                            act.wait_ge(p_split, 2 * HEADS * j + n - 1)
                        if n == 0 and cj is None:
                            act.wait_ge(w_split, 3)
                        act.activation(prob[:, n % 2, :, :], scores, ACT.Exp, scale=L2_SCALE).then_inc(st_exp, 1)
                    if n == HEADS // 2 + LAG - 1 or n == HEADS + HEADS // 2 + LAG - 1:
                        o2_copy(j, n // HEADS, 0)
                    if n == HEADS + LAG - 1:
                        o2_copy(j, 0, 1)
                    if s == OUT_SLOT + 1:
                        h_copy(j, 0)
                    if s in FIRST_OUT and cj is not None and not (i is None and FIRST_OUT[s] == 2):
                        first_copy(cj, FIRST_OUT[s])
                    if s in STAGE and i is not None:
                        stage(STAGE[s], i)
                if i is not None:
                    qk_high_parts(i, "q")
                o2_copy(j, 1, 1)
                if i is not None:
                    qk_high_parts(i, "k")
                else:
                    first_copy(cj, 2)

            act.wait_ge(pool_set, 1)
            act.activation(z1[:, :], pow_half[:, 0:1], ACT.Exp).then_inc(table_loaded, 1)
            act.wait_ge(cst_loaded, 16)
            for k in range(STAGES):
                if k == 3:
                    act.wait_ge(vec_set, 5)
                    act.wait_ge(pool_set, 7)
                stage(k, 0)
                if k == 5:
                    split_weights(0, w_hi[:, 0, :])
                if k == 10:
                    split_weights(1, w_hi[:, 1, :])
            qk_high_parts(0, "q")
            qk_high_parts(0, "k")
            slots(0, 1)
            slots(1, 2, 0)
            with act.Fori(3, PAIRS) as i:
                slots(i - 1, i, i - 2)
            slots(PAIRS - 1, None, PAIRS - 2)
            h_copy(PAIRS - 1, 1)
            window_high(PAIRS - 1, 0)
            window_high(PAIRS - 1, 1)
            split_weights(3, w3_hi)
            first_copy(PAIRS - 1, 0)
            first_copy(PAIRS - 1, 1)
            def v3t_copy(b):
                act.wait_ge(v3t_done, b + 1)
                if b >= 2:
                    act.wait_ge(virt_done, b - 1)
                act.activation(v3_t[:, b % 2, :, :], bank[2 + b % 2][:, :], ACT.Copy).then_inc(v3t_copied, 1)

            for b in range(BATCHES + 2):
                if b < BATCHES:
                    act.wait_ge(nmax3_done, b + 1)
                    if b >= 2:
                        act.wait_ge(att3_scaled, b - 1)
                    for g in range(BATCH):
                        act.activation(att3[b % 2][:, g * P:(g + 1) * P], logit3[b % 2][:, g * P:(g + 1) * P], ACT.Exp,
                                       bias=nmax3[:, b % 2, g:g + 1],
                                       accum_out=att3_sum[:, b % 2, g:g + 1]).then_inc(att3_exp, 1)
                else:
                    v3t_copy(b - BATCHES)
                if b == UNITS // UNITS_V[0]:
                    first_copy(PAIRS - 1, 2)
                a = b - 2
                if a >= 0:
                    act.wait_ge(att3t_done, a + 1)
                    act.activation(att3_t[:, batch(a)], bank[4 + a % 2][:, :], ACT.Copy).then_inc(att3t_copied, 1)
            for b in range(2, BATCHES + 1):
                if b < BATCHES:
                    v3t_copy(b)
                for a in (0, 1) if b == 2 else (b - 1,):
                    act.wait_ge(virt_done, a + 1)
                    if a >= 2:
                        act.wait_ge(sum3_done, 2 * (a - 1))
                    act.activation(virt[:, batch(a)], bank[6 + a % 2][:, :], ACT.Copy).then_inc(virt_copied, 1)
                    act.activation(sq3[a % 2], bank[6 + a % 2][:, :], ACT.Square).then_inc(sq3_done, 1)

            def last_inputs(i, s):
                after(act, last_win, 4 * i + 2 * s - 2)
                if isinstance(i, int) and i == 0:
                    act.wait_ge(ln_ready, s + 1)
                for m in range(2):
                    n = 4 * i + 2 * s + m
                    act.activation(act3[s][:, m, :, :].rearrange("p h (t e) -> p h e t", e=2),
                                   tiled(virt)[:, bass.ds(n, 1), :, :].rearrange("p n (h e) t -> p (n h) e t", e=2),
                                   ACT.Relu, bias=lb[:, bass.ds(n, 1)], scale=la[:, bass.ds(n, 1)]).then_inc(act3_done, 1)
                after(act, last_conv, 2 * i + s - 1)
                for h in range(2):
                    act.wait_ge(last_win, 4 * i + 2 * s + h + 1)
                    for m in range(2):
                        ins = act.activation(win_hi[s][:, 2 * h:2 * h + 2, m, 1:H + 1, :],
                                             windows3[s][:, 2 * h:2 * h + 2, m, :, :], ACT.Copy)
                    ins.then_inc(last_high, 1)

            act.wait_ge(pool_set, 8)
            last_inputs(0, 0)
            last_inputs(0, 1)
            with act.Fori(1, PAIRS // 2) as i:
                last_inputs(i, 0)
                last_inputs(i, 1)

        @block.vector
        def _(dve):
            dve.memset(ones_r[:, :].bitcast(F32), 1.0).then_inc(vec_set, 1)
            dve.wait_ge(cst_loaded, 16)
            dve.tensor_scalar(bn_tmp[:, 0:1], c("bn_var"), 1e-5, None, ALU.add).then_inc(vec_pre, 1)
            dve.tensor_scalar(neg_b2[:, :], c("b2"), -1.0, None, ALU.mult).then_inc(vec_set, 1)
            dve.tensor_scalar(neg_gb2[:, :], c("gb2"), -1.0, None, ALU.mult).then_inc(vec_set, 1)
            dve.tensor_scalar(bq_lo[:, :], c("bq"), c("lo_rows"), None, ALU.mult).then_inc(vec_set, 1)
            dve.tensor_tensor(bn_shift[:, :], c("dw_b"), c("bn_mean"), ALU.subtract).then_inc(vec_pre, 1)
            dve.wait_ge(bn_pow, 1)
            dve.tensor_tensor(bn_scale[:, :], bn_tmp[:, 1:2], c("bn_gamma"), ALU.mult).then_inc(vec_pre, 1)
            dve.wait_ge(vec_pre, 3)
            dve.scalar_tensor_tensor(bn_shift[:, :], bn_shift[:, :], bn_scale[:, :], c("bn_beta"),
                                     ALU.mult, ALU.add).then_inc(vec_set, 1)
            dve.wait_ge(bias_mm, 1)
            dve.tensor_tensor(proj_bias[:, :], bank[CONV][:, 0:1], c("bproj"), ALU.add).then_inc(vec_set, 1)
            dve.wait_ge(vec_set, 6)

            def stage(k, i):
                if k == 1:
                    dve.wait_ge(energy_done, i + 1)
                    dve.tensor_reduce(e_min[:, :], bank[1][:, 0:2 * C].rearrange("p (m c) -> p m c", m=2), X,
                                      ALU.min).then_inc(e_min_done, 1)
                    dve.wait_ge(att0_exp, 2 * i + 2)
                    dve.reciprocal(att0_inv[:, :], att0_sum[:, :]).then_inc(att0_inv_done, 1)
                if k == 5:
                    dve.wait_ge(z0_exp, i + 1)
                    dve.tensor_scalar(z0p[:, :], z0[:, :], 1.0, None, ALU.add).then_inc(z0_chain, 1)
                    dve.wait_ge(z0_chain, 2 * i + 1)
                    dve.reciprocal(se[:, :], z0p[:, :]).then_inc(z0_chain, 1)
                    dve.wait_ge(z0_chain, 2 * i + 2)
                    dve.wait_ge(diff0_done, i + 1)
                    for m in range(2):
                        dve.scalar_tensor_tensor(x1[:, m, :], diff0[:, m, :], se[:, m:m + 1], o0[:, m, :],
                                                 ALU.mult, ALU.add).then_inc(x1_done, 1)
                if k in (6, 7, 8):
                    dve.wait_ge(red_copied, i + 1)
                    for t in range(3 * (k - 6), 3 * (k - 5)):
                        tap = red[:, t // 3:t // 3 + H, t % 3:t % 3 + W]
                        wt = c("dw")[:, t:t + 1]
                        if t == 0:
                            dve.tensor_scalar(dwa, tap, wt, None, ALU.mult).then_inc(dw_tap, 1)
                        else:
                            dve.wait_ge(dw_tap, TAPS * i + t)
                            dve.scalar_tensor_tensor(dwa, tap, wt, dwa, ALU.mult,
                                                     ALU.add).then_inc(dw_tap, 1)
                if k == 8:
                    dve.wait_ge(n2_done, i + 1)
                    dve.tensor_scalar(n2m[:, :], n2[:, :], 1e-24, None, ALU.max).then_inc(n2m_done, 1)
                if k == 9:
                    dve.wait_ge(rn_done, i + 1)
                    dve.tensor_scalar(xh, xr[:, :], rn[:, :], None, ALU.mult).then_inc(xh_done, 1)
                    dve.wait_ge(n2m_done, i + 1)
                    dve.tensor_tensor(nrm[:, :], n2m[:, :], rn[:, :], ALU.mult).then_inc(xh_done, 1)
                if k == 10:
                    dve.wait_ge(xht_done, i + 1)
                    dve.tensor_copy(xh_t[:, :, :].rearrange("p k c -> p (k c)"), bank[1][:, 0:HW]).then_inc(xht_copied, 1)
                    dve.wait_ge(z1_exp, i + 1)
                    dve.tensor_scalar(z1p[:, :], z1[:, :], 1.0, None, ALU.add).then_inc(z1_chain, 1)
                    dve.wait_ge(z1_chain, 3 * i + 1)
                    dve.reciprocal(gate1[:, :], z1p[:, :]).then_inc(z1_chain, 1)
                    dve.wait_ge(z1_chain, 3 * i + 2)
                    dve.tensor_tensor(fscale[:, :], gate1[:, :], n2m[:, :], ALU.mult).then_inc(z1_chain, 1)
                if k == 12:
                    if isinstance(i, int) and i == 0:
                        dve.wait_ge(cst2_loaded, 16)
                    dve.wait_ge(dot1_done, i + 1)
                    dve.scalar_tensor_tensor(logit1[:, :], bank[1][:, 0:P], c("temp"), c("mask1"), ALU.mult,
                                             ALU.add).then_inc(logit1_done, 1)
                    dve.wait_ge(logit1_done, i + 1)
                    dve.tensor_reduce(nmax1[:, :], logit1[:, :], X, ALU.max, negate=True).then_inc(nmax1_done, 1)
                    dve.wait_ge(att1_exp, i + 1)
                    dve.reciprocal(att1_inv[:, :], att1_sum[:, :]).then_inc(att1_chain, 1)
                    dve.wait_ge(att1_chain, 2 * i + 1)
                    dve.tensor_scalar(att1_n[:, :], att1[:, :], att1_inv[:, :], None, ALU.mult).then_inc(att1_chain, 1)
                if k == 14:
                    dve.wait_ge(patt_done, i + 1)
                    dve.wait_ge(xh_done, 2 * i + 2)
                    dve.tensor_scalar(post_att[:, :], bank[0][:, 0:C], nrm[:, :], None, ALU.mult).then_inc(patt_copied, 1)
                if k == 15:
                    dve.wait_ge(y1_done, i + 1)
                    dve.wait_ge(x1_done, 2 * i + 2)
                    after(dve, x2_res_done, i)
                    for m in range(2):
                        dve.scalar_tensor_tensor(x2[:, m, :], bank[m][:, 0:HW], c("post_b"), x1[:, m, :],
                                                 ALU.add, ALU.add).then_inc(x2_done, 1)
                    for m in range(2):
                        dve.wait_ge(x2_done, 2 * i + m + 1)
                        dve.bn_stats(stats[:, m, :], x2[:, m, :]).then_inc(gn_chain, 1)
                    dve.wait_ge(gn_chain, 7 * i + 2)
                    dve.tensor_tensor(msq[:, :, :], halves(stats)[:, :, :, 1], halves(stats)[:, :, :, 1],
                                      ALU.mult).then_inc(gn_chain, 1)
                    dve.wait_ge(gn_chain, 7 * i + 3)
                    dve.scalar_tensor_tensor(halves(stats)[:, :, :, 2], halves(stats)[:, :, :, 2], 2.0 / HW,
                                             msq[:, :, :], ALU.mult, ALU.add).then_inc(gn_chain, 1)
                if k == 16:
                    dve.wait_ge(gsum_done, i + 1)
                    dve.tensor_copy(gmv[:, :, :].rearrange("p m k -> p (m k)"), bank[0][:, 0:4]).then_inc(gn_chain, 1)
                    dve.wait_ge(gn_chain, 7 * i + 5)
                    dve.tensor_tensor(gm2[:, :], gmv[:, :, 0], gmv[:, :, 0], ALU.mult).then_inc(gn_chain, 1)
                    dve.wait_ge(gn_chain, 7 * i + 6)
                    dve.tensor_tensor(gm2[:, :], gmv[:, :, 1], gm2[:, :], ALU.subtract).then_inc(gn_chain, 1)
                    dve.wait_ge(gn_chain, 7 * i + 7)
                    dve.tensor_scalar(gvar[:, :], gm2[:, :], 1e-5, None, ALU.add).then_inc(gvar_done, 1)
                    dve.wait_ge(grstd_done, i + 1)
                    dve.tensor_scalar(ga[:, :], grstd[:, :], c("gn_gamma"), None, ALU.mult).then_inc(xn_done, 1)
                    dve.wait_ge(xn_done, 5 * i + 1)
                    dve.tensor_tensor(gma[:, :], gmv[:, :, 0], ga[:, :], ALU.mult).then_inc(xn_done, 1)
                    dve.wait_ge(xn_done, 5 * i + 2)
                    dve.tensor_scalar(gb[:, :], gma[:, :], -1.0, c("gn_beta"), ALU.mult, ALU.add).then_inc(xn_done, 1)
                    dve.wait_ge(xn_done, 5 * i + 3)
                    for m in range(2):
                        dve.tensor_scalar(xn[:, m, :], x2[:, m, :], ga[:, m:m + 1], gb[:, m:m + 1], ALU.mult,
                                          ALU.add).then_inc(xn_done, 1)

            def qk_low_parts(i, what):
                for q in range(QUADS):
                    if what == "q":
                        dve.wait_ge(qk_high, 4 * i + q + 1)
                        dve.scalar_tensor_tensor(q_hl[:, q, :], bank[FRONT[q]][:, :], c("bq")[:, q:q + 1],
                                                 q_hm[:, q, :].bitcast(F32), ALU.add, ALU.subtract).then_inc(qk_low, 1)
                    else:
                        dve.wait_ge(qk_high, 4 * i + QUADS + q + 1)
                        dve.scalar_tensor_tensor(k_lo[:, q, :], bank[ST_BANK[q]][:, :], c("bk")[:, q:q + 1],
                                                 k_hi[:, q, :].bitcast(F32), ALU.add, ALU.subtract).then_inc(qk_low, 1)

            def values(i):
                dve.wait_ge(v_high, 2 * i + 2)
                for m in range(2):
                    v, v_h, v_l = v_views(m)
                    dve.tensor_tensor(v_l, v, v_h.bitcast(F32), ALU.subtract).then_inc(v_copied, 1)

            def join_max(j, m):
                dve.wait_ge(maxt_done, 2 * j + m + 1)
                if m:
                    dve.wait_ge(st_done, 2 * HEADS * j + HEADS)
                dve.scalar_tensor_tensor(q_max[:, :, :], q_hl[:, :, m * HW:(m + 1) * HW].bitcast(F32), c("hi_rows"),
                                         bank[ST_BANK[1]][:, :].rearrange("p (q x) -> p q x", q=QUADS),
                                         ALU.mult, ALU.add).then_inc(maxt_copied, 1)

            def row_max(j, n):
                m, h = n // HEADS, n % HEADS
                dve.wait_ge(s_done, 2 * HEADS * j + n + 1)
                col = SLOT * (h % 4) + DH
                dve.tensor_reduce(nmax2[:, m, :, h // 4, col:col + 1],
                                  bank[s_bank(n)][:, :].rearrange("p (k s) -> p k s", k=CH), X, ALU.max,
                                  negate=True).then_inc(s_max, 1)

            def normalise(j, m):
                out_h = bank[S_BANK][:, :].rearrange("p (n w) -> p n w", w=SLOT)
                dve.wait_ge(ot_done, 2 * j + m + 1)
                dve.reciprocal(den2[:, :, :].rearrange("p k h -> p (k h)"), out_h[:, :, DH]).then_inc(den_done, 1)
                dve.wait_ge(den_done, 2 * j + m + 1)
                dve.tensor_tensor(h_t[:, :, :].rearrange("p k (h d) -> p (k h) d", d=DH), out_h[:, :, 0:DH],
                                  den2[:, :, :].rearrange("p k h -> p (k h)").unsqueeze(2)
                                  .to_broadcast([P, CH * HEADS, DH]), ALU.mult).then_inc(h_scaled, 1)

            def add_x2(j, m):
                dve.wait_ge(proj_done, 2 * j + m + 1)
                dve.wait_ge(x2_res_done, j + 1)
                after(dve, x3_kept, 16 * j)
                dve.tensor_tensor(x3_pair[:, m, :], bank[h_bank(m)][:, HW:2 * HW], x2_res[:, m, :],
                                  ALU.add).then_inc(x3_done, 1)

            def make_window(j, m):
                dve.wait_ge(x3_done, 2 * j + m + 1)
                after(dve, win_low, 2 * j)
                make_windows(dve, x3_pair[:, m:m + 1, :].rearrange("p m (h w) -> p m h w", w=W),
                             windows[:, m, :, :, :].unsqueeze(2))[1].then_inc(win_done, 1)

            def window_low(j, m):
                dve.wait_ge(win_high, 2 * j + m + 1)
                dve.tensor_tensor(win_lo[0][:, :, m, 1:H + 1, :], windows[:, m, :, :, :],
                                  win_hi[0][:, :, m, 1:H + 1, :].bitcast(F32), ALU.subtract).then_inc(win_low, 1)

            def join(j, w):
                second = bank[conv_bank(j, 2 * w + 1)]
                out = tiled(qkv3[w])[:, bass.ds(2 * j, 2), :, :].rearrange("p n (h e) t -> p n h e t", e=2)
                dve.wait_ge(first_summed, 3 * j + w + 1)
                dve.wait_ge(group_done, GROUPS * j + 2 * w + 2)
                dve.tensor_tensor(first[:, 1, :], first[:, 1, :], second[:, 0:HW], ALU.subtract).then_inc(join_chain, 1)
                for e in range(2):
                    if e:
                        dve.wait_ge(join_chain, 3 * j + w + 1)
                    ins = dve.tensor_tensor(out[:, :, :, e, :], first[:, e, :].rearrange("p (n h t) -> p n h t", n=2, t=HT),
                                            second[:, e * HW:(e + 1) * HW].rearrange("p (n h t) -> p n h t", n=2, t=HT),
                                            (ALU.add, ALU.subtract)[e])
                ins.then_inc(joined, 1)

            def slots(j, i=None, cj=None):
                for s in range(SLOTS):
                    if s in (HEADS, 2 * HEADS):
                        join_max(j, s // HEADS - 1)
                    if s == 2 and not (isinstance(j, int) and j == 0):
                        add_x2(j - 1, 1)
                        make_window(j - 1, 1)
                    if s < 2 * HEADS:
                        row_max(j, s)
                    if s == len(UNITS_LATE) - 1 and cj is not None and not (isinstance(cj, int) and cj == 0):
                        join(cj - 1, 2)
                    if s == WINDOW_SLOT and not (isinstance(j, int) and j == 0):
                        window_low(j - 1, 0)
                    if s == K_LOW_SLOT:
                        qk_low_parts(j, "k")
                    if s == V_LOW_SLOT:
                        values(j)
                    if s == OUT_SLOT:
                        normalise(j, 0)
                    if s == OUT_SLOT + 2:
                        add_x2(j, 0)
                    if s in SECOND_OUT and cj is not None:
                        join(cj, SECOND_OUT[s])
                    if s in STAGE and i is not None:
                        stage(STAGE[s], i)
                if i is not None:
                    make_window(j, 0)
                    qk_low_parts(i, "q")
                normalise(j, 1)

            for k in range(STAGES):
                if k == 6:
                    dve.wait_ge(pool_set, 7)
                stage(k, 0)
            qk_low_parts(0, "q")
            slots(0, 1)
            slots(1, 2, 0)
            with dve.Fori(3, PAIRS) as i:
                slots(i - 1, i, i - 2)
            slots(PAIRS - 1, None, PAIRS - 2)
            make_window(PAIRS - 1, 0)
            add_x2(PAIRS - 1, 1)
            window_low(PAIRS - 1, 0)
            make_window(PAIRS - 1, 1)
            join(PAIRS - 2, 2)
            window_low(PAIRS - 1, 1)
            join(PAIRS - 1, 0)
            join(PAIRS - 1, 1)
            dve.wait_ge(w_split, 4)
            mask = c("mask3").unsqueeze(1).to_broadcast([P, BATCH, P])
            for b in range(BATCHES + 1):
                if b < BATCHES:
                    dve.wait_ge(dot3_done, b + 1)
                    if b >= 2:
                        dve.wait_ge(att3_exp, BATCH * (b - 1))
                    logits = logit3[b % 2].rearrange("p (g x) -> p g x", g=BATCH)
                    dve.scalar_tensor_tensor(logits, bank[b % 2][:, :].rearrange("p (g x) -> p g x", g=BATCH),
                                             L3_SCALE, mask, ALU.mult, ALU.add).then_inc(logit3_done, 1)
                    dve.wait_ge(logit3_done, b + 1)
                    dve.tensor_reduce(nmax3[:, b % 2, :], logits, X, ALU.max, negate=True).then_inc(nmax3_done, 1)
                a = b - 1
                if a >= 0:
                    dve.wait_ge(att3_exp, BATCH * (a + 1))
                    if a >= 2:
                        dve.wait_ge(att3_scaled, a - 1)
                    dve.reciprocal(att3_inv[:, a % 2, :], att3_sum[:, a % 2, :]).then_inc(att3_inv_done, 1)
                if b == BATCHES - 1:
                    join(PAIRS - 1, 2)
            for b in range(BATCHES):
                if b >= 2:
                    dve.wait_ge(tot3_done, b - 1)
                for k, (source, ready) in enumerate(((virt[:, batch(b)], virt_copied), (sq3[b % 2], sq3_done))):
                    dve.wait_ge(ready, b + 1)
                    dve.tensor_reduce(sum3[:, b % 2, k, :], source.rearrange("p (g n x) -> p n g x", n=N, x=GPX), XY,
                                      ALU.add).then_inc(sum3_done, 1)
            dve.wait_ge(tot3_done, BATCHES)
            dve.tensor_copy(tmv3[:, :, :].rearrange("p k n -> p (k n)"), bank[0][:, 0:2 * N]).then_inc(ln_chain, 1)
            dve.wait_ge(ln_chain, 1)
            dve.tensor_tensor(tm3[:, :], tmv3[:, 0, :], tmv3[:, 0, :], ALU.mult).then_inc(ln_chain, 1)
            dve.wait_ge(ln_chain, 2)
            dve.scalar_tensor_tensor(var3[:, :], tmv3[:, 1, :], 1e-5, tm3[:, :], ALU.add, ALU.subtract).then_inc(var3_done, 1)
            def factors(g):
                cols = LN_GROUPS[g]
                dve.wait_ge(rstd3_done, g + 1)
                dve.tensor_scalar(la[:, cols], rstd3[:, cols], c("ln_gamma"), None, ALU.mult).then_inc(ln_chain, 1)
                dve.wait_ge(ln_chain, 2 * g + 3)
                dve.tensor_tensor(lma[:, cols], tmv3[:, 0, cols], la[:, cols], ALU.mult).then_inc(ln_chain, 1)
                dve.wait_ge(ln_chain, 2 * g + 4)
                dve.tensor_scalar(lb[:, cols], lma[:, cols], -1.0, c("ln_beta"), ALU.mult, ALU.add).then_inc(ln_ready, 1)

            def last_windows(i, s):
                dve.wait_ge(act3_done, 4 * i + 2 * s + 2)
                after(dve, last_low, 4 * i + 2 * s - 2)
                for half in make_windows(dve, act3[s], windows3[s]):
                    half.then_inc(last_win, 1)

            def first_low(h):
                dve.wait_ge(last_high, h + 1)
                for m in range(2):
                    ins = dve.tensor_tensor(win_lo[0][:, 2 * h:2 * h + 2, m, 1:H + 1, :],
                                            windows3[0][:, 2 * h:2 * h + 2, m, :, :],
                                            win_hi[0][:, 2 * h:2 * h + 2, m, 1:H + 1, :].bitcast(F32), ALU.subtract)
                ins.then_inc(last_low, 1)

            def last_join(i, s):
                m0, m1 = [bank[2 * s][:, e * HW:(e + 1) * HW] for e in range(2)]
                m2, m3 = [bank[2 * s + 1][:, e * HW:(e + 1) * HW] for e in range(2)]
                k = 5 * (2 * i + s)
                dve.wait_ge(last_conv, 2 * i + s + 1)
                dve.tensor_copy(partial3[0], m1).then_inc(last_chain, 1)
                dve.wait_ge(last_chain, k + 1)
                dve.tensor_tensor(partial3[1], partial3[0], m2, ALU.subtract).then_inc(last_chain, 1)
                dve.tensor_tensor(partial3[0], partial3[0], m0, ALU.add).then_inc(last_chain, 1)
                px = [joined3[s][:, :, :, e:W:2] for e in range(2)]
                view = lambda t: t.rearrange("p (m h t) -> p m h t", m=2, t=HT)
                dve.wait_ge(last_chain, k + 2)
                dve.tensor_tensor(px[1], view(partial3[1]), view(m3), ALU.subtract).then_inc(last_chain, 1)
                dve.wait_ge(last_chain, k + 3)
                dve.tensor_tensor(px[0], view(partial3[0]), view(m2), ALU.add).then_inc(last_chain, 1)
                dve.wait_ge(last_chain, k + 5)
                cols = bass.ds((2 * i + s) * PX, PX)
                dve.tensor_tensor(y[:, cols], joined3[s].rearrange("p m h w -> p (m h w)"), x3_back[:, cols],
                                  ALU.add).then_inc(y_done, 1)

            factors(0)
            last_windows(0, 0)
            first_low(0)
            first_low(1)
            factors(1)
            last_windows(0, 1)
            dve.wait_ge(x3_back_in, 16)
            with dve.Fori(0, PAIRS // 2 - 1) as i:
                for s in range(2):
                    last_windows(i + 1, s)
                    last_join(i, s)
            for s in range(2):
                last_join(PAIRS // 2 - 1, s)

        @block.tensor
        def _(pe):
            mm, tr = pe.matmul, pe.transpose
            ident = c("ident")

            def product(w, slot, dst, g, k):
                hi, lo = (w_hi[:, w, :], w_lo[:, w, :]) if w < 3 else (w3_hi, w3_lo)
                mix, row = 2 * (g % 2) + k // KH, k % KH
                o = POS[mix] * KC + row * C
                hi, lo = hi[:, o:o + C], lo[:, o:o + C]
                x_hi, x_lo = [t[slot][:, mix, :, row:row + H, :] for t in (win_hi, win_lo)]
                dst = dst[:, k // KH * HW:(k // KH + 1) * HW]
                mm(dst, hi, x_hi, start=(row == 0), stop=False)
                mm(dst, hi, x_lo, start=False, stop=False)
                return mm(dst, lo, x_hi, start=False, stop=(row == KH - 1))

            def stage(k, i):
                if k == 0:
                    pe.wait_ge(x_loaded, 16 * i + 16)
                    after(pe, qk_low, 4 * i - QUADS)
                    for m in range(2):
                        for q in range(CH):
                            o = (m * CH + q) * C
                            ins = tr(bank[0][:, o:o + C], x_in[:, m, q * P:(q + 1) * P], ident)
                    ins.then_inc(xt_done, 1)
                if k == 1:
                    pe.wait_ge(xt_copied, i + 1)
                    after(pe, qk_low, 4 * i - QUADS)
                    after(pe, x3_done, 2 * i - 2)
                    for m in range(2):
                        for q in range(CH):
                            ins = mm(bank[1][:, m * C:(m + 1) * C], x_t[:, m, q, :], x_t[:, m, q, :],
                                     start=(q == 0), stop=(q == CH - 1))
                    ins.then_inc(energy_done, 1)
                if k == 2:
                    pe.wait_ge(att0_exp, 2 * i + 2)
                    for m in range(2):
                        ins = tr(bank[0][:, m * C:(m + 1) * C], att0[:, m, :], ident)
                    ins.then_inc(att0t_done, 1)
                if k == 3:
                    pe.wait_ge(att0t_copied, i + 1)
                    for m in range(2):
                        ins = mm(bank[1][:, m * HW:(m + 1) * HW], att0_t[:, m, :], x_in[:, m, :], start=True, stop=True)
                    ins.then_inc(o0_done, 1)
                if k == 4:
                    pe.wait_ge(sum_x_done, i + 1)
                    pe.wait_ge(o0_scaled, 2 * i + 2)
                    mm(bank[0][0:HID0, 0:2], c("w1x"), sum_x[:, :], start=True, stop=False)
                    mm(bank[0][0:HID0, 0:2], c("w1o"), sum_o0[:, :], start=False, stop=True).then_inc(hid0_done, 1)
                if k == 5:
                    pe.wait_ge(hid0_relu, i + 1)
                    mm(bank[1][:, 0:2], c("w2", HID0), hid0[:, :], start=True, stop=True).then_inc(z0_done, 1)
                if k == 6:
                    pe.wait_ge(x1_done, 2 * i + 2)
                    for m in range(2):
                        ins = mm(bank[0][m * MID:(m + 1) * MID, 0:HW], c("reduce_w"), x1[:, m, :], start=True, stop=True)
                    ins.then_inc(red_done, 1)
                if k == 9:
                    if isinstance(i, int) and i == 0:
                        pe.wait_ge(cst2_loaded, 16)
                    pe.wait_ge(xr_done, i + 1)
                    mm(bank[1][0:2 * HID1, 0:1], c("gw1"), sum_xr[:, :], start=True, stop=True).then_inc(hid1_done, 1)
                if k == 10:
                    pe.wait_ge(hid1_relu, i + 1)
                    mm(bank[0][:, 0:1], c("gw2", 2 * HID1), hid1[:, :], start=True, stop=True).then_inc(z1_done, 1)
                    pe.wait_ge(xh_done, 2 * i + 1)
                    for q in range(CH):
                        ins = tr(bank[1][:, q * P:(q + 1) * P], xh[:, q * P:(q + 1) * P], ident)
                    ins.then_inc(xht_done, 1)
                if k == 11:
                    pe.wait_ge(xht_copied, i + 1)
                    pe.wait_ge(z1_exp, i + 1)
                    fwd = c("fwd").rearrange("p (k r f) -> p k r f", k=CH, r=2)
                    for r in range(2):
                        for q in range(CH):
                            ins = mm(bank[0][:, r * P:(r + 1) * P], fwd[:, q, r, :], xh_t[:, q, :],
                                     start=(q == 0), stop=(q == CH - 1))
                    ins.then_inc(dft_done, 1)
                if k == 12:
                    pe.wait_ge(ab_copied, i + 1)
                    pe.wait_ge(b_signed_done, i + 1)
                    mm(bank[1][:, 0:P], ab[:, 0, :], ab[:, 0, :], start=True, stop=False)
                    mm(bank[1][:, 0:P], ab[:, 1, :], b_signed[:, :], start=False, stop=True).then_inc(dot1_done, 1)
                    mm(bank[0][:, 0:HW], ab[:, 0, :], c("even_a"), start=True, stop=False)
                    mm(bank[0][:, 0:HW], ab[:, 1, :], c("even_b"), start=False, stop=True).then_inc(even_done, 1)
                if k == 13:
                    pe.wait_ge(squares_done, 2 * i + 2)
                    pe.wait_ge(logit1_done, i + 1)
                    mm(bank[1][:, 0:HW], ab_sq[:, 0, :], c("inv_aa"), start=True, stop=False)
                    mm(bank[1][:, 0:HW], ab_sq[:, 1, :], c("inv_bb"), start=False, stop=False)
                    mm(bank[1][:, 0:HW], a_times_b[:, :], c("inv_ab"), start=False, stop=True).then_inc(filt_done, 1)
                if k == 14:
                    pe.wait_ge(att1_chain, 2 * i + 2)
                    pe.wait_ge(even_copied, i + 1)
                    mm(bank[0][:, 0:C], att1_n[:, :], c("post1"), start=True, stop=True).then_inc(patt_done, 1)
                if k == 15:
                    pe.wait_ge(patt_copied, i + 1)
                    pe.wait_ge(filt_scaled, i + 1)
                    for m in range(2):
                        r0 = m * MID
                        mm(bank[m][:, 0:HW], post_att[r0:r0 + MID, :], even[r0:r0 + MID, :], start=True, stop=False)
                        ins = mm(bank[m][:, 0:HW], c("post2", MID, r0), filt[r0:r0 + MID, :], start=False, stop=True)
                    ins.then_inc(y1_done, 1)
                if k == 16:
                    pe.wait_ge(gn_chain, 7 * i + 4)
                    mm(bank[0][:, 0:4], c("group"), halves(stats)[:, :, 0, 1:3], start=True, stop=False)
                    mm(bank[0][:, 0:4], c("group"), halves(stats)[:, :, 1, 1:3], start=False, stop=True).then_inc(gsum_done, 1)

            def project(i, what, quads=range(QUADS)):
                xn_all = xn[:, :, :].rearrange("p m x -> p (m x)")
                if what == "q":
                    pe.wait_ge(xn_done, 5 * i + 5)
                if what in "qk":
                    for q in quads:
                        if what == "k":
                            after(pe, st_exp, 2 * HEADS * i - QUADS + 1 + q)
                        dst = bank[(FRONT if what == "q" else ST_BANK)[q]][:, :]
                        mm(dst, c("w" + what)[:, q * P:(q + 1) * P], xn_all, start=True, stop=True).then_inc(qk_done, 1)
                if what == "v":
                    after(pe, h_scaled, 2 * i)
                    for m in range(2):
                        for k in range(CH):
                            o = (m * CH + k) * C
                            ins = mm(bank[S_BANK][:, o:o + C], xn[:, m, k * P:(k + 1) * P], c("wv"), start=True, stop=True)
                    ins.then_inc(v_done, 1)

            def scores(j, n):
                m, h = n // HEADS, n % HEADS
                r = slice(SLOT * (h % 4), SLOT * (h % 4) + SLOT)
                if n == 0:
                    pe.wait_ge(qk_low, 4 * j + QUADS)
                    pe.wait_ge(qk_high, 4 * j + 2 * QUADS)
                if s_before(n):
                    pe.wait_ge(s_max, 2 * HEADS * j + s_before(n))
                elif s_bank(n) == S_BANK:
                    pe.wait_ge(v_copied, 2 * j + 2)
                else:
                    after(pe, o2_copied, 4 * j)
                for k in range(CH):
                    ins = mm(bank[s_bank(n)][:, k * HW:(k + 1) * HW],
                             q_hl[r, h // 4, m * HW + k * P:m * HW + (k + 1) * P],
                             k_hi[r, h // 4, m * HW:(m + 1) * HW], start=True, stop=True)
                ins.then_inc(s_done, 1)

            def scores_t(j, n):
                m, h = n // HEADS, n % HEADS
                r = slice(SLOT * (h % 4), SLOT * (h % 4) + SLOT)
                if n % HEADS == 0:
                    pe.wait_ge(maxt_copied, 2 * j + m + 1)
                if n >= 2:
                    pe.wait_ge(st_exp, 2 * HEADS * j + n - 1)
                if n == 0:
                    pe.wait_ge(k_rows, 2 * j + 2)
                for k in range(CH):
                    dst = bank[ST_BANK[n % 2]][:, k * HW:(k + 1) * HW]
                    key = slice(m * HW + k * P, m * HW + (k + 1) * P)
                    mm(dst, k_hi[r, h // 4, key], q_hl[r, h // 4, m * HW:(m + 1) * HW], start=True, stop=False)
                    ins = mm(dst, k_lo[r, h // 4, key], q_max[r, h // 4, :], start=False, stop=True)
                ins.then_inc(st_done, 1)

            def maxima_t(j, m):
                pe.wait_ge(s_max, 2 * HEADS * j + HEADS * (m + 1))
                if m:
                    pe.wait_ge(st_exp, 2 * HEADS * j + HEADS)
                else:
                    pe.wait_ge(qk_low, 4 * j + 2 * QUADS)
                for q in range(QUADS):
                    for k in range(CH):
                        o = q * HW + k * P
                        ins = tr(bank[ST_BANK[1]][:, o:o + P], nmax2[:, m, k, q, :], ident)
                ins.then_inc(maxt_done, 1)

            def values(j, n):
                m, h = n // HEADS, n % HEADS
                pe.wait_ge(p_split, 2 * HEADS * j + n + 1)
                if n == 0:
                    pe.wait_ge(v_copied, 2 * j + 2)
                if h % 4 == 0:
                    after(pe, o2_copied, 4 * j + 2 * m + h // 4 - 1)
                if n == HEADS // 2:
                    pe.wait_ge(s_max, 2 * HEADS * j + HEADS + HEADS // 2 + LAG)
                t, a = h // 2, h % 2
                dst = bank[O_BANK[t // 2]][:, t % 2 * HW:(t % 2 + 1) * HW]
                for k in range(CH):
                    v = v_t[:, m, k, t, a * 2 * SLOT:a * 2 * SLOT + P]
                    mm(dst, v, p_hi[:, n % 3, k, :], start=(a == 0 and k == 0), stop=False)
                    ins = mm(dst, v, p_lo[:, n % 3, k, :], start=False, stop=(a == 1 and k == CH - 1))
                ins.then_inc(pv_done, 1)

            def result_t(j, m):
                pe.wait_ge(o2_copied, 4 * j + 2 * m + 2)
                if m:
                    pe.wait_ge(x3_done, 2 * j + 1)
                else:
                    pe.wait_ge(s_max, 2 * HEADS * (j + 1))
                for k in range(CH):
                    for t in range(2 * QUADS):
                        o = k * HW + t * 2 * SLOT
                        ins = mm(bank[S_BANK][:, o:o + 2 * SLOT], o2[:, t, k * P:(k + 1) * P], c("combine"),
                                 start=True, stop=True)
                ins.then_inc(ot_done, 1)

            def heads_t(j, m):
                pe.wait_ge(h_scaled, 2 * j + m + 1)
                for k in range(CH):
                    ins = tr(bank[h_bank(m)][:, k * P:(k + 1) * P], h_t[:, k, :], ident)
                ins.then_inc(ht_done, 1)

            def project_out(j, m):
                pe.wait_ge(ht_copied, 2 * j + m + 1)
                mm(bank[h_bank(m)][:, HW:2 * HW], c("wproj"), h_c[:, m, :], start=True, stop=True).then_inc(proj_done, 1)

            def convolve(j, u0, u1):
                last_pair = isinstance(j, int) and j == PAIRS - 1
                for u in range(u0, u1):
                    g, k = divmod(u, UNITS)
                    if u == 0:
                        pe.wait_ge(win_low, 2 * j + 2)
                        after(pe, joined, 3 * j)
                    if k == 0 and g and not last_pair:
                        if g % 2:
                            pe.wait_ge(first_copied, 3 * j + g // 2 + 1)
                        else:
                            pe.wait_ge(joined, 3 * j + g // 2)
                    if k == 0 and g >= 2 and last_pair:
                        pe.wait_ge(joined if g % 2 else first_copied, 3 * j + g // 2)
                    ins = product(g // 2, 0, bank[conv_bank(j, g)][:, :], g, k)
                    if k == UNITS - 1:
                        ins.then_inc(group_done, 1)

            def slots(j, i=None, cj=None):
                before = not (isinstance(j, int) and j == 0)
                units = GROUPS * UNITS - (sum(UNITS_END) if i is None else sum(UNITS_LATE))
                late = cj is not None and not (isinstance(cj, int) and cj == 0)
                for s in range(SLOTS):
                    n = s - HEADS
                    if n in (0, HEADS):
                        maxima_t(j, n // HEADS)
                    if n >= 0 and n % HEADS:
                        scores_t(j, n)
                    if n < HEADS:
                        scores(j, s)
                    if s == 1:
                        project(j, "v")
                    if s == 1 and before:
                        heads_t(j - 1, 1)
                    if s == 2 and before:
                        project_out(j - 1, 1)
                    if late and s < len(UNITS_LATE):
                        u = GROUPS * UNITS - sum(UNITS_LATE[s:])
                        convolve(cj - 1, u, u + UNITS_LATE[s])
                    if cj is not None:
                        convolve(cj, min(sum(UNITS_IN[:s]), units), min(sum(UNITS_IN[:s + 1]), units))
                    if n >= LAG:
                        values(j, n - LAG)
                    if s == OUT_SLOT:
                        result_t(j, 0)
                    if s == OUT_SLOT + 1:
                        heads_t(j, 0)
                    if s == OUT_SLOT + 2:
                        project_out(j, 0)
                    if s in STAGE and i is not None:
                        stage(STAGE[s], i)
                    if n in (0, HEADS):
                        scores_t(j, n)
                if i is not None:
                    project(i, "q")
                    values(j, 2 * HEADS - 2)
                    project(i, "k", [0])
                    values(j, 2 * HEADS - 1)
                    project(i, "k", [1])
                    result_t(j, 1)
                else:
                    values(j, 2 * HEADS - 2)
                    for k, step in enumerate((lambda: values(j, 2 * HEADS - 1), lambda: result_t(j, 1),
                                              lambda: heads_t(j, 1), lambda: project_out(j, 1))):
                        convolve(cj, units, units + UNITS_END[k])
                        units += UNITS_END[k]
                        step()

            pe.wait_ge(cst_loaded, 16)
            mm(bank[CONV][:, 0:1], c("wproj"), c("bv"), start=True, stop=True).then_inc(bias_mm, 1)
            for k in range(STAGES):
                if k == 6:
                    pe.wait_ge(vec_set, 6)
                stage(k, 0)
            for what in "qk":
                project(0, what)
            slots(0, 1)
            pe.wait_ge(w_split, 3)
            slots(1, 2, 0)
            with pe.Fori(3, PAIRS) as i:
                slots(i - 1, i, i - 2)
            slots(PAIRS - 1, None, PAIRS - 2)
            convolve(PAIRS - 1, 0, 4 * UNITS)
            pe.wait_ge(joined, 3 * PAIRS - 1)
            pe.wait_ge(x3_done, 2 * PAIRS)
            q3, k3, v3 = qkv3

            def tile(b, g):
                return slice((b * BATCH + g) * P, (b * BATCH + g + 1) * P)

            def v3_transposed(b):
                if b == 0:
                    pe.wait_ge(joined, 3 * PAIRS)
                if b >= 2:
                    pe.wait_ge(v3t_copied, b - 1)
                for g in range(BATCH):
                    ins = tr(bank[2 + b % 2][:, g * C:(g + 1) * C], v3[:, tile(b, g)], ident)
                ins.then_inc(v3t_done, 1)

            def attended(a):
                pe.wait_ge(att3t_copied, a + 1)
                pe.wait_ge(v3t_copied, a + 1)
                if a >= 2:
                    pe.wait_ge(sq3_done, a - 1)
                for g in range(BATCH):
                    ins = mm(bank[6 + a % 2][:, g * P:(g + 1) * P], v3_t[:, a % 2, g, :], att3_t[:, tile(a, g)],
                             start=True, stop=True)
                ins.then_inc(virt_done, 1)

            units = 4 * UNITS
            for b in range(BATCHES + 2):
                if b < BATCHES:
                    if b >= 2:
                        pe.wait_ge(logit3_done, b - 1)
                    for g in range(BATCH):
                        ins = mm(bank[b % 2][:, g * P:(g + 1) * P], q3[:, tile(b, g)], k3[:, tile(b, g)],
                                 start=True, stop=True)
                    ins.then_inc(dot3_done, 1)
                else:
                    v3_transposed(b - BATCHES)
                if b == BATCHES + 1:
                    attended(0)
                if b < len(UNITS_V):
                    convolve(PAIRS - 1, units, units + UNITS_V[b])
                    units += UNITS_V[b]
                a = b - 2
                if a >= 0:
                    pe.wait_ge(att3_scaled, a + 1)
                    if a >= 2:
                        pe.wait_ge(att3t_copied, a - 1)
                    for g in range(BATCH):
                        ins = tr(bank[4 + a % 2][:, g * P:(g + 1) * P], att3_n[a % 2][:, g * P:(g + 1) * P], ident)
                    ins.then_inc(att3t_done, 1)
            for b in range(2, BATCHES + 3):
                if b < BATCHES:
                    v3_transposed(b)
                if 1 <= b - 1 < BATCHES:
                    attended(b - 1)
                a = b - 3
                if a >= 0:
                    pe.wait_ge(sum3_done, 2 * a + 2)
                    mm(bank[0][:, 0:2 * N], c("mean_all"), sum3[:, a % 2, :, :], start=(a == 0),
                       stop=(a == BATCHES - 1)).then_inc(tot3_done, 1)
            pe.wait_ge(w_split, 4)

            def last_convs(i):
                for s in range(2):
                    after(pe, y_done, 2 * i + s - 1)
                    for g in range(2):
                        pe.wait_ge(last_low, 4 * i + 2 * s + g + 1)
                        for k in range(UNITS):
                            ins = product(3, s, bank[2 * s + g][:, :], g, k)
                    ins.then_inc(last_conv, 1)

            last_convs(0)
            with pe.Fori(1, PAIRS // 2) as i:
                last_convs(i)


def constants():
    t = {"ident": np.eye(P, dtype=np.float32)}
    r = np.arange(P)
    t["mask1"] = np.where(r[:, None] // HID1 == r[None, :] // HID1, 0.0, FAR)
    t["mask3"] = np.where(r[:, None] % GPX == r[None, :] % GPX, 0.0, FAR)
    t["group"] = np.where(r[:, None] // GC == r[None, :] // GC, 0.5 / GC, 0.0)
    t["mean_all"] = np.full((P, P), 1.0 / (C * HW))
    half = [(0, 0), (0, W // 2), (H // 2, 0), (H // 2, W // 2)]
    pairs, seen = [], set(half)
    for u in range(H):
        for v in range(W):
            if (u, v) not in seen:
                pairs.append((u, v))
                seen |= {(u, v), (-u % H, -v % W)}
    h, w = np.divmod(np.arange(HW), W)
    angle = lambda f: 2 * np.pi * ((f[0] * h + f[1] * w) % H) / H
    root = float(np.sqrt(HW))
    a = [np.cos(angle(f)) / root for f in half[:2]] + [np.sqrt(2) * np.cos(angle(f)) / root for f in pairs]
    b = [np.cos(angle(f)) / root for f in half[2:]] + [np.sqrt(2) * np.sin(angle(f)) / root for f in pairs]
    a, b = np.array(a), np.array(b)
    t["fwd"] = np.stack([a.T.reshape(CH, P, P), b.T.reshape(CH, P, P)], 1).transpose(2, 0, 1, 3).reshape(P, -1)
    t["even_a"] = a
    t["even_b"] = np.where(r[:, None] < 2, b, 0.0)
    t["inv_aa"] = np.array([np.cos(angle(f)) / root for f in half[:2] + pairs])
    t["inv_bb"] = np.array([np.cos(angle(f)) / root for f in half[2:]] + [-np.cos(angle(f)) / root for f in pairs])
    t["inv_ab"] = np.array([0 * h for f in half[2:]] + [2 * np.sin(angle(f)) / root for f in pairs])
    t["sign_b"] = np.where(r < 2, 1.0, -1.0)[:, None]
    t["lo_rows"] = np.where(r % SLOT >= DH, 1.0, 0.0)[:, None]
    t["hi_rows"] = 1.0 - t["lo_rows"]
    t["one_row"] = np.where(r % SLOT == DH, 1.0, 0.0)[:, None]
    col = np.arange(2 * SLOT)
    t["combine"] = np.where((r[:, None] % SLOT == col % SLOT) & (r[:, None] // (2 * SLOT) == col // SLOT), 1.0, 0.0)
    return {k: v.astype(np.float32) for k, v in t.items()}


_OUT = ((N, C, H, W), "float32")


def kernel(**inputs):
    import numpy as _np
    import concourse.bacc as _bacc
    from concourse import mybir as _mybir
    from concourse.bass_utils import run_bass_kernel_spmd as _run

    a = {k: _np.asarray(v) for k, v in inputs.items()}
    col = lambda v: v.reshape(-1, 1)
    twice = lambda v: _np.concatenate([v, v], 0)
    q_rows = _np.array([[3 * DH * (4 * q + s // SLOT) + s % DH for s in range(P)] for q in range(QUADS)])
    v_rows = _np.array([3 * DH * h + 2 * DH + d for h in range(HEADS) for d in range(DH)])
    wqkv, bqkv = a["L2_conv_w_qkv"], a["L2_conv_b_qkv"]
    gw1 = _np.zeros((P, 2 * HID1), _np.float32)
    gw2 = _np.zeros((2 * HID1, P), _np.float32)
    for m in range(2):
        gw1[m * MID:(m + 1) * MID, m * HID1:(m + 1) * HID1] = a["L1_conv_gate_w1"].T
        gw2[m * HID1:(m + 1) * HID1, m * MID:(m + 1) * MID] = a["L1_conv_gate_w2"].T
    t = constants()
    t["w1x"], t["w1o"] = a["L0_conv_w1"].T[:C], a["L0_conv_w1"].T[C:]
    t["w2"], t["b1"], t["b2"] = a["L0_conv_w2"].T, col(a["L0_conv_b1"]), col(a["L0_conv_b2"])
    t["reduce_w"] = a["L1_conv_reduce_w"].T
    t["reduce_b"] = twice(col(a["L1_conv_reduce_b"]))
    t["dw"] = twice(a["L1_conv_dw_w"].reshape(MID, TAPS))
    for k in ("dw_b", "bn_gamma", "bn_beta", "bn_mean", "bn_var"):
        t[k] = twice(col(a["L1_conv_" + k]))
    t["gw1"], t["gw2"] = gw1, gw2
    t["gb1"], t["gb2"] = twice(col(a["L1_conv_gate_b1"])), twice(col(a["L1_conv_gate_b2"]))
    t["temp"] = twice(_np.repeat(col(a["L1_conv_temperature"]), MID // 8, 0))
    post = a["L1_conv_post_w"].T
    t["post1"], t["post2"], t["post_b"] = twice(post[:MID]), twice(post[MID:]), col(a["L1_conv_post_b"])
    t["gn_gamma"], t["gn_beta"] = col(a["L2_conv_gamma"]), col(a["L2_conv_beta"])
    t["wq"] = _np.concatenate([wqkv[q_rows[q]].T for q in range(QUADS)], 1)
    t["wk"] = _np.concatenate([wqkv[q_rows[q] + DH].T for q in range(QUADS)], 1)
    t["bq"] = bqkv[q_rows].T
    t["bk"] = bqkv[q_rows + DH].T
    t["wv"], t["bv"] = wqkv[v_rows].T, col(bqkv[v_rows])
    t["wproj"], t["bproj"] = a["L2_conv_w_proj"].T, col(a["L2_conv_b_proj"])
    t["ln_gamma"], t["ln_beta"] = col(a["L3_conv_gamma"]), col(a["L3_conv_beta"])
    small = _np.zeros((P, SMALL_W), _np.float32)
    for k, (b, e) in AT.items():
        small[:t[k].shape[0], b:e] = t[k]
    convs = _np.concatenate([a["L3_conv_W" + k].transpose(1, 3, 2, 0).reshape(C, TAPS * C) for k in "qkvc"], 1)
    arrays = {"x": _np.ascontiguousarray(a["x"]), "small": small, "convs": _np.ascontiguousarray(convs)}

    nc = _bacc.Bacc("TRN2", target_bir_lowering=False, num_devices=1)
    ap = {k: nc.dram_tensor(k, v.shape, _mybir.dt.from_np(v.dtype), kind="ExternalInput").ap()
          for k, v in arrays.items()}
    out = nc.dram_tensor("out", _OUT[0], _mybir.dt.from_np(_np.dtype(_OUT[1])), kind="ExternalOutput").ap()
    program(nc, ap["x"], ap["small"], ap["convs"], out)
    r = _run(nc, [arrays], core_ids=[0])
    return r.results[0]["out"]
```
